# Optimizing a Trainium2 kernel written in Bass

```python
import numpy as np
import jax
import jax.numpy as jnp

def _softmax(x, axis=-1):
    return jax.nn.softmax(x, axis=axis)

def _gelu(x):
    return jax.nn.gelu(x, approximate=True)

def _silu(x):
    return jax.nn.silu(x)

def _sigmoid(x):
    return jax.nn.sigmoid(x)

def _layernorm(x, axis=-1, eps=1e-05):
    m = jnp.mean(x, axis=axis, keepdims=True)
    v = jnp.var(x, axis=axis, keepdims=True)
    return (x - m) / jnp.sqrt(v + eps)

def _scatter_add(tgt, idx, src, axis=0):
    return tgt.at[idx].add(src)

def _segment_sum(src, seg, n):
    return jax.ops.segment_sum(src, seg, n)
kernel_name = 'mk_seq_preln_d2_jaxref_r8_9781be'

def setup_inputs(seed: int=0):
    np.random.seed(seed)
    _w = jnp.asarray

    def _L0_attn_setup():
        import jax, jax.numpy as jnp
        import numpy as np
        B, S, E = (4, 256, 128)
        H, KVH = (16, 4)
        D = E // H
        QL, KVL = (64, 32)
        ROPE_BASE = 10000.0

        def _rope(x):
            d = x.shape[-1]
            inv_freq = 1.0 / ROPE_BASE ** (jnp.arange(0, d, 2, dtype=jnp.float32) / d)
            t = jnp.arange(x.shape[1], dtype=jnp.float32)
            freqs = jnp.outer(t, inv_freq)
            cos = jnp.cos(freqs)[None, :, None, :].astype(x.dtype)
            sin = jnp.sin(freqs)[None, :, None, :].astype(x.dtype)
            x1, x2 = (x[..., ::2], x[..., 1::2])
            r1 = x1 * cos - x2 * sin
            r2 = x1 * sin + x2 * cos
            return jnp.stack([r1, r2], axis=-1).reshape(x.shape)
        key = jax.random.key(seed)
        ks = jax.random.split(key, 7)
        s = 0.02
        return {'x': jax.random.normal(ks[0], (B, S, E), dtype=jnp.float32), 'Wqa': jax.random.normal(ks[1], (E, QL), dtype=jnp.float32) * s, 'Wqb': jax.random.normal(ks[2], (QL, E), dtype=jnp.float32) * s, 'Wkva': jax.random.normal(ks[3], (E, KVL), dtype=jnp.float32) * s, 'Wkvb': jax.random.normal(ks[4], (KVL, KVH * D * 2), dtype=jnp.float32) * s, 'Wout': jax.random.normal(ks[5], (E, E), dtype=jnp.float32) * s, 'bout': jax.random.normal(ks[6], (E,), dtype=jnp.float32) * s}
    _L0_attn_in = _L0_attn_setup()

    def _L0_ffn_setup():
        import jax, jax.numpy as jnp
        import numpy as np
        B, S, D, E, H, DO = (4, 256, 128, 8, 512, 128)
        TOP_K = 2
        LN_EPS = 1e-05
        key = jax.random.key(seed)
        ks = jax.random.split(key, 9)
        s = 0.02
        return {'x': jax.random.normal(ks[0], (B, S, D), dtype=jnp.float32), 'W1': jax.random.normal(ks[1], (E, D, H), dtype=jnp.float32) * s, 'b1': jnp.zeros((E, H), dtype=jnp.float32), 'W2': jax.random.normal(ks[2], (E, H, DO), dtype=jnp.float32) * s, 'b2': jnp.zeros((E, DO), dtype=jnp.float32), 'gate_W': jax.random.normal(ks[3], (D, E), dtype=jnp.float32) * s, 'shared_W': jax.random.normal(ks[4], (D, DO), dtype=jnp.float32) * s, 'shared_b': jnp.zeros((DO,), dtype=jnp.float32), 'gamma': jnp.ones((DO,), dtype=jnp.float32), 'beta': jnp.zeros((DO,), dtype=jnp.float32)}
    _L0_ffn_in = _L0_ffn_setup()

    def _L1_attn_setup():
        import jax, jax.numpy as jnp
        import numpy as np
        H_HEADS = 16
        SEG = 32
        EPS = 1e-06
        key = jax.random.key(seed)
        ks = jax.random.split(key, 6)
        B, T, D = (2, 512, 128)
        sc = 1.0 / np.sqrt(D)
        return {'x': jax.random.normal(ks[0], (B, T, D), jnp.float32), 'norm_w': jnp.ones((D,), jnp.float32), 'Wq': jax.random.normal(ks[1], (D, D), jnp.float32) * sc, 'Wk': jax.random.normal(ks[2], (D, D), jnp.float32) * sc, 'Wv': jax.random.normal(ks[3], (D, D), jnp.float32) * sc, 'Wo': jax.random.normal(ks[4], (D, D), jnp.float32) * sc, 'Wu': jax.random.normal(ks[5], (D, D), jnp.float32) * sc}
    _L1_attn_in = _L1_attn_setup()

    def _L1_ffn_setup():
        import jax, jax.numpy as jnp
        import numpy as np
        HIDDEN = 128
        FFN = 4 * HIDDEN
        NUM_EXPERTS = 8
        TOP_K = 2
        B, S = (4, 256)
        key = jax.random.key(seed)
        ks = jax.random.split(key, 7)
        scale = 0.02
        return {'x': jax.random.normal(ks[0], (B, S, HIDDEN), dtype=jnp.float32), 'gate_w': jax.random.normal(ks[1], (HIDDEN, NUM_EXPERTS), dtype=jnp.float32) * scale, 'gate_b': jnp.zeros((NUM_EXPERTS,), dtype=jnp.float32), 'w1': jax.random.normal(ks[2], (NUM_EXPERTS, HIDDEN, FFN), dtype=jnp.float32) * scale, 'b1': jnp.zeros((NUM_EXPERTS, FFN), dtype=jnp.float32), 'w2': jax.random.normal(ks[3], (NUM_EXPERTS, FFN, HIDDEN), dtype=jnp.float32) * scale, 'b2': jnp.zeros((NUM_EXPERTS, HIDDEN), dtype=jnp.float32)}
    _L1_ffn_in = _L1_ffn_setup()
    _d = {'L0_attn_x': _L0_attn_in['x'], 'L0_attn_Wqa': _L0_attn_in['Wqa'], 'L0_attn_Wqb': _L0_attn_in['Wqb'], 'L0_attn_Wkva': _L0_attn_in['Wkva'], 'L0_attn_Wkvb': _L0_attn_in['Wkvb'], 'L0_attn_Wout': _L0_attn_in['Wout'], 'L0_attn_bout': _L0_attn_in['bout'], 'L0_ffn_W1': _L0_ffn_in['W1'], 'L0_ffn_b1': _L0_ffn_in['b1'], 'L0_ffn_W2': _L0_ffn_in['W2'], 'L0_ffn_b2': _L0_ffn_in['b2'], 'L0_ffn_gate_W': _L0_ffn_in['gate_W'], 'L0_ffn_shared_W': _L0_ffn_in['shared_W'], 'L0_ffn_shared_b': _L0_ffn_in['shared_b'], 'L0_ffn_gamma': _L0_ffn_in['gamma'], 'L0_ffn_beta': _L0_ffn_in['beta'], 'L1_attn_norm_w': _L1_attn_in['norm_w'], 'L1_attn_Wq': _L1_attn_in['Wq'], 'L1_attn_Wk': _L1_attn_in['Wk'], 'L1_attn_Wv': _L1_attn_in['Wv'], 'L1_attn_Wo': _L1_attn_in['Wo'], 'L1_attn_Wu': _L1_attn_in['Wu'], 'L1_ffn_gate_w': _L1_ffn_in['gate_w'], 'L1_ffn_gate_b': _L1_ffn_in['gate_b'], 'L1_ffn_w1': _L1_ffn_in['w1'], 'L1_ffn_b1': _L1_ffn_in['b1'], 'L1_ffn_w2': _L1_ffn_in['w2'], 'L1_ffn_b2': _L1_ffn_in['b2']}
    _x0 = _d['L0_attn_x']
    _d['L0_attn_x'] = jax.random.normal(jax.random.fold_in(jax.random.key(seed), 1), (8, 256, 128), dtype=_x0.dtype)
    del _x0
    return _d

def reference(L0_attn_x, L0_attn_Wqa, L0_attn_Wqb, L0_attn_Wkva, L0_attn_Wkvb, L0_attn_Wout, L0_attn_bout, L0_ffn_W1, L0_ffn_b1, L0_ffn_W2, L0_ffn_b2, L0_ffn_gate_W, L0_ffn_shared_W, L0_ffn_shared_b, L0_ffn_gamma, L0_ffn_beta, L1_attn_norm_w, L1_attn_Wq, L1_attn_Wk, L1_attn_Wv, L1_attn_Wo, L1_attn_Wu, L1_ffn_gate_w, L1_ffn_gate_b, L1_ffn_w1, L1_ffn_b1, L1_ffn_w2, L1_ffn_b2):

    def _L0_attn_ref(x, Wqa, Wqb, Wkva, Wkvb, Wout, bout):
        import jax, jax.numpy as jnp
        import numpy as np
        B, S, E = (4, 256, 128)
        H, KVH = (16, 4)
        D = E // H
        QL, KVL = (64, 32)
        ROPE_BASE = 10000.0

        def _rope(x):
            d = x.shape[-1]
            inv_freq = 1.0 / ROPE_BASE ** (jnp.arange(0, d, 2, dtype=jnp.float32) / d)
            t = jnp.arange(x.shape[1], dtype=jnp.float32)
            freqs = jnp.outer(t, inv_freq)
            cos = jnp.cos(freqs)[None, :, None, :].astype(x.dtype)
            sin = jnp.sin(freqs)[None, :, None, :].astype(x.dtype)
            x1, x2 = (x[..., ::2], x[..., 1::2])
            r1 = x1 * cos - x2 * sin
            r2 = x1 * sin + x2 * cos
            return jnp.stack([r1, r2], axis=-1).reshape(x.shape)
        b, s, _ = x.shape
        scale = D ** (-0.5)
        q = (x @ Wqa @ Wqb).reshape(b, s, H, D)
        kv = (x @ Wkva @ Wkvb).reshape(b, s, KVH, D, 2)
        k, v = (kv[..., 0], kv[..., 1])
        q = _rope(q)
        k = _rope(k)
        g = H // KVH
        k = jnp.repeat(k, g, axis=2)
        v = jnp.repeat(v, g, axis=2)
        scores = jnp.einsum('bqhd,bkhd->bhqk', q, k) * scale
        causal = jnp.triu(jnp.ones((s, s), dtype=bool), k=1)
        scores = jnp.where(causal[None, None], -jnp.inf, scores)
        w = jax.nn.softmax(scores, axis=-1)
        out = jnp.einsum('bhqk,bkhd->bqhd', w, v).reshape(b, s, E)
        return out @ Wout + bout

    def _L0_ffn_ref(x, W1, b1, W2, b2, gate_W, shared_W, shared_b, gamma, beta):
        import jax, jax.numpy as jnp
        import numpy as np
        B, S, D, E, H, DO = (4, 256, 128, 8, 512, 128)
        TOP_K = 2
        LN_EPS = 1e-05
        d = x.shape[-1]
        flat = x.reshape(-1, d)
        n_exp = gate_W.shape[-1]
        probs = jax.nn.softmax(flat @ gate_W, axis=-1)
        topk_w, topk_idx = jax.lax.top_k(probs, TOP_K)
        topk_w = topk_w / topk_w.sum(axis=-1, keepdims=True)
        combine = (jax.nn.one_hot(topk_idx, n_exp, dtype=flat.dtype) * topk_w[..., None]).sum(axis=1)
        out = 0.5 * jax.nn.gelu(flat @ shared_W + shared_b, approximate=False)
        for e in range(n_exp):
            h = jax.nn.gelu(flat @ W1[e] + b1[e], approximate=False)
            out = out + combine[:, e:e + 1] * (h @ W2[e] + b2[e])
        mean = out.mean(axis=-1, keepdims=True)
        var = ((out - mean) ** 2).mean(axis=-1, keepdims=True)
        out = (out - mean) * jax.lax.rsqrt(var + LN_EPS) * gamma + beta
        return out.reshape(*x.shape[:-1], out.shape[-1])

    def _L1_attn_ref(x, norm_w, Wq, Wk, Wv, Wo, Wu):
        import jax, jax.numpy as jnp
        import numpy as np
        H_HEADS = 16
        SEG = 32
        EPS = 1e-06
        B, T, D = x.shape
        H = H_HEADS
        dk = D // H
        N = T // SEG
        xn = x * jax.lax.rsqrt(jnp.mean(x * x, axis=-1, keepdims=True) + EPS) * norm_w

        def proj(W):
            return (xn @ W.T).reshape(B, T, H, dk)
        q, k, v = (proj(Wq), proj(Wk), proj(Wv))
        pq = jax.nn.elu(q) + 1.0
        pk = jax.nn.elu(k) + 1.0
        pqc = pq.reshape(B, N, SEG, H, dk)
        pkc = pk.reshape(B, N, SEG, H, dk)
        vc = v.reshape(B, N, SEG, H, dk)
        S_chunk = jnp.einsum('bnchk,bnchv->bnhkv', pkc, vc)
        S_cum = jnp.cumsum(S_chunk, axis=1)
        S_excl = S_cum - S_chunk
        boundary_states = S_cum
        inter = jnp.einsum('bnchk,bnhkv->bnchv', pqc, S_excl)
        tri = jnp.tril(jnp.ones((SEG, SEG), x.dtype))
        A = jnp.einsum('bnchk,bndhk->bnhcd', pqc, pkc) * tri
        intra = jnp.einsum('bnhcd,bndhv->bnchv', A, vc)
        zk = pkc.sum(axis=2)
        z_excl = jnp.cumsum(zk, axis=1) - zk
        z = z_excl[:, :, None] + jnp.cumsum(pkc, axis=2)
        denom = jnp.einsum('bnchk,bnchk->bnch', pqc, z) + EPS
        attn_out = ((inter + intra) / denom[..., None]).reshape(B, T, D) @ Wo.T
        x_out = x + attn_out
        xc = x.reshape(B, N, SEG, D)
        m_stack = xc.mean(axis=2)
        counts = jnp.arange(1, SEG + 1, dtype=x.dtype)[None, None, :, None]
        m_current = (jnp.cumsum(xc, axis=2) / counts).reshape(B, T, D)
        causal_mask = (jnp.arange(T) // SEG)[:, None] > jnp.arange(N)[None, :]
        u = x @ Wu.T
        scale = 1.0 / jnp.sqrt(jnp.asarray(D, x.dtype))
        sc_cached = jnp.einsum('btd,bnd->btn', u, m_stack) * scale
        sc_cached = jnp.where(causal_mask[None], sc_cached, -jnp.inf)
        sc_cur = jnp.sum(u * m_current, axis=-1, keepdims=True) * scale
        attn_w = jax.nn.softmax(jnp.concatenate([sc_cached, sc_cur], axis=-1), axis=-1)
        gates_cached = attn_w[..., :N]
        gate_current = attn_w[..., N:]
        h_retrieved = jnp.einsum('btn,bthk,bnhkv->bthv', gates_cached, pq, boundary_states).reshape(B, T, D)
        retrieval_scale = 1.0
        return gate_current * x_out + retrieval_scale * h_retrieved

    def _L1_ffn_ref(x, gate_w, gate_b, w1, b1, w2, b2):
        import jax, jax.numpy as jnp
        import numpy as np
        HIDDEN = 128
        FFN = 4 * HIDDEN
        NUM_EXPERTS = 8
        TOP_K = 2
        B, S = (4, 256)
        b, s, h = x.shape
        xt = x.reshape(b * s, h)
        probs = jax.nn.softmax(xt @ gate_w + gate_b, axis=-1)
        _, idx = jax.lax.top_k(probs, TOP_K)
        one_hot = jax.nn.one_hot(idx, NUM_EXPERTS, dtype=xt.dtype)
        mask = (one_hot.sum(axis=1) > 0).astype(xt.dtype)
        h1 = jax.nn.relu(jnp.einsum('th,ehf->etf', xt, w1) + b1[:, None, :])
        out_e = jnp.einsum('etf,efh->eth', h1, w2) + b2[:, None, :]
        out = jnp.einsum('eth,te->th', out_e, mask)
        return out.reshape(b, s, h)
    x = L0_attn_x
    x = x + _L0_attn_ref(_layernorm(x, axis=-1), L0_attn_Wqa, L0_attn_Wqb, L0_attn_Wkva, L0_attn_Wkvb, L0_attn_Wout, L0_attn_bout)
    x = x + _L0_ffn_ref(_layernorm(x, axis=-1), L0_ffn_W1, L0_ffn_b1, L0_ffn_W2, L0_ffn_b2, L0_ffn_gate_W, L0_ffn_shared_W, L0_ffn_shared_b, L0_ffn_gamma, L0_ffn_beta)
    x = x + _L1_attn_ref(_layernorm(x, axis=-1), L1_attn_norm_w, L1_attn_Wq, L1_attn_Wk, L1_attn_Wv, L1_attn_Wo, L1_attn_Wu)
    x = x + _L1_ffn_ref(_layernorm(x, axis=-1), L1_ffn_gate_w, L1_ffn_gate_b, L1_ffn_w1, L1_ffn_b1, L1_ffn_w2, L1_ffn_b2)
    return x

_drawn_inputs = setup_inputs


def setup_inputs(seed=0):
    import zlib

    import numpy as np

    out = dict(_drawn_inputs(seed))
    spreads = {'L0_ffn_b1': (0.0, 0.1),
     'L0_ffn_b2': (0.0, 0.1),
     'L0_ffn_shared_b': (0.0, 0.1),
     'L0_ffn_gamma': (1.0, 0.2),
     'L0_ffn_beta': (0.0, 0.1),
     'L1_attn_norm_w': (1.0, 0.2),
     'L1_ffn_gate_b': (0.0, 2.0),
     'L1_ffn_b1': (0.0, 2.0),
     'L1_ffn_b2': (0.0, 2.0)}
    factors = {'L0_attn_Wqa': 8.0,
     'L0_attn_Wqb': 8.0,
     'L0_attn_Wkva': 8.0,
     'L0_attn_Wkvb': 8.0,
     'L0_attn_Wout': 8.0,
     'L1_attn_Wo': 34.493,
     'L1_ffn_gate_w': 8.0,
     'L1_ffn_w1': 8.0,
     'L1_ffn_w2': 8.0}
    for name, (base, spread) in spreads.items():
        noise = np.random.default_rng([zlib.crc32(name.encode()), seed]).standard_normal(out[name].shape)
        drawn = base * np.exp(spread * noise) if base else spread * noise
        out[name] = jnp.asarray(drawn.astype(out[name].dtype))
    for name, factor in factors.items():
        out[name] = (out[name] * factor).astype(out[name].dtype)
    return out
```

```python
from contextlib import ExitStack

import numpy as np

import concourse.bass as bass
from concourse import mybir

F32 = mybir.dt.float32
F32R = mybir.dt.float32r
BF16 = mybir.dt.bfloat16
I32 = mybir.dt.int32
ALU = mybir.AluOpType
ACT = mybir.ActivationFunctionType
AX = mybir.AxisListType
ds = bass.ds

P = 128
B, S, D = 8, 256, 128
NT = B * S // P
H, HD = 16, 8
KVH, QL, KVL = 4, 64, 32
G = 4
LN_EPS = 1e-5
QK_SCALE = float(HD) ** -0.5
SEG = 32
NC = S // SEG
NS = NC - 1
RMS_EPS = 1e-6
NEG = -1e30
E, FF, TOPK = 8, 512, 2
FC = FF // P
ET = (B * S * TOPK - E) // P + E
ET += ET % 2
ETS = ET + 2
LOWEST = -3e38
MAGIC = 0x5F3759DF


def _constants():
    inv = (1.0 / np.float32(10000.0) ** (np.arange(0, HD, 2, dtype=np.float32) / np.float32(HD))).astype(np.float32)
    angle = np.outer(np.arange(S, dtype=np.float32), inv)
    row = np.arange(P) % HD
    cos = np.cos(angle)[:, row // 2].T
    sin = (np.sin(angle)[:, row // 2] * np.where(row % 2 == 0, -1.0, 1.0)).T
    rope = np.concatenate([cos, cos, sin, sin], axis=1).astype(np.float32)
    sel = np.zeros((4, P, G, P), np.float32)
    for h in range(H):
        for d in range(HD):
            for s in range(4):
                sel[s % 2, h * HD + d, h // 4, 32 * (h % 4) + 8 * s + d] = 1.0
                sel[2 + s // 2, h * HD + d, h // 4, 32 * (h % 4) + 8 * s + d] = 1.0
    p = np.arange(P)
    above = np.where(p[None, :] > p[:, None], np.float32(NEG), np.float32(0.0))
    pick = np.zeros((P, 4, P), np.float32)
    for part in range(3):
        for j in range(4):
            pick[4 * part + j, j, :] = 1.0
    ident = np.eye(P, dtype=np.float32)
    before = (p[:, None] < p[None, :]).astype(np.float32)
    pair = 2 * (P * np.arange(NT)[None, :, None] + p[:, None, None]) + np.arange(TOPK)[None, None, :] + 1
    of_expert = np.zeros((P, E, P), np.float32)
    for part in range(3):
        for e in range(E):
            of_expert[32 * part + e, e, :] = 1.0
    same = (p[:, None] // SEG == p[None, :] // SEG) & (p[:, None] <= p[None, :])
    running = np.where(same, np.float32(1) / (p[None, :] % SEG + 1).astype(np.float32), np.float32(0))
    chunk = np.where(p[:, None] // SEG == np.arange(P // SEG)[None, :], np.float32(1 / SEG), np.float32(0))
    at = (p[:, None] // SEG + (P // SEG) * np.arange(2)[None, :])[:, :, None]
    unseen = np.where(at > np.arange(NC)[None, None, :], np.float32(0), np.float32(NEG)).reshape(P, 2 * NC)
    own_head = (p[:, None] // HD == p[None, :] // HD).astype(np.float32)
    every = lambda a: np.broadcast_to(np.asarray(a, np.float32), (P, len(a)))
    route = np.concatenate([before, np.ones((P, P)), every(np.arange(P)), every(np.arange(ETS)),
                            pair.reshape(P, NT * TOPK), every(E - np.arange(E)), TOPK * B * S + 1 + p[:, None] + P * (np.arange(ETS)[None, :] % 2),
                            of_expert.reshape(P, E * P)], axis=1).astype(np.float32)
    return {"c_look": np.concatenate([running, chunk, unseen, own_head], axis=1).astype(np.float32),
            "c_rope": rope, "c_sel": sel.transpose(1, 0, 2, 3).reshape(P, 4 * G * P).copy(),
            "c_route": route,
            "c_misc": np.concatenate([ident, above, pick.reshape(P, 4 * P)], axis=1)}


def _layout(a):
    f = {k: np.asarray(v) for k, v in a.items()}
    swap = np.arange(P) ^ 1
    kv = f["L0_attn_Wkvb"].reshape(KVL, KVH, HD, 2)
    k_rep = np.repeat(kv[..., 0][:, :, None, :], H // KVH, axis=2).reshape(KVL, P)
    v_own = kv[..., 1].reshape(KVL, KVH * HD)
    out = {
        "x": f["L0_attn_x"].reshape(NT, P, D),
        "wqa_t": f["L0_attn_Wqa"].T,
        "wqb": np.concatenate([f["L0_attn_Wqb"], f["L0_attn_Wqb"][:, swap]], axis=1),
        "wkva_t": f["L0_attn_Wkva"].T,
        "wkvb": np.concatenate([k_rep, k_rep[:, swap], v_own], axis=1),
        "wout": f["L0_attn_Wout"],
        "bout": f["L0_attn_bout"].reshape(1, D),
    }
    for n, names in enumerate((("W1", "b1", "W2", "b2"), ("w1", "b1", "w2", "b2"))):
        w1, b1, w2, b2 = (f[f"L{n}_ffn_{m}"] for m in names)
        out |= {f"w1_{n}": w1.transpose(1, 0, 2), f"w2_{n}": w2.reshape(E, FC, P, D).transpose(2, 0, 1, 3),
                f"b_{n}": np.concatenate([b1, b2], axis=1)}
    out["w_look"] = np.concatenate([f["L1_attn_Wq"].T, f["L1_attn_Wk"].T, f["L1_attn_Wv"].T, f["L1_attn_Wo"].T,
                                    f["L1_attn_Wu"].T, f["L1_attn_Wu"]], axis=1)
    out["norm_w"] = f["L1_attn_norm_w"].reshape(D, 1)
    out["gates_0"] = np.concatenate([f["L0_ffn_shared_W"], f["L0_ffn_gate_W"]], axis=1)
    out["gates_1"] = f["L1_ffn_gate_w"]
    out["rows"] = np.concatenate([f["L0_ffn_shared_b"], f["L0_ffn_gamma"], f["L0_ffn_beta"], f["L1_ffn_gate_b"]]).reshape(1, -1)
    out |= _constants()
    return {k: np.ascontiguousarray(v) for k, v in out.items()}


class Chain:

    def __init__(self, eng, sem, n=0):
        self.eng, self.sem, self.n = eng, sem, n

    def add(self, ins):
        ins.then_inc(self.sem, 1)
        self.n += 1

    def wait(self):
        self.eng.wait_ge(self.sem, self.n)

    def __call__(self, ins):
        self.add(ins)
        self.wait()


def build(nc, inp, out, last_stage=3):
    ctx = ExitStack()
    with ctx:
        def sb(name, shape, dt=F32):
            return ctx.enter_context(nc.sbuf_tensor(name, shape, dt))

        def sem(name):
            return ctx.enter_context(nc.semaphore(name))

        ps = ctx.enter_context(nc.psum_tensor("ps", [P, 8, 512], F32))
        BT, BA, BB, BO = 4, 5, 6, 7

        X = sb("X", [P, NT + 2, D])
        stats = sb("stats", [P, NT + 2, 6])
        mv = sb("mv", [P, NT + 2, 2])
        rstd = sb("rstd", [P, NT + 2])
        nt1 = sb("nt1", [P, NT + 2])
        nt2 = sb("nt2", [P, NT + 2])
        rope = sb("rope", [P, 2, 2 * S])
        misc = sb("misc", [P, 6 * P])
        selr = sb("selr", [P, 4, G, P], F32R)
        ident = misc[:, 0:P]
        identb = sb("identb", [P, P], BF16)
        aboveb = sb("aboveb", [P, P], BF16)
        pickb = sb("pickb", [P, 4, P], BF16)
        wqa_t = sb("wqa_t", [QL, D])
        wqb = sb("wqb", [QL, 2 * D])
        wkva_t = sb("wkva_t", [KVL, D])
        wkvb = sb("wkvb", [KVL, 2 * D + KVH * HD])
        wq = sb("wq", [D, 2, D])
        wkv = sb("wkv", [D, 2 * D + KVH * HD])
        wout = sb("wout", [D, D])
        boutb = sb("boutb", [P, D])

        xn = [sb(f"xn{r}", [P, 2, D]) for r in range(2)]
        xnT = [sb(f"xnT{r}", [D, S]) for r in range(2)]
        rot = [sb(f"rot{r}", [P, 2 * S]) for r in range(3)]
        hi = sb("hi", [P, 2 * S], F32R)
        lo = sb("lo", [P, 2 * S], F32R)
        qst = [sb(f"qst{r}", [P, G, S], F32R) for r in range(2)]
        kst = [sb(f"kst{r}", [P, G, S], F32R) for r in range(2)]
        vst = [sb(f"vst{r}", [P, 2, H, 32]) for r in range(2)]
        negm = [sb(f"negm{r}", [P, 2, 4]) for r in range(2)]
        mrest = [sb(f"mrest{r}", [P, 2, 4]) for r in range(2)]
        mparts = [sb(f"mparts{r}", [P, 2, 3, 4], BF16) for r in range(2)]
        mT = [sb(f"mT{r}", [P, S], BF16) for r in range(2)]
        probs = [sb(f"probs{r}", [P, 4, 3 * P]) for r in range(2)]
        oT = sb("oT", [P, G, S])
        rden = sb("rden", [P, 2, H])
        on = sb("on", [P, 2, H, HD])
        onT = sb("onT", [P, S])

        look = sb("look", [P, 2 * P + P // SEG + 2 * NC])
        running, chunk_mean = look[:, 0:P], look[:, P:P + P // SEG]
        unseen = look[:, P + P // SEG:P + P // SEG + 2 * NC]
        own_head = look[:, P + P // SEG + 2 * NC:]
        w_look = sb("w_look", [D, 6, D])
        norm_w = sb("norm_w", [D, 1])
        wqkv = sb("wqkv", [D, 3, D])
        rms = sb("rms", [P, 3, NT + 2])
        usb = [rot[r][:, 0:2 * D] for r in range(2)]
        um = [rot[r][:, 2 * D:4 * D] for r in range(2)]
        means = [sb(f"means{r}", [D, NC]) for r in range(2)]
        wmeans = [sb(f"wmeans{r}", [D, NC]) for r in range(2)]
        SC = sb("SC", [P, NT, NC + 1])
        SCd = sb("SCd", [P, NT, NC + 1])
        GT = sb("GT", [P, NT + 2, NC + 1])
        sct = sb("sct", [P, 3, NT])
        pqk = [sb(f"pqk{r}", [P, 2 * S]) for r in range(2)]
        pkt = [sb(f"pkt{r}", [P, 2, D]) for r in range(2)]
        states = sb("states", [P, NS, D])
        found = rot[2][:, 0:2 * D].rearrange("p (t d) -> p t d", d=D)
        zt = rot[2][:, 2 * D:4 * D].rearrange("p (t d) -> p t d", d=D)

        NROUTE = 3 * P + 2 * ETS + NT * TOPK + E
        route = sb("route", [P, NROUTE])
        before_m, ones_m, iota_p = route[:, 0:P], route[:, P:2 * P], route[:, 2 * P:3 * P]
        iota_t = route[:, 3 * P:3 * P + ETS]
        pair_no = route[:, 3 * P + ETS:3 * P + ETS + NT * TOPK]
        rev_e = route[:, NROUTE - ETS - E:NROUTE - ETS]
        spare_no = route[:, NROUTE - ETS:NROUTE]
        of_expert = sb("of_expert", [P, E * P], BF16)
        rows = sb("rows", [P, 3 * D + E])
        shared_b, gamma, beta, gate_b = rows[:, 0:D], rows[:, D:2 * D], rows[:, 2 * D:3 * D], rows[:, 3 * D:]
        w1 = sb("w1", [D, E * FF])
        w2 = sb("w2", [P, E * FC * D])
        gates = [sb("gates_0", [D, D + E]), sb("gates_1", [D, E])]
        bias = [sb(f"bias_{n}", [E, FF + D]) for n in range(2)]
        bias_rest = sb("bias_rest", [E, FF + D])
        bias_mid = sb("bias_mid", [E, FF + D], BF16)
        bias3 = [sb(f"bias3_{n}", [P, FF + D], BF16) for n in range(2)]
        LG = sb("LG", [P, NT, E])
        LG2 = sb("LG2", [P, NT, E])
        rt = [sb(f"rt{n}", [P, NT, E]) for n in range(3)]
        top = sb("top", [P, 4, NT])
        first = [sb(f"first{n}", [P, NT, E]) for n in range(2)]
        picked = sb("picked", [P, NT, E])
        wts = sb("wts", [P, 5, NT])
        totals = sb("totals", [P, E, NT])
        upto = sb("upto", [P, E, NT])
        per_e = sb("per_e", [P, 8, E])
        per_ei = sb("per_ei", [P, E], I32)
        slot = sb("slot", [P, NT, TOPK])
        sloti = sb("sloti", [P, 3, NT * TOPK], I32)
        slotf = sb("slotf", [P, 2, NT * TOPK])
        hot = [sb(f"hot{n}", [P, P]) for n in range(2)]
        hotn = [sb(f"hotn{n}", [P, ETS]) for n in range(2)]
        etab = sb("etab", [P, ETS, E])
        eidf = sb("eidf", [P, 2, ETS])
        eid = sb("eid", [P, ETS], I32)
        inv = sb("inv", [P, 3, ETS])
        tab = sb("tab", [P, 2, ETS], I32)
        gidx = [sb(f"gidx{r}", [P, 1], I32) for r in range(2)]
        sidx = [sb(f"sidx{r}", [P, 1], I32) for r in range(2)]
        xg = [sb(f"xg{r}", [P, D]) for r in range(2)]
        xgT = [sb(f"xgT{r}", [D, P]) for r in range(2)]
        hid = [sb(f"hid{r}", [P, FF]) for r in range(2)]
        hidT = [sb(f"hidT{r}", [P, FF]) for r in range(2)]
        yt = [sb(f"yt{r}", [P, D]) for r in range(2)]
        SH = sb("SH", [P, NT, D])
        YB = sb("YB", [P, NT, TOPK * D])
        xbuf = [nc.dram_tensor(f"xbuf_{n}", (B * S + P, D), F32, kind="Internal").ap() for n in range(2)]
        ybuf = [nc.dram_tensor(f"ybuf_{n}", (TOPK * B * S + 2 * P, D), F32, kind="Internal").ap() for n in range(2)]

        loaded = sem("loaded")
        w_loaded = [sem(f"w_loaded_{n}") for n in range(2)]
        moe_cast = sem("moe_cast")
        MN = ("stats", "rstd", "normed", "xT", "xT_copied", "gated", "logits", "routed", "exp_diff",
              "counted", "hot_a", "hot_b", "hot_used", "inverse", "tabled", "idx", "x_turned", "x_copied",
              "h_ready", "h_active", "h_turned", "h_copied", "y_ready", "y_copied", "gelu", "mixed", "combined")
        ms = [{n: sem(f"m{l}_{n}") for n in MN} for l in range(2)]
        ms_rows = [[sem(f"m{l}_rows_out{r}") for r in range(2)] for l in range(2)]
        ms_gath = [[sem(f"m{l}_gathered{r}") for r in range(2)] for l in range(2)]
        ms_scat = [[sem(f"m{l}_scattered{r}") for r in range(2)] for l in range(2)]
        ms_back = [[sem(f"m{l}_back{q}") for q in range(4)] for l in range(2)]
        consts_cast = sem("consts_cast")
        w_mm = sem("w_mm")
        w_copied = sem("w_copied")
        init_done = sem("init_done")
        stats_done = sem("stats_done")
        rstd_step = sem("rstd_step")
        bias_added = sem("bias_added")
        stored = sem("stored")

        class A0:
            names = dict(normed=2, xT=1, xT_copied=1, proj=1, rope_step=5, hi_done=1, v_copied=1,
                         sel=4, stacked=4, p1=8, maxed=16, msplit=16, mTr=4, mT_copied=4, p2=8,
                         probs_done=8, masked=4, pv=4, o_copied=4, oTT=2, normed_o=4, onTr=1,
                         onT_copied=1, outp=1, residual=1)
        s0 = {n: (sem("a0_" + n), c) for n, c in A0.names.items()}

        A1 = dict(normed=2, xT=1, xT_copied=1, proj=1, elu_step=4, elu_exp=1, v_copied=1, sel=4, stacked=4,
                  pkT=1, pk_copied=1, p2=8, probs_done=8, masked=4, pv=4, o_copied=4, oTT=2, normed_o=6,
                  onTr=1, onT_copied=1, outp=1, state=2, state_own=2, looked=1, found=10, residual=6)
        s1 = {n: (sem("a1_" + n), c) for n, c in A1.items()}
        LN = ("stats", "rstd", "normed", "zT", "zT_copied", "means", "means_copied", "wmeans", "wmeans_copied", "scores",
              "u_copied", "gate_in", "um", "soft", "soft_exp", "w_scaled")
        ls = {n: sem("look_" + n) for n in LN}
        look_loaded = sem("look_loaded")
        tables = [s0]

        def wait(eng, name, b, k):
            sm, c = tables[-1][name]
            eng.wait_ge(sm, b * c + k + 1)

        def signal(ins, name):
            ins.then_inc(tables[-1][name][0], 1)

        block = ctx.enter_context(nc.Block())

        USES = []
        for g in range(G + 1):
            if g < G:
                USES += [(1, 2 * g), (1, 2 * g + 1)]
            if g > 0:
                USES += [(2, 2 * g - 2), (2, 2 * g - 1)]
        slot_of = {u: n % 2 for n, u in enumerate(USES)}
        before = {u: (USES[n - 2] if n >= 2 else None) for n, u in enumerate(USES)}

        @block.sync
        def _(sp):
            for t in range(4):
                sp.dma_start(X[:, 4 * t:4 * t + 4, :], inp["x"][4 * t:4 * t + 4].rearrange("t p d -> p t d")).then_inc(loaded, 16)
            sp.dma_start(wqa_t[:], inp["wqa_t"][:, :]).then_inc(loaded, 16)
            sp.dma_start(wqb[:], inp["wqb"][:, :]).then_inc(loaded, 16)
            sp.dma_start(wkva_t[:], inp["wkva_t"][:, :]).then_inc(loaded, 16)
            sp.dma_start(wkvb[:], inp["wkvb"][:, :]).then_inc(loaded, 16)
            sp.dma_start(wout[:], inp["wout"][:, :]).then_inc(loaded, 16)
            sp.dma_start(boutb[:], inp["bout"][0:1, :].broadcast_to((P, D))).then_inc(loaded, 16)
            sp.dma_start(rope[:].rearrange("p a s -> p (a s)"), inp["c_rope"][:, :]).then_inc(loaded, 16)
            sp.dma_start(misc[:], inp["c_misc"][:, :]).then_inc(loaded, 16)
            sp.dma_start(probs[0][:].rearrange("p a s -> p (a s)")[:, 0:1024], inp["c_sel"][:, 0:1024]).then_inc(loaded, 16)
            sp.dma_start(probs[1][:].rearrange("p a s -> p (a s)")[:, 0:1024], inp["c_sel"][:, 1024:2048]).then_inc(loaded, 16)
            for sm in [a for a, _ in s0.values()] + (list(ms[0].values()) if last_stage >= 1 else []) \
                    + ([a for a, _ in s1.values()] + list(ls.values()) if last_stage >= 2 else []) \
                    + (list(ms[1].values()) if last_stage >= 3 else []):
                sp.sem_inc(sm, 1)
            sp.dma_start(route[:], inp["c_route"][:, 0:NROUTE]).then_inc(w_loaded[0], 16)
            sp.dma_start(YB[:].rearrange("p a s -> p (a s)")[:, 0:E * P], inp["c_route"][:, NROUTE:]).then_inc(w_loaded[0], 16)
            sp.dma_start(rows[:], inp["rows"][0:1, :].broadcast_to((P, 3 * D + E))).then_inc(w_loaded[0], 16)
            def load_experts(n):
                sp.dma_start(gates[n][:], inp[f"gates_{n}"][:, :]).then_inc(w_loaded[n], 16)
                sp.dma_start(bias[n][:], inp[f"b_{n}"][:, :]).then_inc(w_loaded[n], 16)
                sp.dma_start(w1[:].rearrange("p (e f) -> p e f", e=E), inp[f"w1_{n}"][:, :, :]).then_inc(w_loaded[n], 16)
                sp.dma_start(w2[:].rearrange("p (e c d) -> p e c d", e=E, c=FC), inp[f"w2_{n}"][:, :, :, :]).then_inc(w_loaded[n], 16)

            load_experts(0)
            sp.dma_start(look[:], inp["c_look"][:, :]).then_inc(look_loaded, 16)
            sp.dma_start(w_look[:].rearrange("p a d -> p (a d)"), inp["w_look"][:, :]).then_inc(look_loaded, 16)
            sp.dma_start(norm_w[:], inp["norm_w"][:, :]).then_inc(look_loaded, 16)

            def experts(l):
                m = ms[l]
                xr = xbuf[l][0:B * S, :].rearrange("(t p) d -> t p d", p=P)
                sp.wait_ge(init_done, 7)
                for r in range(2):
                    sp.dma_start(xbuf[l][B * S + r * P // 2:B * S + (r + 1) * P // 2, :], X[r * 64:r * 64 + P // 2, NT, :]).then_inc(ms_rows[l][r], 16)
                with sp.Fori(0, NT // 4) as i:
                    for r in range(2):
                        sp.wait_ge(m["normed"], 4 * i + 2 * r + 2 + 1)
                        sp.dma_start(xr[ds(4 * i + 2 * r, 2), :, :].rearrange("t p d -> p t d"), xn[r][:]).then_inc(ms_rows[l][r], 16)
                for r in range(2):
                    sp.wait_ge(ms_scat[l][r], 16 * (ET // 2) + 16)
                yr = ybuf[l][0:TOPK * B * S, :].rearrange("(t p k) d -> p t (k d)", p=P, k=TOPK)
                for q in range(4):
                    sp.dma_start(YB[:, 4 * q:4 * q + 4, :], yr[:, 4 * q:4 * q + 4, :]).then_inc(ms_back[l][q], 16)

            if last_stage == 0:
                sp.wait_ge(s0["residual"][0], B + 2)
            if last_stage >= 1:
                experts(0)
                if last_stage >= 3:
                    load_experts(1)
                sp.wait_ge(ms[0]["combined"], 1 + 1)
            if last_stage >= 2:
                sp.wait_ge(s1["residual"][0], 6 * B + 1)
            if last_stage >= 3:
                experts(1)
                sp.wait_ge(ms[1]["combined"], 1 + 1)
            sp.dma_start(out.rearrange("(t p) d -> p t d", p=P), X[:, 0:NT, :]).then_inc(stored, 16)
            sp.wait_ge(stored, 16)
        NLOAD = 14

        @block.gpsimd
        def _(pool):
            def own_wait():
                pool.nop(nofuse=True)

            for r in range(2):
                pool.memset(vst[r][:], 0.0).then_inc(init_done, 1)
                pool.memset(mT[r][:], 0.0).then_inc(init_done, 1)
            pool.memset(X[:, NT:NT + 2, :], 0.0).then_inc(init_done, 1)
            pool.wait_ge(init_done, 5)
            for r in range(2):
                pool.memset(vst[r][:, :, :, HD:HD + 1], 1.0).then_inc(init_done, 1)

            def split_max(b, g):
                m = g % 2
                k = 4 * g
                wait(pool, "maxed", b, 4 * g + 4)
                wait(pool, "mTr", b, max(g - 1, 0))
                wait(pool, "msplit", b, k)
                own_wait()
                signal(pool.tensor_copy(mparts[m][:, :, 0, :], negm[m][:]), "msplit")
                wait(pool, "msplit", b, k + 1)
                own_wait()
                signal(pool.tensor_tensor(mrest[m][:], negm[m][:], mparts[m][:, :, 0, :], ALU.subtract), "msplit")
                wait(pool, "msplit", b, k + 2)
                own_wait()
                signal(pool.tensor_copy(mparts[m][:, :, 1, :], mrest[m][:]), "msplit")
                wait(pool, "msplit", b, k + 3)
                own_wait()
                signal(pool.tensor_tensor(mparts[m][:, :, 2, :], mrest[m][:], mparts[m][:, :, 1, :], ALU.subtract), "msplit")

            def mask_probs(b, g):
                wait(pool, "probs_done", b, 2 * g + 2)
                own_wait()
                for c in (0, 2):
                    diag = probs[g % 2][:, :, c * P:(c + 1) * P]
                    last = pool.affine_select(out=diag, in_=diag, compare_op=ALU.is_ge, fill=0.0, base=0,
                                              pattern=[[0, 4], [1, P]], channel_multiplier=-1)
                signal(last, "masked")

            with pool.Fori(0, B) as b:
                for g in range(G + 1):
                    if g < G:
                        split_max(b, g)
                    if g > 0:
                        mask_probs(b, g - 1)

            def experts(l):
                m = ms[l]
                for r in range(2):
                    pool.dma_start(ybuf[l][TOPK * B * S + r * P:TOPK * B * S + (r + 1) * P, :], X[:, NT, :]).then_inc(ms_scat[l][r], 16)
                pool.wait_ge(m["tabled"], 6 + 1)
                own_wait()
                for r in range(2):
                    pool.wait_ge(ms_rows[l][r], 16 * (NT // 4) + 16)
                own_wait()

                def fetch(n, r, k, copies):
                    pool.tensor_copy(gidx[r][:], tab[:, 1, ds(n, 1)]).then_inc(m["idx"], 1)
                    pool.wait_ge(m["idx"], copies + 1)
                    own_wait()
                    pool.indirect_dma_start(out=xg[r][:], out_offset=None, in_=xbuf[l][:, :],
                                            in_offset=bass.IndirectOffsetOnAxis(ap=gidx[r][:], axis=0)).then_inc(ms_gath[l][r], 16)
                for r in range(2):
                    fetch(r, r, 0, r + 1)
                with pool.Fori(0, ET // 2) as i:
                    for r in range(2):
                        n = 2 * i + r
                        pool.wait_ge(ms_gath[l][r], 16 * i + 16)
                        pool.wait_ge(m["x_turned"], n + 2)
                        own_wait()
                        fetch(n + 2, r, i + 1, 2 * n + 3)
                        pool.wait_ge(ms_scat[l][r], 16 * i + 16)
                        own_wait()
                        pool.tensor_copy(sidx[r][:], tab[:, 0, ds(n, 1)]).then_inc(m["idx"], 1)
                        pool.wait_ge(m["idx"], 2 * n + 4 + 1)
                        pool.wait_ge(m["y_copied"], n + 2)
                        own_wait()
                        pool.indirect_dma_start(out=ybuf[l][:, :], out_offset=bass.IndirectOffsetOnAxis(ap=sidx[r][:], axis=0),
                                                in_=yt[r][:], in_offset=None).then_inc(ms_scat[l][r], 16)

            if last_stage >= 1:
                experts(0)
            if last_stage >= 2:
                tables.append(s1)
                with pool.Fori(0, B) as b:
                    for g in range(G):
                        mask_probs(b, g)
                tables.pop()
            if last_stage >= 3:
                experts(1)

        @block.vector
        def _(dve):
            dve.wait_ge(loaded, 16 * NLOAD)
            for n in range(2):
                dve.tensor_copy(selr[:, 2 * n:2 * n + 2].rearrange("p a g m -> p (a g m)"),
                                probs[n][:].rearrange("p a s -> p (a s)")[:, 0:1024]).then_inc(consts_cast, 1)
            dve.tensor_copy(identb[:], misc[:, 0:P]).then_inc(consts_cast, 1)
            dve.tensor_copy(aboveb[:], misc[:, P:2 * P]).then_inc(consts_cast, 1)
            dve.tensor_copy(pickb[:].rearrange("p a m -> p (a m)"), misc[:, 2 * P:6 * P]).then_inc(consts_cast, 1)
            dve.wait_ge(w_mm, 1)
            dve.tensor_copy(wq[:].rearrange("p a m -> p (a m)"), ps[:, BA, 0:2 * D]).then_inc(w_copied, 1)
            dve.tensor_copy(wkv[:], ps[:, BB, 0:2 * D + KVH * HD]).then_inc(w_copied, 1)

            def all_stats(sem_stats, first):
                with dve.Fori(0, NT) as t:
                    dve.bn_stats(stats[:, ds(t, 1), :].rearrange("p a s -> p (a s)"),
                                 X[:, ds(t, 1), :].rearrange("p a d -> p (a d)")).then_inc(sem_stats, 1)
                dve.wait_ge(sem_stats, first + NT)
                for t in range(NT):
                    dve.bn_aggr(mv[:, t, :], stats[:, t, :]).then_inc(sem_stats, 1)
                dve.wait_ge(sem_stats, first + 2 * NT)

            def inv_sqrt(y, v, t1, t2, eps, step, n0):
                n = n0

                def then(ins):
                    nonlocal n
                    n += 1
                    ins.then_inc(step, 1)
                    dve.wait_ge(step, n)
                then(dve.tensor_scalar(t1, v, eps, None, ALU.add))
                then(dve.tensor_scalar(y.bitcast(I32), t1.bitcast(I32), 1, None, ALU.logical_shift_right))
                then(dve.tensor_scalar(y.bitcast(I32), y.bitcast(I32), -1.0, float(MAGIC), ALU.mult, ALU.add))
                for _ in range(4):
                    then(dve.tensor_tensor(t2, y, y, ALU.mult))
                    then(dve.tensor_tensor(t2, t2, t1, ALU.mult))
                    then(dve.tensor_scalar(t2, t2, -0.5, 1.5, ALU.mult, ALU.add))
                    then(dve.tensor_tensor(y, y, t2, ALU.mult))
                return n

            dve.memset(mv[:, NT:NT + 2, :], 0.0).then_inc(stats_done, 1)
            all_stats(stats_done, 1)
            inv_sqrt(rstd[:], mv[:, :, 1], nt1[:], nt2[:], LN_EPS, rstd_step, 0)

            def norm(b, b2, r):
                for t in range(2):
                    signal(dve.tensor_scalar(xn[r][:, t, :], X[:, ds(b2 + t, 1), :].rearrange("p a d -> p (a d)"),
                                             mv[:, ds(b2 + t, 1), 0:1].rearrange("p a s -> p (a s)"),
                                             rstd[:, ds(b2 + t, 1)], ALU.subtract, ALU.mult), "normed")

            def rotate(b):
                k = 0
                wait(dve, "proj", b, 1)
                wait(dve, "sel", b, 0)
                wait(dve, "rope_step", b, 0)
                signal(dve.tensor_tensor(rot[0][:], ps[:, BA, :], rope[:, 0, :], ALU.mult), "rope_step")
                signal(dve.tensor_tensor(rot[1][:], ps[:, BB, :], rope[:, 1, :], ALU.mult), "rope_step")
                wait(dve, "rope_step", b, 2)
                signal(dve.tensor_tensor(rot[2][:], rot[0][:], rot[1][:], ALU.add), "rope_step")
                wait(dve, "rope_step", b, 3)
                signal(dve.tensor_copy(hi[:], rot[2][:]), "rope_step")
                wait(dve, "rope_step", b, 4)
                signal(dve.tensor_tensor(lo[:], rot[2][:], hi[:].bitcast(F32), ALU.subtract), "rope_step")

            def maxima(b, g):
                for u in (2 * g, 2 * g + 1):
                    s = 2 * slot_of[(1, u)]
                    wait(dve, "p1", b, u + 1)
                    if u % 2 == 0:
                        wait(dve, "msplit", b, 4 * (g - 1)) if g >= 2 else wait(dve, "msplit", b, 0)
                        wait(dve, "maxed", b, 2 * u)
                    j = 2 * (u % 2)
                    signal(dve.tensor_reduce(negm[g % 2][:, 0, j:j + 2], ps[:, s:s + 2, 0:P], AX.X, ALU.max, negate=True), "maxed")
                    signal(dve.tensor_reduce(negm[g % 2][:, 1, j:j + 2], ps[:, s:s + 2, P:3 * P], AX.X, ALU.max, negate=True), "maxed")

            def normalise_out(b):
                for t in range(2):
                    bank = ps[:, BT + t, :].rearrange("p (h c) -> p h c", c=32)
                    wait(dve, "oTT", b, t + 1)
                    wait(dve, "normed_o", b, 2 * t)
                    wait(dve, "onTr", b, 0)
                    signal(dve.reciprocal(rden[:, t, :], bank[:, :, HD]), "normed_o")
                    wait(dve, "normed_o", b, 2 * t + 1)
                    signal(dve.tensor_tensor(on[:, t], bank[:, :, 0:HD], rden[:, t, :].unsqueeze(2).broadcast_to((P, H, HD)), ALU.mult), "normed_o")

            def residual(b2, b):
                wait(dve, "outp", b, 1)
                signal(dve.tensor_tensor(X[:, ds(b2, 2), :].rearrange("p a d -> p (a d)"),
                                         X[:, ds(b2, 2), :].rearrange("p a d -> p (a d)"), ps[:, BT, 0:2 * D], ALU.add), "residual")

            norm(0, 0, 0)
            rotate(0)
            with dve.Fori(0, B // 2) as i:
                for r in range(2):
                    b = 2 * i + r
                    norm(b + 1, 4 * i + 2 * r + 2, 1 - r)
                    for g in range(G):
                        maxima(b, g)
                        if g == 1:
                            rotate(b + 1)
                    normalise_out(b)
                    residual(4 * i + 2 * r, b)
            dve.wait_ge(s0["residual"][0], B + 1)
            dve.tensor_tensor(X[:, 0:NT, :], X[:, 0:NT, :], boutb[:].unsqueeze(1).broadcast_to((P, NT, D)), ALU.add).then_inc(s0["residual"][0], 1)
            dve.wait_ge(s0["residual"][0], B + 2)

            def expert_constants(l):
                dve.wait_ge(w_loaded[l], 16 * (7 if l == 0 else 4))
                c = Chain(dve, moe_cast, 7 * l)
                if l == 0:
                    c(dve.tensor_copy(of_expert[:], YB[:].rearrange("p a s -> p (a s)")[:, 0:E * P]))
                c(dve.memset(bias3[l][:], 0.0))
                c(dve.tensor_copy(bias3[l][0:E, :], bias[l][:]))
                c(dve.tensor_tensor(bias_rest[:], bias[l][:], bias3[l][0:E, :], ALU.subtract))
                c(dve.tensor_copy(bias_mid[:], bias_rest[:]))
                c(dve.tensor_copy(bias3[l][32:32 + E, :], bias_mid[:]))
                c(dve.tensor_tensor(bias3[l][64:64 + E, :], bias_rest[:], bias_mid[:], ALU.subtract))

            def experts(l, have):
                m = ms[l]
                expert_constants(l)
                all_stats(m["stats"], 1)
                inv_sqrt(rstd[:], mv[:, :, 1], nt1[:], nt2[:], LN_EPS, m["rstd"], 1)

                def norm_pair(k, i, r):
                    dve.wait_ge(ms_rows[l][r], 16 * i + 16)
                    dve.wait_ge(m["xT"], 2 * i + 1)
                    for t in range(2):
                        dve.tensor_scalar(xn[r][:, t, :], X[:, ds(2 * k + t, 1), :].rearrange("p a d -> p (a d)"),
                                          mv[:, ds(2 * k + t, 1), 0:1].rearrange("p a s -> p (a s)"),
                                          rstd[:, ds(2 * k + t, 1)], ALU.subtract, ALU.mult).then_inc(m["normed"], 1)

                with dve.Fori(0, NT // 4) as i:
                    for r in range(2):
                        norm_pair(2 * i + r, i, r)
                    for r in range(2):
                        k = 2 * i + r
                        dve.wait_ge(m["gated"], k + 2)
                        w = D + E if l == 0 else E
                        src = ps[:, 6 + r, 0:2 * w].rearrange("p (t w) -> p t w", t=2)
                        if l == 0:
                            dve.tensor_tensor(SH[:, ds(2 * k, 2), :], src[:, :, 0:D], shared_b.unsqueeze(1).broadcast_to((P, 2, D)), ALU.add).then_inc(m["logits"], 1)
                            dve.tensor_copy(LG[:, ds(2 * k, 2), :], src[:, :, D:D + E]).then_inc(m["logits"], 1)
                        else:
                            dve.tensor_tensor(LG[:, ds(2 * k, 2), :], src, gate_b.unsqueeze(1).broadcast_to((P, 2, E)), ALU.add).then_inc(m["logits"], 1)
                dve.wait_ge(m["logits"], (NT if l == 0 else NT // 2) + 1)

                c = Chain(dve, m["routed"], 1)
                wide = lambda a: a.unsqueeze(2).broadcast_to((P, NT, E))
                for n in range(2):
                    L = LG if n == 0 else LG2
                    c(dve.tensor_reduce(top[:, n, :], L[:], AX.X, ALU.max))
                    c(dve.tensor_tensor(rt[0][:], L[:], wide(top[:, n, :]), ALU.is_ge))
                    c(dve.tensor_tensor(rt[1][:], rt[0][:], rev_e.unsqueeze(1).broadcast_to((P, NT, E)), ALU.mult))
                    c(dve.tensor_reduce(top[:, 2, :], rt[1][:], AX.X, ALU.max))
                    c(dve.tensor_tensor(first[n][:], rt[1][:], wide(top[:, 2, :]), ALU.is_equal))
                    if n == 0:
                        c(dve.scalar_tensor_tensor(LG2[:], first[0][:], LOWEST, LG[:], ALU.mult, ALU.add))
                c(dve.tensor_tensor(picked[:], first[0][:], first[1][:], ALU.add))
                c(dve.tensor_tensor(wts[:, 0, :], top[:, 1, :], top[:, 0, :], ALU.subtract))
                ROUTED = c.n
                assert ROUTED == 14
                dve.wait_ge(m["counted"], 1 + 1)
                c(dve.tensor_copy(totals[:], ps[:, BT, P:2 * P].rearrange("p (t e) -> p e t", e=E)))
                flat = lambda a: a[:].rearrange("p e t -> p (e t)")
                c(dve.tensor_tensor_scan(flat(upto), ones_m, flat(totals), 0.0, ALU.mult, ALU.add))
                last = upto[:, :, NT - 1]
                cnt, til, cum, off = (per_e[:, n, :] for n in range(4))
                c(dve.tensor_copy(cnt, last))
                c(dve.tensor_tensor(per_e[:, 4, 1:E], last[:, 1:E], last[:, 0:E - 1], ALU.subtract))
                c(dve.tensor_copy(per_e[:, 4, 0:1], last[:, 0:1]))
                num = per_e[:, 4, :]
                c(dve.tensor_scalar(per_ei[:], num, float(P - 1), None, ALU.add))
                c(dve.tensor_scalar(per_ei[:], per_ei[:], P.bit_length() - 1, None, ALU.arith_shift_right))
                c(dve.tensor_copy(til, per_ei[:]))
                c(dve.tensor_tensor_scan(cum, ones_m[:, 0:E], til, 0.0, ALU.mult, ALU.add))
                c(dve.tensor_tensor(per_e[:, 5, :], cum, til, ALU.subtract))
                c(dve.tensor_tensor(per_e[:, 6, :], num, last, ALU.subtract))
                c(dve.scalar_tensor_tensor(off, per_e[:, 5, :], float(P), per_e[:, 6, :], ALU.mult, ALU.add))
                c(dve.tensor_tensor(flat(upto), flat(upto), flat(totals), ALU.subtract))
                c(dve.tensor_tensor(upto[:], upto[:], off.unsqueeze(2).broadcast_to((P, E, NT)), ALU.add))
                c(dve.tensor_tensor(rt[0][:], ps[:, BT, 0:P].rearrange("p (t e) -> p t e", e=E), upto[:].rearrange("p e t -> p t e"), ALU.add))
                for n in range(TOPK):
                    c(dve.tensor_tensor(rt[1][:], rt[0][:], first[n][:], ALU.mult))
                    c(dve.tensor_reduce(slot[:, :, n], rt[1][:], AX.X, ALU.add))
                c(dve.tensor_copy(sloti[:, 0, :], slot[:].rearrange("p t k -> p (t k)")))
                c(dve.tensor_scalar(sloti[:, 1, :], sloti[:, 0, :], P - 1, None, ALU.bitwise_and))
                c(dve.tensor_scalar(sloti[:, 2, :], sloti[:, 0, :], P.bit_length() - 1, None, ALU.arith_shift_right))
                c(dve.tensor_copy(slotf[:], sloti[:, 1:3, :]))
                c(dve.tensor_tensor(etab[:], iota_t.unsqueeze(2).broadcast_to((P, ETS, E)), cum.unsqueeze(1).broadcast_to((P, ETS, E)), ALU.is_ge))
                c(dve.tensor_reduce(eidf[:, 0, :], etab[:], AX.X, ALU.add))
                c(dve.tensor_scalar(eidf[:, 1, :], eidf[:, 0, :], float(E - 1), None, ALU.min))
                with dve.Fori(0, NT) as t:
                    for k in range(TOPK):
                        q = 2 * t + k
                        dve.wait_ge(m["hot_used"], 2 * t + 1)
                        if k == 0:
                            dve.wait_ge(m["hot_b"], 2 * t + 1)
                        dve.tensor_scalar(hot[k][:], iota_p, slotf[:, 0, ds(q, 1)], None, ALU.is_equal).then_inc(m["hot_a"], 1)
                        dve.tensor_scalar(hotn[k][:], iota_t, slotf[:, 1, ds(q, 1)], pair_no[:, ds(q, 1)], ALU.is_equal, ALU.mult).then_inc(m["hot_b"], 1)
                dve.wait_ge(m["inverse"], 1 + 1)
                c = Chain(dve, m["tabled"], 1)
                c(dve.tensor_copy(eid[:], eidf[:, 1, :]))
                c(dve.tensor_copy(inv[:, 0, :], ps[:, BA, 0:ETS]))
                c(dve.scalar_tensor_tensor(inv[:, 1, :], inv[:, 0, :], 0.0, spare_no, ALU.is_equal, ALU.mult))
                c(dve.scalar_tensor_tensor(inv[:, 2, :], inv[:, 0, :], -1.0, inv[:, 1, :], ALU.add, ALU.add))
                c(dve.tensor_copy(tab[:, 0, :], inv[:, 2, :]))
                c(dve.tensor_scalar(tab[:, 1, :], tab[:, 0, :], 1, None, ALU.arith_shift_right))

                c = Chain(dve, m["mixed"], 1)
                if l == 0:
                    dve.wait_ge(m["exp_diff"], 1 + 1)
                    c(dve.tensor_scalar(wts[:, 2, :], wts[:, 1, :], 1.0, None, ALU.add))
                    c(dve.reciprocal(wts[:, 3, :], wts[:, 2, :]))
                    c(dve.tensor_tensor(wts[:, 4, :], wts[:, 3, :], wts[:, 1, :], ALU.mult))
                n_mixed = c.n

                with dve.Fori(0, ET // 2) as i:
                    for r in range(2):
                        n = 2 * i + r
                        dve.wait_ge(m["h_turned"], n + 2)
                        dve.wait_ge(m["y_ready"], n + 1)
                        dve.tensor_copy(hidT[r][:], ps[:, 2 + r, :]).then_inc(m["h_copied"], 1)
                        dve.wait_ge(m["y_ready"], n + 2)
                        dve.wait_ge(ms_scat[l][r], 16 * i + 16)
                        dve.tensor_copy(yt[r][:], ps[:, 6 + r, 0:D]).then_inc(m["y_copied"], 1)

                if l == 0:
                    dve.wait_ge(m["gelu"], 1 + 1)
                    c(dve.tensor_scalar(SH[:], SH[:], 0.5, None, ALU.mult))
                for t in range(NT):
                    if t % 4 == 0:
                        dve.wait_ge(ms_back[l][t // 4], 16)
                    for k in range(TOPK):
                        if l == 0:
                            dve.wait_ge(m["mixed"], c.n)
                            c.n += 1
                            dve.scalar_tensor_tensor(SH[:, t, :], YB[:, t, k * D:(k + 1) * D], wts[:, 3 + k, t:t + 1], SH[:, t, :], ALU.mult, ALU.add).then_inc(m["mixed"], 1)
                if l == 1:
                    for q in range(4):
                        dve.wait_ge(ms_back[l][q], 16)
                    c(dve.tensor_tensor(X[:, 0:NT, :], X[:, 0:NT, :], YB[:, :, 0:D], ALU.add))
                    dve.tensor_tensor(X[:, 0:NT, :], X[:, 0:NT, :], YB[:, :, D:], ALU.add).then_inc(m["combined"], 1)
                    return
                dve.wait_ge(m["mixed"], c.n)
                for t in range(NT):
                    c.add(dve.bn_stats(stats[:, t, :], SH[:, t, :]))
                c.wait()
                for t in range(NT):
                    c.add(dve.bn_aggr(mv[:, t, :], stats[:, t, :]))
                c.wait()
                c.n = inv_sqrt(rstd[:], mv[:, :, 1], nt1[:], nt2[:], LN_EPS, m["mixed"], c.n)
                for t in range(NT):
                    c.add(dve.tensor_scalar(SH[:, t, :], SH[:, t, :], mv[:, t, 0:1], rstd[:, t:t + 1], ALU.subtract, ALU.mult))
                c.wait()
                row = lambda a: a.unsqueeze(1).broadcast_to((P, NT, D))
                c(dve.tensor_tensor(SH[:], SH[:], row(gamma), ALU.mult))
                c(dve.tensor_tensor(SH[:], SH[:], row(beta), ALU.add))
                dve.tensor_tensor(X[:, 0:NT, :], X[:, 0:NT, :], SH[:], ALU.add).then_inc(m["combined"], 1)

            def look_up():
                all_stats(ls["stats"], 1)
                n = inv_sqrt(rstd[:], mv[:, :, 1], nt1[:], nt2[:], LN_EPS, ls["rstd"], 1)
                c = Chain(dve, ls["rstd"], n)
                c(dve.tensor_tensor(rms[:, 0, :], rstd[:], rstd[:], ALU.mult))
                c(dve.tensor_tensor(rms[:, 1, :], rms[:, 0, :], mv[:, :, 1], ALU.mult))
                c.n = inv_sqrt(rms[:, 2, :], rms[:, 1, :], nt1[:], nt2[:], RMS_EPS, ls["rstd"], c.n)
                c(dve.tensor_tensor(rms[:, 0, :], rms[:, 2, :], rstd[:], ALU.mult))
                dve.wait_ge(look_loaded, 48)
                dve.tensor_scalar(wqkv[:], w_look[:, 0:3, :], norm_w[:], None, ALU.mult).then_inc(ls["w_scaled"], 1)
                with dve.Fori(0, NT // 4) as i:
                    for r in range(2):
                        k = 2 * i + r
                        dve.wait_ge(ls["scores"], 2 * i + 1)
                        for t in range(2):
                            dve.tensor_scalar(xn[r][:, t, :], X[:, ds(2 * k + t, 1), :].rearrange("p a d -> p (a d)"),
                                              mv[:, ds(2 * k + t, 1), 0:1].rearrange("p a s -> p (a s)"),
                                              rstd[:, ds(2 * k + t, 1)], ALU.subtract, ALU.mult).then_inc(ls["normed"], 1)
                    for r in range(2):
                        k = 2 * i + r
                        dve.wait_ge(ls["u_copied"], k + 2)
                        dve.wait_ge(ls["means"], k + 2)
                        dve.wait_ge(ls["um"], 2 * (2 * i) + 1)
                        dve.tensor_tensor(um[r], usb[r], ps[:, 6 + r, 0:2 * D], ALU.mult).then_inc(ls["um"], 1)
                        dve.wait_ge(ls["um"], 2 * k + 2)
                        dve.tensor_reduce(SC[:, ds(2 * k, 2), NC:NC + 1].rearrange("p a o -> p (a o)"), um[r].rearrange("p (t d) -> p t d", t=2), AX.X, ALU.add).then_inc(ls["um"], 1)
                        dve.wait_ge(ls["scores"], k + 2)
                        dve.tensor_tensor(SC[:, ds(2 * k, 2), 0:NC], ps[:, 2 + r, 2 * NC:4 * NC].rearrange("p (t n) -> p t n", t=2),
                                          unseen.rearrange("p (t n) -> p t n", t=2), ALU.add).then_inc(ls["gate_in"], 1)
                dve.wait_ge(ls["gate_in"], NT // 2 + 1)
                c = Chain(dve, ls["soft"], 1)
                wide = lambda a: a.unsqueeze(2).broadcast_to((P, NT, NC + 1))
                c(dve.tensor_reduce(sct[:, 0, :], SC[:], AX.X, ALU.max))
                c(dve.tensor_tensor(SCd[:], SC[:], wide(sct[:, 0, :]), ALU.subtract))
                dve.wait_ge(ls["soft_exp"], 1 + 1)
                c(dve.tensor_reduce(sct[:, 1, :], SC[:], AX.X, ALU.add))
                c(dve.reciprocal(sct[:, 2, :], sct[:, 1, :]))
                c(dve.tensor_tensor(GT[:, 0:NT, :], SC[:], wide(sct[:, 2, :]), ALU.mult))

            def norm1(b, b2, r):
                for t in range(2):
                    signal(dve.tensor_scalar(xn[r][:, t, :], X[:, ds(b2 + t, 1), :].rearrange("p a d -> p (a d)"),
                                             mv[:, ds(b2 + t, 1), 0:1].rearrange("p a s -> p (a s)"),
                                             rms[:, 0, ds(b2 + t, 1)], ALU.subtract, ALU.mult), "normed")

            def elu(b, r):
                wait(dve, "proj", b, 1)
                wait(dve, "sel", b, 0)
                wait(dve, "elu_step", b, 0)
                signal(dve.tensor_scalar(rot[0][:], ps[:, BA, :], 0.0, None, ALU.min), "elu_step")
                wait(dve, "elu_exp", b, 1)
                signal(dve.scalar_tensor_tensor(pqk[r][:], ps[:, BA, :], 0.0, rot[1][:], ALU.max, ALU.add), "elu_step")
                wait(dve, "elu_step", b, 2)
                signal(dve.tensor_copy(hi[:], pqk[r][:]), "elu_step")
                wait(dve, "elu_step", b, 3)
                signal(dve.tensor_tensor(lo[:], pqk[r][:], hi[:].bitcast(F32), ALU.subtract), "elu_step")

            def normalise_out1(b):
                for t in range(2):
                    bank = ps[:, BT + t, :].rearrange("p (h c) -> p h c", c=32)
                    wait(dve, "oTT", b, t + 1)
                    wait(dve, "normed_o", b, 3 * t)
                    wait(dve, "onTr", b, 0)
                    signal(dve.tensor_scalar(rden[:, t, :], bank[:, :, HD], RMS_EPS, None, ALU.add), "normed_o")
                    wait(dve, "normed_o", b, 3 * t + 1)
                    signal(dve.reciprocal(rden[:, t, :], rden[:, t, :]), "normed_o")
                    wait(dve, "normed_o", b, 3 * t + 2)
                    signal(dve.tensor_tensor(on[:, t], bank[:, :, 0:HD], rden[:, t, :].unsqueeze(2).broadcast_to((P, H, HD)), ALU.mult), "normed_o")

            def own_states(b):
                for n, c in ((0, 4), (1, NS - 4)):
                    wait(dve, "state", b, n + 1)
                    wait(dve, "looked", b, 0)
                    signal(dve.tensor_tensor(states[:, 4 * n:4 * n + c, :], ps[:, BA + n, 0:c * D].rearrange("p (n d) -> p n d", d=D),
                                             own_head.unsqueeze(1).broadcast_to((P, c, D)), ALU.mult), "state_own")

            def retrieve(b, b2):
                wait(dve, "looked", b, 1)
                wait(dve, "residual", b, 0)
                where = [[(2, n) for n in range(3)], [(0, n) for n in range(4)] + [(1, n) for n in range(3)]]
                k = 0
                for n in range(NS):
                    for t in range(2):
                        if n >= len(where[t]):
                            continue
                        bank, at = where[t][n]
                        gate = GT[:, ds(b2 + t, 1), n:n + 1].rearrange("p a n -> p (a n)")
                        src = ps[:, bank, at * D:(at + 1) * D]
                        if n == 0:
                            signal(dve.tensor_scalar(found[:, t, :], src, gate, None, ALU.mult), "found")
                        else:
                            wait(dve, "found", b, k - (1 if n < 3 else 0)) if n <= 3 else wait(dve, "found", b, k)
                            signal(dve.scalar_tensor_tensor(found[:, t, :], src, gate, found[:, t, :], ALU.mult, ALU.add), "found")
                        k += 1

            def residual1(b, b2):
                for t in range(2):
                    signal(dve.tensor_scalar(zt[:, t, :], X[:, ds(b2 + t, 1), :].rearrange("p a d -> p (a d)"),
                                             mv[:, ds(b2 + t, 1), 0:1].rearrange("p a s -> p (a s)"),
                                             rstd[:, ds(b2 + t, 1)], ALU.subtract, ALU.mult), "residual")
                wait(dve, "outp", b, 1)
                wait(dve, "residual", b, 2)
                flat = lambda a: a.rearrange("p t d -> p (t d)")
                signal(dve.tensor_tensor(flat(zt), flat(zt), ps[:, BT, 0:2 * D], ALU.add), "residual")
                wait(dve, "residual", b, 3)
                wait(dve, "found", b, 10)
                for t in range(2):
                    gate = GT[:, ds(b2 + t, 1), NC:NC + 1].rearrange("p a n -> p (a n)")
                    signal(dve.scalar_tensor_tensor(zt[:, t, :], zt[:, t, :], gate, found[:, t, :], ALU.mult, ALU.add), "residual")
                wait(dve, "residual", b, 5)
                signal(dve.tensor_tensor(X[:, ds(b2, 2), :], X[:, ds(b2, 2), :], zt, ALU.add), "residual")

            if last_stage >= 1:
                experts(0, 0)
            if last_stage >= 2:
                dve.wait_ge(ms[0]["combined"], 1 + 1)
                look_up()
                tables.append(s1)
                norm1(0, 0, 0)
                elu(0, 0)
                with dve.Fori(0, B // 2) as i:
                    for r in range(2):
                        b, b2 = 2 * i + r, 4 * i + 2 * r
                        norm1(b + 1, b2 + 2, 1 - r)
                        elu(b + 1, 1 - r)
                        normalise_out1(b)
                        own_states(b)
                        retrieve(b, b2)
                        residual1(b, b2)
                tables.pop()
                dve.wait_ge(s1["residual"][0], 6 * B + 1)
            if last_stage >= 3:
                experts(1, 0)

        @block.scalar
        def _(act):
            def copy_xT(b, r):
                wait(act, "xT", b, 1)
                signal(act.activation(xnT[r][:], ps[:, BT, 0:S], ACT.Copy), "xT_copied")

            def copy_v(b, r):
                wait(act, "proj", b, 1)
                signal(act.activation(vst[r][:, :, 0:KVH, 0:HD], ps[:, BT, S:S + 2 * KVH * HD].rearrange("p (t h d) -> p t h d", t=2, d=HD), ACT.Copy), "v_copied")

            def stack(b, r, n):
                wait(act, "sel", b, n + 1)
                dst = (qst if n < 2 else kst)[r][:, 2 * (n % 2):2 * (n % 2) + 2, :]
                signal(act.activation(dst.rearrange("p g s -> p (g s)"), ps[:, BA + n % 2, :], ACT.Copy), "stacked")

            def copy_mT(b, g):
                wait(act, "mTr", b, g + 1)
                src = ps[0:12, BO, 0:P].bitcast(BF16)
                signal(act.activation(mT[g % 2][0:12, :], src, ACT.Copy), "mT_copied")

            def exps(b, g):
                for u in (2 * g, 2 * g + 1):
                    s = 2 * slot_of[(2, u)]
                    wait(act, "p2", b, u + 1)
                    if u % 2 == 0:
                        wait(act, "pv", b, max(g - 1, 0))
                    signal(act.activation(probs[g % 2][:, 2 * (u % 2):2 * (u % 2) + 2, :], ps[:, s:s + 2, 0:3 * P], ACT.Exp, scale=QK_SCALE), "probs_done")

            def copy_o(b, g):
                wait(act, "pv", b, g + 1)
                signal(act.activation(oT[:, g, :], ps[:, BO, 0:S], ACT.Copy), "o_copied")

            def copy_onT(b):
                wait(act, "onTr", b, 1)
                signal(act.activation(onT[:], ps[:, BB, 0:S], ACT.Copy), "onT_copied")

            act.wait_ge(init_done, 7)
            copy_xT(0, 0)
            copy_v(0, 0)
            for n in range(4):
                stack(0, 0, n)
            with act.Fori(0, B // 2) as i:
                for r in range(2):
                    b = 2 * i + r
                    for g in range(G + 1):
                        if g == 0:
                            copy_xT(b + 1, 1 - r)
                        if g > 0:
                            copy_mT(b, g - 1)
                            exps(b, g - 1)
                        if g == 1:
                            copy_v(b + 1, 1 - r)
                        if g == 2:
                            stack(b + 1, 1 - r, 0)
                            stack(b + 1, 1 - r, 1)
                        if g == 3:
                            stack(b + 1, 1 - r, 2)
                            stack(b + 1, 1 - r, 3)
                        if g > 1:
                            copy_o(b, g - 2)
                    copy_o(b, G - 1)
                    copy_onT(b)

            def experts(l):
                m = ms[l]
                with act.Fori(0, NT // 4) as i:
                    for r in range(2):
                        k = 2 * i + r
                        act.wait_ge(m["xT"], k + 2)
                        act.wait_ge(m["gated"], 2 * i + 1)
                        act.activation(xnT[r][:], ps[:, BT + r, 0:S], ACT.Copy).then_inc(m["xT_copied"], 1)
                if l == 0:
                    act.wait_ge(m["routed"], 13 + 1)
                    act.activation(wts[:, 1, :], wts[:, 0, :], ACT.Exp).then_inc(m["exp_diff"], 1)
                    act.wait_ge(m["logits"], NT + 1)
                    act.activation(SH[:], SH[:], ACT.Gelu).then_inc(m["gelu"], 1)

                def tile(n, r):
                    act.wait_ge(m["x_turned"], n + 2)
                    act.activation(xgT[r][:], ps[:, 4 + r, 0:P], ACT.Copy).then_inc(m["x_copied"], 1)
                    act.wait_ge(m["h_ready"], n + 2)
                    act.activation(hid[r][:], ps[:, r, :], ACT.Gelu if l == 0 else ACT.Relu).then_inc(m["h_active"], 1)
                tile(0, 0)
                with act.Fori(0, ET // 2) as i:
                    for r in range(2):
                        act.wait_ge(m["h_turned"], 2 * i + r + 1)
                        tile(2 * i + r + 1, 1 - r)

            def look_up():
                with act.Fori(0, NT // 4) as i:
                    for r in range(2):
                        k = 2 * i + r
                        act.wait_ge(ls["zT"], k + 2)
                        act.activation(xnT[r][:], ps[:, BT + r, 0:S], ACT.Copy).then_inc(ls["zT_copied"], 1)
                    for r in range(2):
                        k = 2 * i + r
                        act.wait_ge(ls["means"], k + 2)
                        act.wait_ge(ls["um"], 4 * i + 1)
                        act.activation(usb[r], ps[:, r, 0:2 * D], ACT.Copy).then_inc(ls["u_copied"], 1)
                        act.activation(means[r][:], ps[:, 2 + r, 0:NC], ACT.Copy).then_inc(ls["means_copied"], 1)
                    for r in range(2):
                        act.wait_ge(ls["wmeans"], 2 * i + r + 2)
                        act.activation(wmeans[r][:], ps[:, 2 + r, NC:2 * NC], ACT.Copy).then_inc(ls["wmeans_copied"], 1)
                act.wait_ge(ls["soft"], 2 + 1)
                act.activation(SC[:], SCd[:], ACT.Exp, scale=float(D) ** -0.5).then_inc(ls["soft_exp"], 1)

            def elu_exp(b):
                wait(act, "elu_step", b, 1)
                signal(act.activation(rot[1][:], rot[0][:], ACT.Exp), "elu_exp")

            def copy_v1(b, r):
                wait(act, "proj", b, 1)
                signal(act.activation(vst[r][:, :, :, 0:HD], ps[:, BT, S:2 * S].rearrange("p (t h d) -> p t h d", t=2, d=HD), ACT.Copy), "v_copied")

            def products(b, g):
                for u in (2 * g, 2 * g + 1):
                    s = 2 * (u % 2)
                    wait(act, "p2", b, u + 1)
                    if u % 2 == 0:
                        wait(act, "pv", b, max(g - 1, 0))
                    signal(act.activation(probs[g % 2][:, 2 * (u % 2):2 * (u % 2) + 2, :], ps[:, s:s + 2, 0:3 * P], ACT.Copy), "probs_done")

            def copy_pk(b, r):
                wait(act, "pkT", b, 1)
                signal(act.activation(pkt[r][:].rearrange("p t d -> p (t d)"), ps[:, BB, 0:2 * D], ACT.Copy), "pk_copied")

            if last_stage >= 1:
                experts(0)
            if last_stage >= 2:
                look_up()
                tables.append(s1)
                copy_xT(0, 0)
                elu_exp(0)
                copy_v1(0, 0)
                copy_pk(0, 0)
                for n in range(4):
                    stack(0, 0, n)
                with act.Fori(0, B // 2) as i:
                    for r in range(2):
                        b = 2 * i + r
                        for g in range(G):
                            products(b, g)
                            if g == 0:
                                copy_xT(b + 1, 1 - r)
                            if g == 1:
                                elu_exp(b + 1)
                                copy_v1(b + 1, 1 - r)
                            if g == 2:
                                copy_pk(b + 1, 1 - r)
                                stack(b + 1, 1 - r, 0)
                                stack(b + 1, 1 - r, 1)
                            if g == 3:
                                stack(b + 1, 1 - r, 2)
                                stack(b + 1, 1 - r, 3)
                            if g > 0:
                                copy_o(b, g - 1)
                        copy_o(b, G - 1)
                        copy_onT(b)
                tables.pop()
            if last_stage >= 3:
                experts(1)

        @block.tensor
        def _(pe):
            pe.wait_ge(loaded, 16 * NLOAD)
            pe.matmul(ps[:, BA, 0:2 * D], wqa_t[:], wqb[:], start=True, stop=True)
            pe.matmul(ps[:, BB, 0:2 * D + KVH * HD], wkva_t[:], wkvb[:], start=True, stop=True).then_inc(w_mm, 1)
            pe.wait_ge(consts_cast, 5)
            pe.wait_ge(w_copied, 2)
            pe.wait_ge(init_done, 7)

            def turn_x(b, r):
                wait(pe, "normed", b, 2)
                wait(pe, "v_copied", b, 0)
                wait(pe, "xT_copied", b, 0)
                wait(pe, "residual", b - 1, 0) if r == 0 and False else None
                for t in range(2):
                    mm = pe.transpose(ps[:, BT, t * P:(t + 1) * P], xn[r][:, t, :], ident)
                signal(mm, "xT")

            def project(b, r):
                wait(pe, "xT_copied", b, 1)
                wait(pe, "stacked", b, 0)
                pe.matmul(ps[:, BA, 0:S], wq[:, 0, :], xnT[r][:], start=True, stop=True)
                pe.matmul(ps[:, BA, S:2 * S], wkv[:, 0:D], xnT[r][:], start=True, stop=True)
                pe.matmul(ps[:, BB, 0:S], wq[:, 1, :], xnT[r][:], start=True, stop=True)
                pe.matmul(ps[:, BB, S:2 * S], wkv[:, D:2 * D], xnT[r][:], start=True, stop=True)
                for t in range(2):
                    c = S + t * KVH * HD
                    mm = pe.matmul(ps[:, BT, c:c + KVH * HD], xnT[r][:, t * P:(t + 1) * P], wkv[:, 2 * D:], start=True, stop=True)
                signal(mm, "proj")

            def spread(b, n):
                if tables[-1] is s0:
                    wait(pe, "rope_step", b, 5)
                else:
                    wait(pe, "elu_step", b, 4)
                    wait(pe, "pk_copied", b, 1)
                if n >= 2:
                    wait(pe, "stacked", b, n - 1)
                c = 0 if n < 2 else S
                for gg in range(2):
                    g = 2 * (n % 2) + gg
                    w = 0 if n < 2 else 2
                    dst = ps[:, BA + n % 2, gg * S:(gg + 1) * S]
                    pe.matmul(dst, selr[:, w, g, :], hi[:, c:c + S], start=True, stop=False)
                    mm = pe.matmul(dst, selr[:, w + 1, g, :], lo[:, c:c + S], start=False, stop=True)
                signal(mm, "sel")

            def ring(b, use):
                prev = before[use]
                if prev is None:
                    wait(pe, "probs_done", b, 0)
                elif prev[0] == 1:
                    wait(pe, "maxed", b, 2 * prev[1] + 2)
                else:
                    wait(pe, "probs_done", b, prev[1] + 1)
                return 2 * slot_of[use]

            def max_scores(b, r, u):
                g, s = u // 2, ring(b, (1, u))
                for c in range(2):
                    j = 2 * (u % 2) + c
                    q, k = qst[r][32 * j:32 * j + 32, g, :], kst[r][32 * j:32 * j + 32, g, :]
                    pe.matmul(ps[:, s + c, 0:P], q[:, 0:P], k[:, 0:P], start=True, stop=False)
                    pe.matmul(ps[:, s + c, 0:P], identb[:], aboveb[:], start=False, stop=True)
                    pe.matmul(ps[:, s + c, P:3 * P], q[:, P:S], k[:, 0:S], start=True, stop=False)
                    mm = pe.matmul(ps[:, s + c, 2 * P:3 * P], identb[:], aboveb[:], start=False, stop=True)
                signal(mm, "p1")

            def turn_max(b, g):
                wait(pe, "msplit", b, 4 * g + 4)
                wait(pe, "o_copied", b, max(g - 1, 0))
                wait(pe, "mT_copied", b, g)
                dst = ps[0:12, BO, 0:P].bitcast(BF16)
                for t in range(2):
                    mm = pe.transpose(dst[:, t * P:(t + 1) * P], mparts[g % 2][:, t].rearrange("p a j -> p (a j)"), identb[:])
                signal(mm, "mTr")

            def prob_scores(b, r, u):
                g, s = u // 2, ring(b, (2, u))
                wait(pe, "mT_copied", b, g + 1)
                for c in range(2):
                    j = 2 * (u % 2) + c
                    q, k = qst[r][32 * j:32 * j + 32, g, :], kst[r][32 * j:32 * j + 32, g, :]
                    pe.matmul(ps[:, s + c, 0:S], k[:, 0:P], q[:, 0:S], start=True, stop=False)
                    pe.matmul(ps[:, s + c, 0:S], pickb[:, j, :], mT[g % 2][:, 0:S], start=False, stop=True)
                    pe.matmul(ps[:, s + c, S:3 * P], k[:, P:S], q[:, P:S], start=True, stop=False)
                    mm = pe.matmul(ps[:, s + c, S:3 * P], pickb[:, j, :], mT[g % 2][:, P:S], start=False, stop=True)
                signal(mm, "p2")

            def weigh(b, r, g):
                wait(pe, "masked", b, g + 1)
                wait(pe, "o_copied", b, g)
                if tables[-1] is s0:
                    wait(pe, "mT_copied", b, min(g + 2, G))
                for j in range(4):
                    pe.matmul(ps[32 * j:32 * j + 32, BO, 0:S], vst[r][:, 0, g if tables[-1] is s0 else 4 * g + j, :], probs[g % 2][:, j, 0:S], start=True, stop=False)
                for j in range(4):
                    mm = pe.matmul(ps[32 * j:32 * j + 32, BO, P:S], vst[r][:, 1, g if tables[-1] is s0 else 4 * g + j, :], probs[g % 2][:, j, S:3 * P], start=False, stop=True)
                signal(mm, "pv")

            def finish(b):
                wait(pe, "o_copied", b, 4)
                wait(pe, "stacked", b + 1, 4)
                wait(pe, "v_copied", b + 1, 1)
                for t in range(2):
                    for g in range(G):
                        mm = pe.transpose(ps[:, BT + t, g * P:(g + 1) * P], oT[:, g, t * P:(t + 1) * P], ident)
                    signal(mm, "oTT")
                for t in range(2):
                    wait(pe, "normed_o", b, (2 if tables[-1] is s0 else 3) * (t + 1))
                    mm = pe.transpose(ps[:, BB, t * P:(t + 1) * P], on[:, t].rearrange("p h d -> p (h d)"), ident)
                signal(mm, "onTr")
                wait(pe, "onT_copied", b, 1)
                for t in range(2):
                    mm = pe.matmul(ps[:, BT, t * P:(t + 1) * P], onT[:, t * P:(t + 1) * P], wout[:] if tables[-1] is s0 else w_look[:, 3, :], start=True, stop=True)
                signal(mm, "outp")

            turn_x(0, 0)
            project(0, 0)
            for n in range(4):
                spread(0, n)
            with pe.Fori(0, B // 2) as i:
                for r in range(2):
                    b = 2 * i + r
                    for g in range(G + 1):
                        if g < G:
                            if g == 0:
                                wait(pe, "stacked", b, 4)
                                wait(pe, "v_copied", b, 1)
                            max_scores(b, r, 2 * g)
                            max_scores(b, r, 2 * g + 1)
                        if g > 0:
                            turn_max(b, g - 1)
                        if g == 0:
                            wait(pe, "residual", b, 0)
                            turn_x(b + 1, 1 - r)
                        if g > 0:
                            prob_scores(b, r, 2 * g - 2)
                            prob_scores(b, r, 2 * g - 1)
                        if g == 1:
                            project(b + 1, 1 - r)
                        if g == 2:
                            spread(b + 1, 0)
                            spread(b + 1, 1)
                        if g == 3:
                            spread(b + 1, 2)
                            spread(b + 1, 3)
                        if g > 1:
                            weigh(b, r, g - 2)
                    weigh(b, r, G - 1)
                    finish(b)

            def experts(l):
                m = ms[l]
                pe.wait_ge(w_loaded[l], 16 * (7 if l == 0 else 4))

                def turn_pair(k, i, r):
                    pe.wait_ge(m["normed"], 2 * k + 2 + 1)
                    pe.wait_ge(m["xT_copied"], 2 * i + 1)
                    for t in range(2):
                        mm = pe.transpose(ps[:, BT + r, t * P:(t + 1) * P], xn[r][:, t, :], ident)
                    mm.then_inc(m["xT"], 1)

                w = D + E if l == 0 else E
                per = 2 if l == 0 else 1
                with pe.Fori(0, NT // 4) as i:
                    for r in range(2):
                        turn_pair(2 * i + r, i, r)
                    for r in range(2):
                        k = 2 * i + r
                        pe.wait_ge(m["xT_copied"], k + 2)
                        pe.wait_ge(m["logits"], 2 * i * per + 1)
                        for t in range(2):
                            mm = pe.matmul(ps[:, 6 + r, t * w:(t + 1) * w], xnT[r][:, t * P:(t + 1) * P], gates[l][:], start=True, stop=True)
                        mm.then_inc(m["gated"], 1)
                pe.wait_ge(m["routed"], 13 + 1)
                picks = picked[:].rearrange("p t e -> p (t e)")
                pe.matmul(ps[:, BT, 0:P], before_m, picks, start=True, stop=True)
                pe.matmul(ps[:, BT, P:2 * P], ones_m, picks, start=True, stop=True).then_inc(m["counted"], 1)
                nothing = X[:, NT, :]
                pe.matmul(ps[:, BA, 0:ETS], nothing, iota_t, start=True, stop=False)
                with pe.Fori(0, NT) as t:
                    for k in range(TOPK):
                        pe.wait_ge(m["hot_b"], 2 * t + k + 2)
                        pe.matmul(ps[:, BA, 0:ETS], hot[k][:], hotn[k][:], start=False, stop=False).then_inc(m["hot_used"], 1)
                pe.matmul(ps[:, BA, 0:ETS], nothing, iota_t, start=False, stop=True).then_inc(m["inverse"], 1)
                pe.wait_ge(m["tabled"], 6 + 1)
                pe.wait_ge(moe_cast, 7 + 6 * l)

                def into_hidden(n, i, r):
                    e = pe.value_load(eid[0:1, ds(n, 1)], min_val=0, max_val=E - 1)
                    pe.wait_ge(ms_gath[l][r], 16 * i + 16)
                    pe.transpose(ps[:, 4 + r, 0:P], xg[r][:], ident).then_inc(m["x_turned"], 1)
                    pe.matmul(ps[:, r, :], of_expert[:, ds(e * P, P)], bias3[l][:, 0:FF], start=True, stop=False)
                    pe.wait_ge(m["x_copied"], n + 2)
                    pe.matmul(ps[:, r, :], xgT[r][:], w1[:, ds(e * FF, FF)], start=False, stop=True).then_inc(m["h_ready"], 1)

                def out_of_hidden(n, r):
                    e = pe.value_load(eid[0:1, ds(n, 1)], min_val=0, max_val=E - 1)
                    pe.wait_ge(m["h_active"], n + 2)
                    for c in range(FC):
                        mm = pe.transpose(ps[:, 2 + r, c * P:(c + 1) * P], hid[r][:, c * P:(c + 1) * P], ident)
                    mm.then_inc(m["h_turned"], 1)
                    pe.matmul(ps[:, 6 + r, 0:D], of_expert[:, ds(e * P, P)], bias3[l][:, FF:], start=True, stop=False)
                    pe.wait_ge(m["h_copied"], n + 2)
                    for c in range(FC):
                        mm = pe.matmul(ps[:, 6 + r, 0:D], hidT[r][:, c * P:(c + 1) * P], w2[:, ds(e * FF + c * D, D)], start=False, stop=(c == FC - 1))
                    mm.then_inc(m["y_ready"], 1)

                into_hidden(0, 0, 0)
                with pe.Fori(0, ET // 2) as i:
                    for r in range(2):
                        n = 2 * i + r
                        pe.wait_ge(m["y_copied"], n + 1)
                        into_hidden(n + 1, i + r, 1 - r)
                        out_of_hidden(n, r)

            def look_up():
                pe.wait_ge(look_loaded, 48)
                with pe.Fori(0, NT // 4) as i:
                    for r in range(2):
                        k = 2 * i + r
                        pe.wait_ge(ls["normed"], 2 * k + 2 + 1)
                        pe.wait_ge(ls["zT_copied"], 2 * i + 1)
                        for t in range(2):
                            mm = pe.transpose(ps[:, BT + r, t * P:(t + 1) * P], xn[r][:, t, :], ident)
                        mm.then_inc(ls["zT"], 1)
                    for r in range(2):
                        k = 2 * i + r
                        pe.wait_ge(ls["gate_in"], 2 * i + 1)
                        pe.wait_ge(ls["zT_copied"], k + 2)
                        for t in range(2):
                            pe.matmul(ps[:, 6 + r, t * D:(t + 1) * D], running, xn[r][:, t, :], start=True, stop=True)
                            pe.matmul(ps[:, r, t * D:(t + 1) * D], xnT[r][:, t * P:(t + 1) * P], w_look[:, 4, :], start=True, stop=True)
                            mm = pe.matmul(ps[:, 2 + r, 4 * t:4 * t + 4], xn[r][:, t, :], chunk_mean, start=True, stop=True)
                        mm.then_inc(ls["means"], 1)
                    for r in range(2):
                        pe.wait_ge(ls["means_copied"], 2 * i + r + 2)
                        pe.matmul(ps[:, 2 + r, NC:2 * NC], w_look[:, 5, :], means[r][:], start=True, stop=True).then_inc(ls["wmeans"], 1)
                    for r in range(2):
                        pe.wait_ge(ls["wmeans_copied"], 2 * i + r + 2)
                        for t in range(2):
                            mm = pe.matmul(ps[:, 2 + r, (2 + t) * NC:(3 + t) * NC], xnT[r][:, t * P:(t + 1) * P], wmeans[r][:], start=True, stop=True)
                        mm.then_inc(ls["scores"], 1)

            def project1(b, r):
                wait(pe, "xT_copied", b, 1)
                wait(pe, "stacked", b, 0)
                for n in range(2):
                    pe.matmul(ps[:, BA, n * S:(n + 1) * S], wqkv[:, n, :], xnT[r][:], start=True, stop=True)
                for t in range(2):
                    mm = pe.matmul(ps[:, BT, S + t * D:S + (t + 1) * D], xnT[r][:, t * P:(t + 1) * P], wqkv[:, 2, :], start=True, stop=True)
                signal(mm, "proj")

            def turn_keys(b, r):
                wait(pe, "elu_step", b, 2)
                for t in range(2):
                    mm = pe.transpose(ps[:, BB, t * D:(t + 1) * D], pqk[r][:, S + t * P:S + (t + 1) * P], ident)
                signal(mm, "pkT")

            def product_scores(b, r, u):
                g, s = u // 2, 2 * (u % 2)
                wait(pe, "probs_done", b, max(u - 1, 0))
                if u < 2:
                    wait(pe, "found", b, 0)
                for c in range(2):
                    j = 2 * (u % 2) + c
                    q, k = qst[r][32 * j:32 * j + 32, g, :], kst[r][32 * j:32 * j + 32, g, :]
                    pe.matmul(ps[:, s + c, 0:S], k[:, 0:P], q[:, 0:S], start=True, stop=True)
                    mm = pe.matmul(ps[:, s + c, S:3 * P], k[:, P:S], q[:, P:S], start=True, stop=True)
                signal(mm, "p2")

            def chunk_states(b, r):
                wait(pe, "normed_o", b, 6)
                for n in range(NS):
                    rows_n = SEG * (n % 4 + 1)
                    dst = ps[:, BA + n // 4, (n % 4) * D:(n % 4 + 1) * D].rearrange("p (h d) -> p h d", d=HD)
                    if n == 4:
                        wait(pe, "onT_copied", b, 1)
                    if n >= 4:
                        pe.matmul(dst, pkt[r][:, 0, :], vst[r][:, 0, :, 0:HD], start=True, stop=False)
                    mm = pe.matmul(dst, pkt[r][0:rows_n, n // 4, :], vst[r][0:rows_n, n // 4, :, 0:HD], start=(n < 4), stop=True)
                    if n in (3, NS - 1):
                        signal(mm, "state")

            def look_states(b, r):
                wait(pe, "probs_done", b, 8)
                wait(pe, "state_own", b, 2)
                q = pqk[r]
                pe.matmul(ps[:, 2, 0:3 * D], q[:, 0:P], states[:, 0:3, :], start=True, stop=True)
                pe.matmul(ps[:, 0, 0:4 * D], q[:, P:S], states[:, 0:4, :], start=True, stop=True)
                mm = pe.matmul(ps[:, 1, 0:3 * D], q[:, P:S], states[:, 4:7, :], start=True, stop=True)
                signal(mm, "looked")

            if last_stage >= 1:
                experts(0)
            if last_stage >= 2:
                look_up()
                tables.append(s1)
                pe.wait_ge(ls["w_scaled"], 1 + 1)
                pe.wait_ge(ls["gate_in"], NT // 2 + 1)
                turn_x(0, 0)
                project1(0, 0)
                turn_keys(0, 0)
                for n in range(4):
                    spread(0, n)
                with pe.Fori(0, B // 2) as i:
                    for r in range(2):
                        b = 2 * i + r
                        for g in range(G):
                            if g == 0:
                                wait(pe, "stacked", b, 4)
                                wait(pe, "v_copied", b, 1)
                            product_scores(b, r, 2 * g)
                            product_scores(b, r, 2 * g + 1)
                            if g == 0:
                                wait(pe, "residual", b, 0)
                                turn_x(b + 1, 1 - r)
                            if g == 1:
                                project1(b + 1, 1 - r)
                            if g == 2:
                                turn_keys(b + 1, 1 - r)
                                spread(b + 1, 0)
                                spread(b + 1, 1)
                            if g == 3:
                                spread(b + 1, 2)
                                spread(b + 1, 3)
                            if g > 0:
                                weigh(b, r, g - 1)
                        weigh(b, r, G - 1)
                        finish(b)
                        chunk_states(b, r)
                        look_states(b, r)
                tables.pop()
            if last_stage >= 3:
                experts(1)


def kernel(**inputs):
    import concourse.bacc as _bacc
    from concourse.bass_utils import run_bass_kernel_spmd as _run

    arrays = {f"in_{k}": v for k, v in _layout(inputs).items()}
    nc = _bacc.Bacc("TRN2", target_bir_lowering=False, num_devices=1)
    aps = {k[3:]: nc.dram_tensor(k, v.shape, mybir.dt.from_np(v.dtype), kind="ExternalInput").ap() for k, v in arrays.items()}
    out = nc.dram_tensor("out_y", (B * S, D), F32, kind="ExternalOutput").ap()
    build(nc, aps, out)
    r = _run(nc, [arrays], core_ids=[0])
    return r.results[0]["out_y"].reshape(B, S, D)
```

```python
from contextlib import ExitStack

import numpy as np

import concourse.bass as bass
from concourse import mybir

F32 = mybir.dt.float32
F32R = mybir.dt.float32r
BF16 = mybir.dt.bfloat16
I32 = mybir.dt.int32
ALU = mybir.AluOpType
ACT = mybir.ActivationFunctionType
AX = mybir.AxisListType
ds = bass.ds

P = 128
B, S, D = 8, 256, 128
NT = B * S // P
H, HD = 16, 8
KVH, QL, KVL = 4, 64, 32
G = 4
LN_EPS = 1e-5
QK_SCALE = float(HD) ** -0.5
SEG = 32
NC = S // SEG
NS = NC - 1
RMS_EPS = 1e-6
NEG = -1e30
E, FF, TOPK = 8, 512, 2
FC = FF // P
ET = (B * S * TOPK - E) // P + E
ET += -ET % 4
ETS = ET + 1
DEPTH = 4
LOWEST = -3e38
MAGIC = 0x5F3759DF


def _constants():
    inv = (1.0 / np.float32(10000.0) ** (np.arange(0, HD, 2, dtype=np.float32) / np.float32(HD))).astype(np.float32)
    angle = np.outer(np.arange(S, dtype=np.float32), inv)
    row = np.arange(P) % HD
    cos = np.cos(angle)[:, row // 2].T
    sin = (np.sin(angle)[:, row // 2] * np.where(row % 2 == 0, -1.0, 1.0)).T
    rope = np.concatenate([cos, cos, sin, sin], axis=1).astype(np.float32)
    sel = np.zeros((4, P, G, P), np.float32)
    for h in range(H):
        for d in range(HD):
            for s in range(4):
                sel[s % 2, h * HD + d, h // 4, 32 * (h % 4) + 8 * s + d] = 1.0
                sel[2 + s // 2, h * HD + d, h // 4, 32 * (h % 4) + 8 * s + d] = 1.0
    p = np.arange(P)
    above = np.where(p[None, :] > p[:, None], np.float32(NEG), np.float32(0.0))
    pick = np.zeros((P, 4, P), np.float32)
    for part in range(2):
        for j in range(4):
            pick[4 * part + j, j, :] = 1.0
    ident = np.eye(P, dtype=np.float32)
    weight_row = (p[:, None] == 32 * np.arange(4)[None, :] + HD).astype(np.float32)
    before = (p[:, None] < p[None, :]).astype(np.float32)
    pair = 2 * (P * np.arange(NT)[None, :, None] + p[:, None, None]) + np.arange(TOPK)[None, None, :] + 1
    of_expert = np.zeros((P, E, P), np.float32)
    for part in range(3):
        for e in range(E):
            of_expert[32 * part + e, e, :] = 1.0
    same = (p[:, None] // SEG == p[None, :] // SEG) & (p[:, None] <= p[None, :])
    running = np.where(same, np.float32(1) / (p[None, :] % SEG + 1).astype(np.float32), np.float32(0))
    chunk = np.where(p[:, None] // SEG == np.arange(P // SEG)[None, :], np.float32(1 / SEG), np.float32(0))
    at = (p[:, None] // SEG + (P // SEG) * np.arange(2)[None, :])[:, :, None]
    unseen = np.where(at > np.arange(NC)[None, None, :], np.float32(0), np.float32(NEG)).reshape(P, 2 * NC)
    own_head = (p[:, None] // HD == p[None, :] // HD).astype(np.float32)
    every = lambda a: np.broadcast_to(np.asarray(a, np.float32), (P, len(a)))
    route = np.concatenate([before, np.ones((P, P)), every(np.arange(P)), every(np.arange(ETS)),
                            pair.reshape(P, NT * TOPK), every(E - np.arange(E)), TOPK * B * S + 1 + p[:, None] + P * (np.arange(ETS)[None, :] % DEPTH),
                            of_expert.reshape(P, E * P)], axis=1).astype(np.float32)
    return {"c_look": np.concatenate([running, chunk, unseen, own_head], axis=1).astype(np.float32),
            "c_rope": rope, "c_sel": sel.transpose(1, 0, 2, 3).reshape(P, 4 * G * P).copy(),
            "c_route": route,
            "c_misc": np.concatenate([ident, above, pick.reshape(P, 4 * P), weight_row], axis=1)}


def _by_head(w, row=None):
    out = np.zeros((G, 4, 32, D), np.float32)
    out[:, :, 0:HD] = w.reshape(G, 4, HD, D)
    if row is not None:
        out[0, 0, HD] = row
    return out.reshape(G, P, D).transpose(1, 0, 2)


def _layout(a):
    f = {k: np.asarray(v) for k, v in a.items()}
    swap = np.arange(P) ^ 1
    kv = f["L0_attn_Wkvb"].reshape(KVL, KVH, HD, 2)
    k_rep = np.repeat(kv[..., 0][:, :, None, :], H // KVH, axis=2).reshape(KVL, P)
    v_own = kv[..., 1].reshape(KVL, KVH * HD)
    out = {
        "x": f["L0_attn_x"].reshape(NT, P, D),
        "wqa_t": f["L0_attn_Wqa"].T,
        "wqb": np.concatenate([f["L0_attn_Wqb"], f["L0_attn_Wqb"][:, swap]], axis=1),
        "wkva_t": f["L0_attn_Wkva"].T,
        "wkvb": np.concatenate([k_rep, k_rep[:, swap], v_own], axis=1),
        "wout": _by_head(f["L0_attn_Wout"], f["L0_attn_bout"]),
    }
    for n, names in enumerate((("W1", "b1", "W2", "b2"), ("w1", "b1", "w2", "b2"))):
        w1, b1, w2, b2 = (f[f"L{n}_ffn_{m}"] for m in names)
        out |= {f"w1_{n}": w1.transpose(1, 0, 2), f"w2_{n}": w2.reshape(E, FC, P, D).transpose(2, 0, 1, 3),
                f"b_{n}": np.concatenate([b1, b2], axis=1)}
    out["w_look"] = np.concatenate([f["L1_attn_Wq"].T, f["L1_attn_Wk"].T, f["L1_attn_Wv"].T,
                                    f["L1_attn_Wu"].T, f["L1_attn_Wu"]], axis=1)
    out["wo"] = _by_head(f["L1_attn_Wo"].T)
    out["norm_w"] = f["L1_attn_norm_w"].reshape(D, 1)
    out["gates_0"] = np.concatenate([f["L0_ffn_shared_W"], f["L0_ffn_gate_W"]], axis=1)
    out["gates_1"] = f["L1_ffn_gate_w"]
    out["rows"] = np.concatenate([f["L0_ffn_shared_b"], f["L0_ffn_gamma"], f["L0_ffn_beta"], f["L1_ffn_gate_b"]]).reshape(1, -1)
    out |= _constants()
    return {k: np.ascontiguousarray(v) for k, v in out.items()}


def first_turn(i):
    return isinstance(i, int) and i == 0


class Chain:

    def __init__(self, eng, sem, n=0):
        self.eng, self.sem, self.n = eng, sem, n

    def add(self, ins):
        ins.then_inc(self.sem, 1)
        self.n += 1

    def wait(self):
        self.eng.wait_ge(self.sem, self.n)

    def __call__(self, ins):
        self.add(ins)
        self.wait()


def build(nc, inp, out, last_stage=3):
    ctx = ExitStack()
    with ctx:
        def sb(name, shape, dt=F32):
            return ctx.enter_context(nc.sbuf_tensor(name, shape, dt))

        def sem(name):
            return ctx.enter_context(nc.semaphore(name))

        ps = ctx.enter_context(nc.psum_tensor("ps", [P, 8, 512], F32))
        BT, BA, BB, BO = 4, 5, 6, 7

        X = sb("X", [P, NT + 2, D])
        stats = sb("stats", [P, NT + 2, 6])
        mv = sb("mv", [P, NT + 2, 2])
        rstd = sb("rstd", [P, NT + 2])
        nt1 = sb("nt1", [P, NT + 2])
        nt2 = sb("nt2", [P, NT + 2])
        rope = sb("rope", [P, 2, 2 * S])
        misc = sb("misc", [P, 6 * P + 4])
        selr = sb("selr", [P, 4, G, P], F32R)
        ident = misc[:, 0:P]
        weight_row = misc[:, 6 * P:]
        identb = sb("identb", [P, P], BF16)
        aboveb = sb("aboveb", [P, P], BF16)
        pickr = sb("pickr", [P, 4, P], F32R)
        wqa_t = sb("wqa_t", [QL, D])
        wqb = sb("wqb", [QL, 2 * D])
        wkva_t = sb("wkva_t", [KVL, D])
        wkvb = sb("wkvb", [KVL, 2 * D + KVH * HD])
        wq = sb("wq", [D, 2, D])
        wkv = sb("wkv", [D, 2 * D + KVH * HD])
        wout = sb("wout", [P, G, D])

        xn = [sb(f"xn{r}", [P, 2, D]) for r in range(2)]
        xnT = [sb(f"xnT{r}", [D, S]) for r in range(2)]
        rot = [sb(f"rot{r}", [P, 2 * S]) for r in range(3)]
        hi = sb("hi", [P, 2 * S], F32R)
        lo = sb("lo", [P, 2 * S], F32R)
        qst = [sb(f"qst{r}", [P, G, S], F32R) for r in range(2)]
        keys_a = [sb(f"keys_a{n}", [P, 4, S], F32R) for n in range(2)]
        with ExitStack() as shared:
            keys_b = [shared.enter_context(nc.sbuf_tensor(f"keys_b{n}", [P, 4, S], F32R)) for n in range(6)]
        SH = sb("SH", [P, NT, D])
        YB = sb("YB", [P, NT, TOPK * D])
        keys = [k[:] for k in keys_a + keys_b]
        keys = [keys[0:G], keys[G:]]
        vst = [sb(f"vst{r}", [P, 2, H, 32]) for r in range(2)]
        negm = [sb(f"negm{r}", [P, 2, 4]) for r in range(2)]
        mparts = [sb(f"mparts{r}", [P, 2, 2, 4], F32R) for r in range(2)]
        mT = [sb(f"mT{r}", [P, S], F32R) for r in range(2)]
        probs = [sb(f"probs{r}", [P, 4 * 3 * P]) for r in range(2)]
        on = sb("on", [P, G, S])
        o = [sb(f"o{r}", [P, FF]) for r in range(2)]
        denq = sb("denq", [P, 2, 4])
        rdenq = sb("rdenq", [P, 2, 4])
        rden = [sb(f"rden{r}", [P, 2, 4, 32]) for r in range(2)]

        look = sb("look", [P, 2 * P + P // SEG + 2 * NC])
        running, chunk_mean = look[:, 0:P], look[:, P:P + P // SEG]
        unseen = look[:, P + P // SEG:P + P // SEG + 2 * NC]
        own_head = look[:, P + P // SEG + 2 * NC:]
        w_look = sb("w_look", [D, 5, D])
        wo = sb("wo", [P, G, D])
        norm_w = sb("norm_w", [D, 1])
        wqkv = sb("wqkv", [D, 3, D])
        rms = sb("rms", [P, 3, NT + 2])
        usb = [rot[r][:, 0:2 * D] for r in range(2)]
        um = [rot[r][:, 2 * D:4 * D] for r in range(2)]
        means = [sb(f"means{r}", [D, NC]) for r in range(2)]
        wmeans = [sb(f"wmeans{r}", [D, NC]) for r in range(2)]
        SC = sb("SC", [P, NT, NC + 1])
        SCd = sb("SCd", [P, NT, NC + 1])
        GT = sb("GT", [P, NT + 2, NC + 1])
        sct = sb("sct", [P, 3, NT])
        pqk = [sb(f"pqk{r}", [P, 2 * S]) for r in range(2)]
        pkt = [sb(f"pkt{r}", [P, 2, D]) for r in range(2)]
        states = sb("states", [P, NS, D])
        found = [rot[2][:, 2 * D * n:2 * D * (n + 1)].rearrange("p (t d) -> p t d", d=D) for n in range(2)]
        zt = sb("zt", [P, 2, D])

        NROUTE = 3 * P + 2 * ETS + NT * TOPK + E
        route = sb("route", [P, NROUTE])
        before_m, ones_m, iota_p = route[:, 0:P], route[:, P:2 * P], route[:, 2 * P:3 * P]
        iota_t = route[:, 3 * P:3 * P + ETS]
        pair_no = route[:, 3 * P + ETS:3 * P + ETS + NT * TOPK]
        rev_e = route[:, NROUTE - ETS - E:NROUTE - ETS]
        spare_no = route[:, NROUTE - ETS:NROUTE]
        of_expert = sb("of_expert", [P, E * P], BF16)
        rows = sb("rows", [P, 3 * D + E])
        shared_b, gamma, beta, gate_b = rows[:, 0:D], rows[:, D:2 * D], rows[:, 2 * D:3 * D], rows[:, 3 * D:]
        w1 = sb("w1", [D, E * FF])
        w2 = sb("w2", [P, E * FC * D])
        gates = [sb("gates_0", [D, D + E]), sb("gates_1", [D, E])]
        bias = [sb(f"bias_{n}", [E, FF + D]) for n in range(2)]
        bias_rest = sb("bias_rest", [E, FF + D])
        bias_mid = sb("bias_mid", [E, FF + D], BF16)
        bias3 = [sb(f"bias3_{n}", [P, FF + D], BF16) for n in range(2)]
        LG = sb("LG", [P, NT, E])
        LG2 = sb("LG2", [P, NT, E])
        rt = [sb(f"rt{n}", [P, NT, E]) for n in range(3)]
        top = sb("top", [P, 4, NT])
        first = [sb(f"first{n}", [P, NT, E]) for n in range(2)]
        picked = sb("picked", [P, NT, E])
        wts = sb("wts", [P, 5, NT])
        totals = sb("totals", [P, E, NT])
        upto = sb("upto", [P, E, NT])
        per_e = sb("per_e", [P, 8, E])
        per_ei = sb("per_ei", [P, E], I32)
        slot = sb("slot", [P, NT, TOPK])
        sloti = sb("sloti", [P, 3, NT * TOPK], I32)
        slotf = sb("slotf", [P, 2, NT * TOPK])
        hot = [sb(f"hot{n}", [P, P]) for n in range(2)]
        hotn = [sb(f"hotn{n}", [P, ETS]) for n in range(2)]
        etab = sb("etab", [P, ETS, E])
        eidf = sb("eidf", [P, 2, ETS])
        eid = sb("eid", [P, ETS], I32)
        inv = sb("inv", [P, 3, ETS])
        tab = sb("tab", [P, 2, ETS], I32)
        gidx = [sb(f"gidx{r}", [P, 1], I32) for r in range(DEPTH)]
        sidx = [sb(f"sidx{r}", [P, 1], I32) for r in range(DEPTH)]
        xg = [sb(f"xg{r}", [P, D]) for r in range(DEPTH)]
        xgT = [sb(f"xgT{r}", [D, P]) for r in range(2)]
        hid = [o[r][:] for r in range(2)]
        hidT = [probs[r][:, 0:FF] for r in range(2)]
        yt = [sb(f"yt{r}", [P, D]) for r in range(DEPTH)]
        xbuf = [nc.dram_tensor(f"xbuf_{n}", (B * S + DEPTH * P // 2, D), F32, kind="Internal").ap() for n in range(2)]
        ybuf = [nc.dram_tensor(f"ybuf_{n}", (TOPK * B * S + DEPTH * P, D), F32, kind="Internal").ap() for n in range(2)]

        loaded = sem("loaded")
        w_loaded = [sem(f"w_loaded_{n}") for n in range(2)]
        moe_cast = sem("moe_cast")
        MN = ("stats", "rstd", "normed", "xT", "xT_copied", "gated", "logits", "routed", "exp_diff",
              "counted", "hot_a", "hot_b", "hot_used", "inverse", "tabled", "gidx", "sidx", "x_turned", "x_copied",
              "h_ready", "h_active", "h_turned", "h_copied", "y_ready", "y_copied", "gelu", "mixed", "combined")
        ms = [{n: sem(f"m{l}_{n}") for n in MN} for l in range(2)]
        ms_rows = [[sem(f"m{l}_rows_out{r}") for r in range(2)] for l in range(2)]
        gathered = [sem(f"gathered{r}") for r in range(DEPTH)]
        scattered = [sem(f"scattered{r}") for r in range(DEPTH)]

        def gathers(l, k):
            return 16 * k + 16 * l * (ET // DEPTH)

        def scatters(l, k):
            return 16 * k + 16 + 16 * l * (ET // DEPTH + 1)

        ms_back = [[sem(f"m{l}_back{q}") for q in range(4)] for l in range(2)]
        consts_cast = sem("consts_cast")
        w_mm = sem("w_mm")
        w_copied = sem("w_copied")
        init_done = sem("init_done")
        started = sem("started")
        recleared = sem("recleared")
        stats_done = sem("stats_done")
        rstd_step = sem("rstd_step")
        bias_added = sem("bias_added")
        stored = sem("stored")

        A0 = dict(normed=2, xT=1, xT_copied=1, proj=1, rope_step=5, v_copied=1, sel=4, stacked=2, keyed=8,
                  p1=12, maxed=12, msplit=8, mTr=4, mT_copied=4, p2=12, probs_done=12, masked=4, pv=4,
                  o_copied=4, den=4, rden=8, wide=4, divided=4, outp=1, residual=3)
        s0 = {n: (sem("a_" + n), c, 0) for n, c in A0.items()}
        A1 = dict(normed=2, xT=1, xT_copied=1, proj=1, elu_step=4, elu_exp=1, v_copied=1, sel=4, stacked=2, keyed=8,
                  pkT=1, pk_copied=1, p2=12, probs_done=12, masked=4, pv=4, o_copied=4, den=4, rden=12, wide=4, divided=4, outp=1,
                  state=2, state_own=2, looked=3, found=10, residual=8)
        s1 = {n: (s0[n][0], c, B * A0[n]) if n in A0 else (sem("a1_" + n), c, 0) for n, c in A1.items()}
        LN = ("stats", "rstd", "normed", "zT", "zT_copied", "means", "means_copied", "wmeans", "wmeans_copied", "scores",
              "u_copied", "gate_in", "um", "soft", "soft_exp", "w_scaled")
        ls = {n: sem("look_" + n) for n in LN}
        look_loaded = sem("look_loaded")
        tables = [s0]

        def wait(eng, name, b, k):
            sm, c, before = tables[-1][name]
            value = b * c + k
            if isinstance(value, int) and value <= 0:
                return
            eng.wait_ge(sm, value + before + 1)

        def signal(ins, name):
            ins.then_inc(tables[-1][name][0], 1)

        def run_steps(eng, step):
            for r in range(DEPTH):
                step(0, r, r >= 2, r >= 3)
            with eng.Fori(1, ET // DEPTH) as i:
                for r in range(DEPTH):
                    step(i, r)
            for r in range(3):
                step(ET // DEPTH, r, r < 2, True)

        block = ctx.enter_context(nc.Block())

        LOOKS = ((0, 3, 0), (1, 4, 0), (1, 3, 4))
        RING0 = [(k, g, n) for g in range(G) for n in range(3) for k in ("prob", "max")]
        RING1 = [("prob", g, n) for g in (0, 1, 2) for n in range(3)] + [("look", 0, n) for n in range(3)] \
            + [("prob", 3, n) for n in range(3)] + [("none", 0, 0)]
        rings = {0: RING0, 1: RING1}

        def ring_at(kind, g, n):
            if tables[-1] is s0 and kind == "prob":
                g = (g + 1) % G
            return rings[len(tables) - 1].index((kind, g, n))

        def bank_of(kind, g, n):
            return ps[:, ring_at(kind, g, n) % 4, :]

        def look_bank(n):
            return bank_of("look", 0, n)

        NLOAD = 13
        NINIT = 7 + 2 * G
        RDEN = (2, 3)
        RESIDUAL_READ = (1, 3)

        def back(b, r, g):
            return (b - 1, 1 - r, g + G) if g < 0 else (b, r, g)

        def all_steps(eng, step, tail):
            for g in range(G):
                step(0, 0, g, first=True)
            with eng.Fori(0, (B - 2) // 2) as i:
                for n in range(2):
                    for g in range(G):
                        step(2 * i + 1 + n, 1 - n, g)
            for g in range(G):
                step(B - 1, (B - 1) % 2, g, prep=False)
            for g in range(tail):
                step(B, B % 2, g, prep=False, tail=True)

        @block.sync
        def _(sp):
            for t in range(4):
                sp.dma_start(X[:, 4 * t:4 * t + 4, :], inp["x"][4 * t:4 * t + 4].rearrange("t p d -> p t d")).then_inc(loaded, 16)
            sp.dma_start(wqa_t[:], inp["wqa_t"][:, :]).then_inc(loaded, 16)
            sp.dma_start(wqb[:], inp["wqb"][:, :]).then_inc(loaded, 16)
            sp.dma_start(wkva_t[:], inp["wkva_t"][:, :]).then_inc(loaded, 16)
            sp.dma_start(wkvb[:], inp["wkvb"][:, :]).then_inc(loaded, 16)
            sp.dma_start(wout[:], inp["wout"][:, :, :]).then_inc(loaded, 16)
            sp.dma_start(rope[:].rearrange("p a s -> p (a s)"), inp["c_rope"][:, :]).then_inc(loaded, 16)
            sp.dma_start(misc[:], inp["c_misc"][:, :]).then_inc(loaded, 16)
            sp.dma_start(probs[0][:, 0:1024], inp["c_sel"][:, 0:1024]).then_inc(loaded, 16)
            sp.dma_start(probs[1][:, 0:1024], inp["c_sel"][:, 1024:2048]).then_inc(loaded, 16)
            for sm in [a for a, _, _ in s0.values()] + (list(ms[0].values()) if last_stage >= 1 else []) \
                    + ([a for n, (a, _, _) in s1.items() if n not in s0] + list(ls.values()) if last_stage >= 2 else []) \
                    + (list(ms[1].values()) if last_stage >= 3 else []):
                sp.sem_inc(sm, 1)
            sp.sem_inc(started, 4)
            sp.dma_start(route[:], inp["c_route"][:, 0:NROUTE]).then_inc(w_loaded[0], 16)
            for n in range(2):
                sp.dma_start(pqk[n][:], inp["c_route"][:, NROUTE + n * FF:NROUTE + (n + 1) * FF]).then_inc(w_loaded[0], 16)
            sp.dma_start(rows[:], inp["rows"][0:1, :].broadcast_to((P, 3 * D + E))).then_inc(w_loaded[0], 16)
            def load_experts(n):
                sp.dma_start(gates[n][:], inp[f"gates_{n}"][:, :]).then_inc(w_loaded[n], 16)
                sp.dma_start(bias[n][:], inp[f"b_{n}"][:, :]).then_inc(w_loaded[n], 16)
                sp.dma_start(w1[:].rearrange("p (e f) -> p e f", e=E), inp[f"w1_{n}"][:, :, :]).then_inc(w_loaded[n], 16)
                sp.dma_start(w2[:].rearrange("p (e c d) -> p e c d", e=E, c=FC), inp[f"w2_{n}"][:, :, :, :]).then_inc(w_loaded[n], 16)

            load_experts(0)
            sp.dma_start(look[:], inp["c_look"][:, :]).then_inc(look_loaded, 16)
            sp.dma_start(w_look[:].rearrange("p a d -> p (a d)"), inp["w_look"][:, :]).then_inc(look_loaded, 16)
            sp.dma_start(norm_w[:], inp["norm_w"][:, :]).then_inc(look_loaded, 16)
            sp.dma_start(wo[:], inp["wo"][:, :, :]).then_inc(look_loaded, 16)

            def experts(l):
                m = ms[l]
                xr = xbuf[l][0:B * S, :].rearrange("(t p) d -> t p d", p=P)
                sp.wait_ge(init_done, NINIT)
                for r in range(2):
                    sp.dma_start(xbuf[l][B * S + r * P:B * S + (r + 1) * P, :], X[:, NT + r, :]).then_inc(ms_rows[l][r], 16)
                with sp.Fori(0, NT // 4) as i:
                    for r in range(2):
                        sp.wait_ge(m["normed"], 4 * i + 2 * r + 2 + 1)
                        sp.dma_start(xr[ds(4 * i + 2 * r, 2), :, :].rearrange("t p d -> p t d"), xn[r][:]).then_inc(ms_rows[l][r], 16)
                for r in range(DEPTH):
                    sp.wait_ge(scattered[r], scatters(l, ET // DEPTH))
                yr = ybuf[l][0:TOPK * B * S, :].rearrange("(t p k) d -> p t (k d)", p=P, k=TOPK)
                for q in range(4):
                    sp.dma_start(YB[:, 4 * q:4 * q + 4, :], yr[:, 4 * q:4 * q + 4, :]).then_inc(ms_back[l][q], 16)

            if last_stage == 0:
                sp.wait_ge(s0["residual"][0], 3 * B + 1)
            if last_stage >= 1:
                experts(0)
                if last_stage >= 3:
                    load_experts(1)
                sp.wait_ge(ms[0]["combined"], 1 + 1)
            if last_stage >= 2:
                sp.wait_ge(s1["residual"][0], (3 + 8) * B + 1)
            if last_stage >= 3:
                experts(1)
                sp.wait_ge(ms[1]["combined"], 1 + 1)
            sp.dma_start(out.rearrange("(t p) d -> p t d", p=P), X[:, 0:NT, :]).then_inc(stored, 16)
            sp.wait_ge(stored, 16)

        @block.gpsimd
        def _(pool):
            def own_wait():
                pool.nop(nofuse=True)

            def clear_keys(sm):
                for r in range(2):
                    for g in range(G):
                        pool.memset(keys[r][g].bitcast(F32), 0.0).then_inc(sm, 1)

            for r in range(2):
                pool.memset(vst[r][:], 0.0).then_inc(init_done, 1)
                pool.memset(mT[r][:].bitcast(F32), 0.0).then_inc(init_done, 1)
            pool.memset(X[:, NT:NT + 2, :], 0.0).then_inc(init_done, 1)
            pool.wait_ge(init_done, 5)
            own_wait()
            for r in range(2):
                pool.memset(vst[r][:, :, :, HD:HD + 1], 1.0).then_inc(init_done, 1)
            clear_keys(init_done)
            pool.wait_ge(started, 4)
            own_wait()

            def mask_probs(b, g):
                wait(pool, "probs_done", b, 3 * g + 3)
                own_wait()
                for diag in (probs[g % 2][:, 0:4 * S].rearrange("p (j s) -> p j s", s=S)[:, :, 0:P],
                             probs[g % 2][:, 4 * S:].rearrange("p (j s) -> p j s", s=P)):
                    last = pool.affine_select(out=diag, in_=diag, compare_op=ALU.is_ge, fill=0.0, base=0,
                                              pattern=[[0, 4], [1, P]], channel_multiplier=-1)
                signal(last, "masked")

            with pool.Fori(0, B) as b:
                for g in range(G):
                    mask_probs(b, g)

            def expert_constants(l):
                pool.wait_ge(w_loaded[l], 16 * (8 if l == 0 else 4))
                own_wait()
                c = Chain(pool, moe_cast, 8 * l)
                if l == 0:
                    for n in range(2):
                        c.add(pool.tensor_copy(of_expert[:, n * FF:(n + 1) * FF], pqk[n][:]))
                c.add(pool.memset(bias3[l][:], 0.0))
                c.wait()
                own_wait()
                for ins in (lambda: pool.tensor_copy(bias3[l][0:E, :], bias[l][:]),
                            lambda: pool.tensor_tensor(bias_rest[:], bias[l][:], bias3[l][0:E, :], ALU.subtract),
                            lambda: pool.tensor_copy(bias_mid[:], bias_rest[:]),
                            lambda: pool.tensor_copy(bias3[l][32:32 + E, :], bias_mid[:]),
                            lambda: pool.tensor_tensor(bias3[l][64:64 + E, :], bias_rest[:], bias_mid[:], ALU.subtract)):
                    c(ins())
                    own_wait()

            def experts(l):
                m = ms[l]
                expert_constants(l)
                for r in range(DEPTH):
                    pool.dma_start(ybuf[l][TOPK * B * S + r * P:TOPK * B * S + (r + 1) * P, :], X[:, NT, :]).then_inc(scattered[r], 16)
                pool.wait_ge(m["tabled"], 6 + 1)
                own_wait()
                for r in range(2):
                    pool.wait_ge(ms_rows[l][r], 16 * (NT // 4) + 16)
                own_wait()

                def gather_index(n, i, r):
                    if i is not None:
                        pool.wait_ge(gathered[r], gathers(l, i))
                        own_wait()
                    pool.tensor_copy(gidx[r][:], tab[:, 1, ds(n, 1)]).then_inc(m["gidx"], 1)

                def gather(n, r):
                    pool.wait_ge(m["gidx"], n + 2)
                    own_wait()
                    pool.indirect_dma_start(out=xg[r][:], out_offset=None, in_=xbuf[l][:, :],
                                            in_offset=bass.IndirectOffsetOnAxis(ap=gidx[r][:], axis=0)).then_inc(gathered[r], 16)

                def scatter_index(n, i, r):
                    pool.wait_ge(scattered[r], scatters(l, i))
                    own_wait()
                    pool.tensor_copy(sidx[r][:], tab[:, 0, ds(n, 1)]).then_inc(m["sidx"], 1)

                def scatter(n, r):
                    pool.wait_ge(m["sidx"], n + 2)
                    pool.wait_ge(m["y_copied"], n + 2)
                    own_wait()
                    pool.indirect_dma_start(out=ybuf[l][:, :], out_offset=bass.IndirectOffsetOnAxis(ap=sidx[r][:], axis=0),
                                            in_=yt[r][:], in_offset=None).then_inc(scattered[r], 16)

                def step(i, r, fetch=True):
                    n = DEPTH * i + r
                    if fetch:
                        pool.wait_ge(m["x_turned"], n + 2)
                        own_wait()
                        gather(n + DEPTH, r)
                    if r == DEPTH - 1 or not first_turn(i):
                        scatter(n - 3, (r + 1) % DEPTH)
                    if fetch:
                        gather_index(n + DEPTH + 1, i + (r + 1) // DEPTH + 1, (r + 1) % DEPTH)
                    if not first_turn(i) or r >= 2:
                        scatter_index(n - 2, i - (r < 2), (r + 2) % DEPTH)
                for r in range(DEPTH):
                    gather_index(r, None, r)
                    gather(r, r)
                gather_index(DEPTH, 1, 0)
                for r in range(DEPTH):
                    step(0, r)
                with pool.Fori(1, ET // DEPTH - 1) as i:
                    for r in range(DEPTH):
                        step(i, r)
                for r in range(DEPTH):
                    step(ET // DEPTH - 1, r, fetch=False)
                for r in range(3):
                    scatter(ET - 3 + r, (r + 1) % DEPTH)
                    if r < 2:
                        scatter_index(ET - 2 + r, ET // DEPTH - 1, (r + 2) % DEPTH)

            if last_stage >= 1:
                experts(0)
            if last_stage >= 2:
                pool.wait_ge(ms[0]["combined"], 1 + 1)
                own_wait()
                clear_keys(recleared)
                tables.append(s1)
                with pool.Fori(0, B) as b:
                    for g in range(G):
                        mask_probs(b, g)
                tables.pop()
            if last_stage >= 3:
                experts(1)

        @block.vector
        def _(dve):
            dve.wait_ge(started, 4)
            dve.wait_ge(loaded, 16 * NLOAD)
            for n in range(2):
                dve.tensor_copy(selr[:, 2 * n:2 * n + 2].rearrange("p a g m -> p (a g m)"),
                                probs[n][:, 0:1024]).then_inc(consts_cast, 1)
            dve.tensor_copy(identb[:], misc[:, 0:P]).then_inc(consts_cast, 1)
            dve.tensor_copy(aboveb[:], misc[:, P:2 * P]).then_inc(consts_cast, 1)
            dve.tensor_copy(pickr[:].rearrange("p a m -> p (a m)"), misc[:, 2 * P:6 * P]).then_inc(consts_cast, 1)
            dve.wait_ge(w_mm, 1)
            dve.tensor_copy(wq[:].rearrange("p a m -> p (a m)"), ps[:, BA, 0:2 * D]).then_inc(w_copied, 1)
            dve.tensor_copy(wkv[:], ps[:, BB, 0:2 * D + KVH * HD]).then_inc(w_copied, 1)

            def all_stats(sem_stats, first):
                with dve.Fori(0, NT) as t:
                    dve.bn_stats(stats[:, ds(t, 1), :].rearrange("p a s -> p (a s)"),
                                 X[:, ds(t, 1), :].rearrange("p a d -> p (a d)")).then_inc(sem_stats, 1)
                dve.wait_ge(sem_stats, first + NT)
                for t in range(NT):
                    dve.bn_aggr(mv[:, t, :], stats[:, t, :]).then_inc(sem_stats, 1)
                dve.wait_ge(sem_stats, first + 2 * NT)

            def inv_sqrt(y, v, t1, t2, eps, step, n0):
                n = n0

                def then(ins):
                    nonlocal n
                    n += 1
                    ins.then_inc(step, 1)
                    dve.wait_ge(step, n)
                then(dve.tensor_scalar(t1, v, eps, None, ALU.add))
                then(dve.tensor_scalar(y.bitcast(I32), t1.bitcast(I32), 1, None, ALU.logical_shift_right))
                then(dve.tensor_scalar(y.bitcast(I32), y.bitcast(I32), -1.0, float(MAGIC), ALU.mult, ALU.add))
                for _ in range(4):
                    then(dve.tensor_tensor(t2, y, y, ALU.mult))
                    then(dve.tensor_tensor(t2, t2, t1, ALU.mult))
                    then(dve.tensor_scalar(t2, t2, -0.5, 1.5, ALU.mult, ALU.add))
                    then(dve.tensor_tensor(y, y, t2, ALU.mult))
                return n

            dve.memset(mv[:, NT:NT + 2, :], 0.0).then_inc(stats_done, 1)
            all_stats(stats_done, 1)
            inv_sqrt(rstd[:], mv[:, :, 1], nt1[:], nt2[:], LN_EPS, rstd_step, 0)

            def norm(b, b2, r):
                for t in range(2):
                    signal(dve.tensor_scalar(xn[r][:, t, :], X[:, ds(b2 + t, 1), :].rearrange("p a d -> p (a d)"),
                                             mv[:, ds(b2 + t, 1), 0:1].rearrange("p a s -> p (a s)"),
                                             rstd[:, ds(b2 + t, 1)], ALU.subtract, ALU.mult), "normed")

            def rotate(b):
                k = 0
                wait(dve, "proj", b, 1)
                wait(dve, "sel", b, 0)
                wait(dve, "rope_step", b, 0)
                signal(dve.tensor_tensor(rot[0][:], ps[:, BA, :], rope[:, 0, :], ALU.mult), "rope_step")
                signal(dve.tensor_tensor(rot[1][:], ps[:, BB, :], rope[:, 1, :], ALU.mult), "rope_step")
                wait(dve, "rope_step", b, 2)
                signal(dve.tensor_tensor(rot[2][:], rot[0][:], rot[1][:], ALU.add), "rope_step")
                wait(dve, "rope_step", b, 3)
                signal(dve.tensor_copy(hi[:], rot[2][:]), "rope_step")
                wait(dve, "rope_step", b, 4)
                signal(dve.tensor_tensor(lo[:], rot[2][:], hi[:].bitcast(F32), ALU.subtract), "rope_step")

            def maximum(b, g, n):
                wait(dve, "p1", b, 3 * g + n + 1)
                if n == 0:
                    wait(dve, "msplit", b, 2 * (g - 1))
                    src = bank_of("max", g, n).rearrange("p (j s) -> p j s", s=P)
                    dst = negm[g % 2][:, 0, :]
                else:
                    src = bank_of("max", g, n).rearrange("p (j s) -> p j s", s=S)
                    dst = negm[g % 2][:, 1, 2 * n - 2:2 * n]
                signal(dve.tensor_reduce(dst, src, AX.X, ALU.max, negate=True), "maxed")

            def split_max(b, g):
                wait(dve, "maxed", b, 3 * g + 3)
                wait(dve, "mTr", b, g - 1)
                signal(dve.tensor_copy(mparts[g % 2][:, :, 0, :], negm[g % 2][:]), "msplit")
                wait(dve, "msplit", b, 2 * g + 1)
                signal(dve.tensor_tensor(mparts[g % 2][:, :, 1, :], negm[g % 2][:], mparts[g % 2][:, :, 0, :].bitcast(F32), ALU.subtract), "msplit")

            def reciprocals(b, g):
                wait(dve, "den", b, g + 1)
                wait(dve, "wide", b, g - 1)
                k = RDEN[len(tables) - 1]
                den = ps[:, BO, S:S + 8].rearrange("p (t j) -> p t j", j=4)
                if tables[-1] is s1:
                    wait(dve, "rden", b, k * g)
                    signal(dve.tensor_scalar(denq[:], den, RMS_EPS, None, ALU.add), "rden")
                    wait(dve, "rden", b, k * g + 1)
                    den = denq[:]
                wait(dve, "rden", b, k * g)
                signal(dve.reciprocal(rdenq[:], den), "rden")
                wait(dve, "rden", b, k * (g + 1) - 1)
                signal(dve.tensor_copy(rden[g % 2][:], rdenq[:].unsqueeze(3).broadcast_to((P, 2, 4, 32))), "rden")

            def divide(b, g):
                wait(dve, "wide", b, g + 1)
                if g == 0:
                    wait(dve, "outp", b, 0)
                signal(dve.tensor_tensor(on[:, g, :], o[g % 2][:, 0:S], ps[:, BO, S:2 * S], ALU.mult), "divided")

            def stats_of(b):
                wait(dve, "residual", b, STEPS_OF_RESIDUAL[len(tables) - 1])
                for t in range(2):
                    signal(dve.bn_stats(stats[:, ds(2 * b + t, 1), :].rearrange("p a s -> p (a s)"),
                                        X[:, ds(2 * b + t, 1), :].rearrange("p a d -> p (a d)")), "residual")

            def residual(b):
                wait(dve, "outp", b, 1)
                signal(dve.tensor_tensor(X[:, ds(2 * b, 2), :].rearrange("p a d -> p (a d)"),
                                         X[:, ds(2 * b, 2), :].rearrange("p a d -> p (a d)"), ps[:, BT, 0:2 * D], ALU.add), "residual")
                stats_of(b)

            STEPS_OF_RESIDUAL = (1, 6)
            norm(0, 0, 0)
            rotate(0)

            def step0(b, r, g, first=False, prep=True, tail=False):
                if g == 0 and prep:
                    norm(b + 1, 2 * b + 2, 1 - r)
                for n in range(3):
                    if not tail:
                        maximum(b, g, n)
                    if n == 0 and (g >= 3 if first else g < 3 if tail else True):
                        bb, _, gg = back(b, r, g - 3)
                        divide(bb, gg)
                if not tail:
                    split_max(b, g)
                if g >= 2 if first else g < 2 if tail else True:
                    bb, _, gg = back(b, r, g - 2)
                    reciprocals(bb, gg)
                if g == 1 and prep:
                    rotate(b + 1)
                if g == 2 and not first:
                    residual(b - 1)
            all_steps(dve, step0, 3)
            dve.wait_ge(s0["residual"][0], 3 * B + 1)

            def experts(l, have):
                m = ms[l]
                for t in range(NT):
                    dve.bn_aggr(mv[:, t, :], stats[:, t, :]).then_inc(m["stats"], 1)
                dve.wait_ge(m["stats"], NT + 1)
                inv_sqrt(rstd[:], mv[:, :, 1], nt1[:], nt2[:], LN_EPS, m["rstd"], 1)

                def norm_pair(k, i, r):
                    dve.wait_ge(ms_rows[l][r], 16 * i + 16)
                    dve.wait_ge(m["xT"], 2 * i + 1)
                    for t in range(2):
                        dve.tensor_scalar(xn[r][:, t, :], X[:, ds(2 * k + t, 1), :].rearrange("p a d -> p (a d)"),
                                          mv[:, ds(2 * k + t, 1), 0:1].rearrange("p a s -> p (a s)"),
                                          rstd[:, ds(2 * k + t, 1)], ALU.subtract, ALU.mult).then_inc(m["normed"], 1)

                with dve.Fori(0, NT // 4) as i:
                    for r in range(2):
                        norm_pair(2 * i + r, i, r)
                    for r in range(2):
                        k = 2 * i + r
                        dve.wait_ge(m["gated"], k + 2)
                        w = D + E if l == 0 else E
                        src = ps[:, 6 + r, 0:2 * w].rearrange("p (t w) -> p t w", t=2)
                        if l == 0:
                            dve.tensor_tensor(SH[:, ds(2 * k, 2), :], src[:, :, 0:D], shared_b.unsqueeze(1).broadcast_to((P, 2, D)), ALU.add).then_inc(m["logits"], 1)
                            dve.tensor_copy(LG[:, ds(2 * k, 2), :], src[:, :, D:D + E]).then_inc(m["logits"], 1)
                        else:
                            dve.tensor_tensor(LG[:, ds(2 * k, 2), :], src, gate_b.unsqueeze(1).broadcast_to((P, 2, E)), ALU.add).then_inc(m["logits"], 1)
                dve.wait_ge(m["logits"], (NT if l == 0 else NT // 2) + 1)

                c = Chain(dve, m["routed"], 1)
                wide = lambda a: a.unsqueeze(2).broadcast_to((P, NT, E))
                for n in range(2):
                    L = LG if n == 0 else LG2
                    c(dve.tensor_reduce(top[:, n, :], L[:], AX.X, ALU.max))
                    c(dve.tensor_tensor(rt[0][:], L[:], wide(top[:, n, :]), ALU.is_ge))
                    c(dve.tensor_tensor(rt[1][:], rt[0][:], rev_e.unsqueeze(1).broadcast_to((P, NT, E)), ALU.mult))
                    c(dve.tensor_reduce(top[:, 2, :], rt[1][:], AX.X, ALU.max))
                    c(dve.tensor_tensor(first[n][:], rt[1][:], wide(top[:, 2, :]), ALU.is_equal))
                    if n == 0:
                        c(dve.scalar_tensor_tensor(LG2[:], first[0][:], LOWEST, LG[:], ALU.mult, ALU.add))
                c(dve.tensor_tensor(picked[:], first[0][:], first[1][:], ALU.add))
                c(dve.tensor_tensor(wts[:, 0, :], top[:, 1, :], top[:, 0, :], ALU.subtract))
                ROUTED = c.n
                assert ROUTED == 14
                dve.wait_ge(m["counted"], 1 + 1)
                c(dve.tensor_copy(totals[:], ps[:, BT, P:2 * P].rearrange("p (t e) -> p e t", e=E)))
                flat = lambda a: a[:].rearrange("p e t -> p (e t)")
                c(dve.tensor_tensor_scan(flat(upto), ones_m, flat(totals), 0.0, ALU.mult, ALU.add))
                last = upto[:, :, NT - 1]
                cnt, til, cum, off = (per_e[:, n, :] for n in range(4))
                c(dve.tensor_copy(cnt, last))
                c(dve.tensor_tensor(per_e[:, 4, 1:E], last[:, 1:E], last[:, 0:E - 1], ALU.subtract))
                c(dve.tensor_copy(per_e[:, 4, 0:1], last[:, 0:1]))
                num = per_e[:, 4, :]
                c(dve.tensor_scalar(per_ei[:], num, float(P - 1), None, ALU.add))
                c(dve.tensor_scalar(per_ei[:], per_ei[:], P.bit_length() - 1, None, ALU.arith_shift_right))
                c(dve.tensor_copy(til, per_ei[:]))
                c(dve.tensor_tensor_scan(cum, ones_m[:, 0:E], til, 0.0, ALU.mult, ALU.add))
                c(dve.tensor_tensor(per_e[:, 5, :], cum, til, ALU.subtract))
                c(dve.tensor_tensor(per_e[:, 6, :], num, last, ALU.subtract))
                c(dve.scalar_tensor_tensor(off, per_e[:, 5, :], float(P), per_e[:, 6, :], ALU.mult, ALU.add))
                c(dve.tensor_tensor(flat(upto), flat(upto), flat(totals), ALU.subtract))
                c(dve.tensor_tensor(upto[:], upto[:], off.unsqueeze(2).broadcast_to((P, E, NT)), ALU.add))
                c(dve.tensor_tensor(rt[0][:], ps[:, BT, 0:P].rearrange("p (t e) -> p t e", e=E), upto[:].rearrange("p e t -> p t e"), ALU.add))
                for n in range(TOPK):
                    c(dve.tensor_tensor(rt[1][:], rt[0][:], first[n][:], ALU.mult))
                    c(dve.tensor_reduce(slot[:, :, n], rt[1][:], AX.X, ALU.add))
                c(dve.tensor_copy(sloti[:, 0, :], slot[:].rearrange("p t k -> p (t k)")))
                c(dve.tensor_scalar(sloti[:, 1, :], sloti[:, 0, :], P - 1, None, ALU.bitwise_and))
                c(dve.tensor_scalar(sloti[:, 2, :], sloti[:, 0, :], P.bit_length() - 1, None, ALU.arith_shift_right))
                c(dve.tensor_copy(slotf[:], sloti[:, 1:3, :]))
                c(dve.tensor_tensor(etab[:], iota_t.unsqueeze(2).broadcast_to((P, ETS, E)), cum.unsqueeze(1).broadcast_to((P, ETS, E)), ALU.is_ge))
                c(dve.tensor_reduce(eidf[:, 0, :], etab[:], AX.X, ALU.add))
                c(dve.tensor_scalar(eidf[:, 1, :], eidf[:, 0, :], float(E - 1), None, ALU.min))
                with dve.Fori(0, NT) as t:
                    for k in range(TOPK):
                        q = 2 * t + k
                        dve.wait_ge(m["hot_used"], 2 * t + 1)
                        if k == 0:
                            dve.wait_ge(m["hot_b"], 2 * t + 1)
                        dve.tensor_scalar(hot[k][:], iota_p, slotf[:, 0, ds(q, 1)], None, ALU.is_equal).then_inc(m["hot_a"], 1)
                        dve.tensor_scalar(hotn[k][:], iota_t, slotf[:, 1, ds(q, 1)], pair_no[:, ds(q, 1)], ALU.is_equal, ALU.mult).then_inc(m["hot_b"], 1)
                dve.wait_ge(m["inverse"], 1 + 1)
                c = Chain(dve, m["tabled"], 1)
                c(dve.tensor_copy(eid[:], eidf[:, 1, :]))
                c(dve.tensor_copy(inv[:, 0, :], ps[:, BA, 0:ETS]))
                c(dve.scalar_tensor_tensor(inv[:, 1, :], inv[:, 0, :], 0.0, spare_no, ALU.is_equal, ALU.mult))
                c(dve.scalar_tensor_tensor(inv[:, 2, :], inv[:, 0, :], -1.0, inv[:, 1, :], ALU.add, ALU.add))
                c(dve.tensor_copy(tab[:, 0, :], inv[:, 2, :]))
                c(dve.tensor_scalar(tab[:, 1, :], tab[:, 0, :], 1, None, ALU.arith_shift_right))

                c = Chain(dve, m["mixed"], 1)
                if l == 0:
                    dve.wait_ge(m["exp_diff"], 1 + 1)
                    c(dve.tensor_scalar(wts[:, 2, :], wts[:, 1, :], 1.0, None, ALU.add))
                    c(dve.reciprocal(wts[:, 3, :], wts[:, 2, :]))
                    c(dve.tensor_tensor(wts[:, 4, :], wts[:, 3, :], wts[:, 1, :], ALU.mult))
                n_mixed = c.n

                def step(i, r, turned=True, ready=True):
                    n = DEPTH * i + r
                    if turned:
                        dve.wait_ge(m["h_turned"], n - 2 + 2)
                        dve.tensor_copy(hidT[r % 2], ps[:, 2 + r % 2, :]).then_inc(m["h_copied"], 1)
                    if ready:
                        q = (r + 1) % DEPTH
                        dve.wait_ge(m["y_ready"], n - 3 + 2)
                        dve.wait_ge(scattered[q], scatters(l, i - (r < 3)))
                        dve.tensor_copy(yt[q][:], ps[:, 6 + (r + 1) % 2, 0:D]).then_inc(m["y_copied"], 1)
                run_steps(dve, step)

                if l == 0:
                    dve.wait_ge(m["gelu"], 1 + 1)
                    c(dve.tensor_scalar(SH[:], SH[:], 0.5, None, ALU.mult))
                for t in range(NT):
                    if t % 4 == 0:
                        dve.wait_ge(ms_back[l][t // 4], 16)
                    for k in range(TOPK):
                        if l == 0:
                            dve.wait_ge(m["mixed"], c.n)
                            c.n += 1
                            dve.scalar_tensor_tensor(SH[:, t, :], YB[:, t, k * D:(k + 1) * D], wts[:, 3 + k, t:t + 1], SH[:, t, :], ALU.mult, ALU.add).then_inc(m["mixed"], 1)
                if l == 1:
                    for q in range(4):
                        dve.wait_ge(ms_back[l][q], 16)
                    c(dve.tensor_tensor(X[:, 0:NT, :], X[:, 0:NT, :], YB[:, :, 0:D], ALU.add))
                    dve.tensor_tensor(X[:, 0:NT, :], X[:, 0:NT, :], YB[:, :, D:], ALU.add).then_inc(m["combined"], 1)
                    return
                dve.wait_ge(m["mixed"], c.n)
                for t in range(NT):
                    c.add(dve.bn_stats(stats[:, t, :], SH[:, t, :]))
                c.wait()
                for t in range(NT):
                    c.add(dve.bn_aggr(mv[:, t, :], stats[:, t, :]))
                c.wait()
                c.n = inv_sqrt(rstd[:], mv[:, :, 1], nt1[:], nt2[:], LN_EPS, m["mixed"], c.n)
                for t in range(NT):
                    c.add(dve.tensor_scalar(SH[:, t, :], SH[:, t, :], mv[:, t, 0:1], rstd[:, t:t + 1], ALU.subtract, ALU.mult))
                c.wait()
                row = lambda a: a.unsqueeze(1).broadcast_to((P, NT, D))
                c(dve.tensor_tensor(SH[:], SH[:], row(gamma), ALU.mult))
                c(dve.tensor_tensor(SH[:], SH[:], row(beta), ALU.add))
                dve.tensor_tensor(X[:, 0:NT, :], X[:, 0:NT, :], SH[:], ALU.add).then_inc(m["combined"], 1)

            def look_up():
                all_stats(ls["stats"], 1)
                n = inv_sqrt(rstd[:], mv[:, :, 1], nt1[:], nt2[:], LN_EPS, ls["rstd"], 1)
                c = Chain(dve, ls["rstd"], n)
                c(dve.tensor_tensor(rms[:, 0, :], rstd[:], rstd[:], ALU.mult))
                c(dve.tensor_tensor(rms[:, 1, :], rms[:, 0, :], mv[:, :, 1], ALU.mult))
                c.n = inv_sqrt(rms[:, 2, :], rms[:, 1, :], nt1[:], nt2[:], RMS_EPS, ls["rstd"], c.n)
                c(dve.tensor_tensor(rms[:, 0, :], rms[:, 2, :], rstd[:], ALU.mult))
                dve.wait_ge(look_loaded, 64)
                dve.tensor_scalar(wqkv[:], w_look[:, 0:3, :], norm_w[:], None, ALU.mult).then_inc(ls["w_scaled"], 1)
                with dve.Fori(0, NT // 4) as i:
                    for r in range(2):
                        k = 2 * i + r
                        dve.wait_ge(ls["scores"], 2 * i + 1)
                        for t in range(2):
                            dve.tensor_scalar(xn[r][:, t, :], X[:, ds(2 * k + t, 1), :].rearrange("p a d -> p (a d)"),
                                              mv[:, ds(2 * k + t, 1), 0:1].rearrange("p a s -> p (a s)"),
                                              rstd[:, ds(2 * k + t, 1)], ALU.subtract, ALU.mult).then_inc(ls["normed"], 1)
                    for r in range(2):
                        k = 2 * i + r
                        dve.wait_ge(ls["u_copied"], k + 2)
                        dve.wait_ge(ls["means"], k + 2)
                        dve.wait_ge(ls["um"], 2 * (2 * i) + 1)
                        dve.tensor_tensor(um[r], usb[r], ps[:, 6 + r, 0:2 * D], ALU.mult).then_inc(ls["um"], 1)
                        dve.wait_ge(ls["um"], 2 * k + 2)
                        dve.tensor_reduce(SC[:, ds(2 * k, 2), NC:NC + 1].rearrange("p a o -> p (a o)"), um[r].rearrange("p (t d) -> p t d", t=2), AX.X, ALU.add).then_inc(ls["um"], 1)
                        dve.wait_ge(ls["scores"], k + 2)
                        dve.tensor_tensor(SC[:, ds(2 * k, 2), 0:NC], ps[:, 2 + r, 2 * NC:4 * NC].rearrange("p (t n) -> p t n", t=2),
                                          unseen.rearrange("p (t n) -> p t n", t=2), ALU.add).then_inc(ls["gate_in"], 1)
                dve.wait_ge(ls["gate_in"], NT // 2 + 1)
                c = Chain(dve, ls["soft"], 1)
                wide = lambda a: a.unsqueeze(2).broadcast_to((P, NT, NC + 1))
                c(dve.tensor_reduce(sct[:, 0, :], SC[:], AX.X, ALU.max))
                c(dve.tensor_tensor(SCd[:], SC[:], wide(sct[:, 0, :]), ALU.subtract))
                dve.wait_ge(ls["soft_exp"], 1 + 1)
                c(dve.tensor_reduce(sct[:, 1, :], SC[:], AX.X, ALU.add))
                c(dve.reciprocal(sct[:, 2, :], sct[:, 1, :]))
                c(dve.tensor_tensor(GT[:, 0:NT, :], SC[:], wide(sct[:, 2, :]), ALU.mult))

            def norm1(b, b2, r):
                for t in range(2):
                    signal(dve.tensor_scalar(xn[r][:, t, :], X[:, ds(b2 + t, 1), :].rearrange("p a d -> p (a d)"),
                                             mv[:, ds(b2 + t, 1), 0:1].rearrange("p a s -> p (a s)"),
                                             rms[:, 0, ds(b2 + t, 1)], ALU.subtract, ALU.mult), "normed")

            def elu(b, r):
                wait(dve, "proj", b, 1)
                wait(dve, "sel", b, 0)
                wait(dve, "elu_step", b, 0)
                signal(dve.tensor_scalar(rot[0][:], ps[:, BA, :], 0.0, None, ALU.min), "elu_step")
                wait(dve, "elu_exp", b, 1)
                signal(dve.scalar_tensor_tensor(pqk[r][:], ps[:, BA, :], 0.0, rot[1][:], ALU.max, ALU.add), "elu_step")
                wait(dve, "elu_step", b, 2)
                signal(dve.tensor_copy(hi[:], pqk[r][:]), "elu_step")
                wait(dve, "elu_step", b, 3)
                signal(dve.tensor_tensor(lo[:], pqk[r][:], hi[:].bitcast(F32), ALU.subtract), "elu_step")

            def own_states(b):
                for n, c in ((0, 4), (1, NS - 4)):
                    wait(dve, "state", b, n + 1)
                    wait(dve, "looked", b, 0)
                    signal(dve.tensor_tensor(states[:, 4 * n:4 * n + c, :], ps[:, BA + n, 0:c * D].rearrange("p (n d) -> p n d", d=D),
                                             own_head.unsqueeze(1).broadcast_to((P, c, D)), ALU.mult), "state_own")

            def retrieve(b, r):
                wait(dve, "residual", b - 1, 0)
                k = 0
                for n, (t, c, at) in enumerate(LOOKS):
                    wait(dve, "looked", b, n + 1)
                    for a in range(c):
                        gate = GT[:, ds(2 * b + t, 1), at + a:at + a + 1].rearrange("p a n -> p (a n)")
                        src = look_bank(n)[:, a * D:(a + 1) * D]
                        if at + a == 0:
                            signal(dve.tensor_scalar(found[r][:, t, :], src, gate, None, ALU.mult), "found")
                        else:
                            wait(dve, "found", b, k)
                            signal(dve.scalar_tensor_tensor(found[r][:, t, :], src, gate, found[r][:, t, :], ALU.mult, ALU.add), "found")
                        k += 1

            def residual1(b, r):
                b2 = 2 * b
                wait(dve, "residual", b, 0)
                for t in range(2):
                    signal(dve.tensor_scalar(zt[:, t, :], X[:, ds(b2 + t, 1), :].rearrange("p a d -> p (a d)"),
                                             mv[:, ds(b2 + t, 1), 0:1].rearrange("p a s -> p (a s)"),
                                             rstd[:, ds(b2 + t, 1)], ALU.subtract, ALU.mult), "residual")
                wait(dve, "outp", b, 1)
                wait(dve, "residual", b, 2)
                flat = lambda a: a[:].rearrange("p t d -> p (t d)")
                signal(dve.tensor_tensor(flat(zt), flat(zt), ps[:, BT, 0:2 * D], ALU.add), "residual")
                wait(dve, "residual", b, 3)
                wait(dve, "found", b, 10)
                for t in range(2):
                    gate = GT[:, ds(b2 + t, 1), NC:NC + 1].rearrange("p a n -> p (a n)")
                    signal(dve.scalar_tensor_tensor(zt[:, t, :], zt[:, t, :], gate, found[r][:, t, :], ALU.mult, ALU.add), "residual")
                wait(dve, "residual", b, 5)
                signal(dve.tensor_tensor(X[:, ds(b2, 2), :], X[:, ds(b2, 2), :], zt[:], ALU.add), "residual")
                stats_of(b)

            if last_stage >= 1:
                experts(0, 0)
            if last_stage >= 2:
                dve.wait_ge(ms[0]["combined"], 1 + 1)
                look_up()
                tables.append(s1)
                norm1(0, 0, 0)
                elu(0, 0)

                def step1(b, r, g, first=False, prep=True, tail=False):
                    if g == 0 and prep:
                        norm1(b + 1, 2 * b + 2, 1 - r)
                    if g >= 2 if first else True:
                        bb, _, gg = back(b, r, g - 2)
                        divide(bb, gg)
                    if g == 1 and not first:
                        residual1(b - 1, 1 - r)
                    if not (first and g == 0) and not (tail and g > 0):
                        bb, _, gg = back(b, r, g - 1)
                        reciprocals(bb, gg)
                    if g == 0 and not tail:
                        own_states(b)
                    if g == 1 and prep:
                        elu(b + 1, 1 - r)
                    if g == 2 and not tail:
                        retrieve(b, r)
                all_steps(dve, step1, 2)
                tables.pop()
                dve.wait_ge(s1["residual"][0], (3 + 8) * B + 1)
            if last_stage >= 3:
                experts(1, 0)

        @block.scalar
        def _(act):
            def copy_xT(b, r):
                wait(act, "xT", b, 1)
                signal(act.activation(xnT[r][:], ps[:, BT, 0:S], ACT.Copy), "xT_copied")

            def copy_v(b, r):
                wait(act, "proj", b, 1)
                signal(act.activation(vst[r][:, :, 0:KVH, 0:HD], ps[:, BT, 0:2 * KVH * HD].rearrange("p (t h d) -> p t h d", t=2, d=HD), ACT.Copy), "v_copied")

            def stack(b, r, n):
                wait(act, "sel", b, 2 * n + 1)
                act_dst = qst[r][:, 2 * n:2 * n + 2, :].rearrange("p g s -> p (g s)")
                signal(act.activation(act_dst, ps[:, BA, :], ACT.Copy), "stacked")

            def key_copies(b, r, n):
                wait(act, "sel", b, 2 * n + 2)
                for g in (2 * n, 2 * n + 1):
                    for j in range(4):
                        ins = act.activation(keys[r][g][32 * j:32 * j + 32, j, :], ps[32 * j:32 * j + 32, BB, (g % 2) * S:(g % 2 + 1) * S], ACT.Copy)
                        if j % 2 == 1:
                            signal(ins, "keyed")

            def copy_mT(b, g):
                wait(act, "mTr", b, g + 1)
                signal(act.activation(mT[g % 2][0:8, :], ps[0:8, BT, S:2 * S], ACT.Copy), "mT_copied")

            def exps(b, g):
                for n in range(3):
                    wait(act, "p2", b, 3 * g + n + 1)
                    if n == 0:
                        wait(act, "pv", b, g - 1)
                    kind, scale = (ACT.Exp, QK_SCALE) if tables[-1] is s0 else (ACT.Copy, 1.0)
                    signal(act.activation(probs[g % 2][:, 512 * n:512 * (n + 1)], bank_of("prob", g, n), kind, scale=scale), "probs_done")

            def copy_o(b, g):
                wait(act, "pv", b, g + 1)
                wait(act, "divided", b, g - 1)
                signal(act.activation(o[g % 2][:, 0:S], ps[:, BO, 0:S], ACT.Copy), "o_copied")

            act.wait_ge(started, 4)
            act.wait_ge(init_done, NINIT)
            copy_xT(0, 0)
            copy_v(0, 0)
            for n in range(2):
                stack(0, 0, n)
                key_copies(0, 0, n)

            def step0(b, r, g, first=False, prep=True, tail=False):
                if not (first and g == 0) and not (tail and g > 0):
                    bb, _, gg = back(b, r, g - 1)
                    exps(bb, gg)
                if g == 0 and prep:
                    copy_xT(b + 1, 1 - r)
                if g >= 2 if first else g < 2 if tail else True:
                    bb, _, gg = back(b, r, g - 2)
                    copy_o(bb, gg)
                if not tail:
                    copy_mT(b, g)
                if g == 1 and prep:
                    copy_v(b + 1, 1 - r)
                if g >= 2 and prep:
                    stack(b + 1, 1 - r, g - 2)
                    key_copies(b + 1, 1 - r, g - 2)
            all_steps(act, step0, 2)

            def experts(l):
                m = ms[l]
                with act.Fori(0, NT // 4) as i:
                    for r in range(2):
                        k = 2 * i + r
                        act.wait_ge(m["xT"], k + 2)
                        act.wait_ge(m["gated"], 2 * i + 1)
                        act.activation(xnT[r][:], ps[:, BT + r, 0:S], ACT.Copy).then_inc(m["xT_copied"], 1)
                if l == 0:
                    act.wait_ge(m["routed"], 13 + 1)
                    act.activation(wts[:, 1, :], wts[:, 0, :], ACT.Exp).then_inc(m["exp_diff"], 1)
                    act.wait_ge(m["logits"], NT + 1)
                    act.activation(SH[:], SH[:], ACT.Gelu).then_inc(m["gelu"], 1)

                def step(i, r, turned=True, hidden=True):
                    n = DEPTH * i + r
                    if turned:
                        act.wait_ge(m["x_turned"], n + 2)
                        act.activation(xgT[r % 2][:], ps[:, 4 + r % 2, 0:P], ACT.Copy).then_inc(m["x_copied"], 1)
                    if hidden:
                        q = (r + 1) % 2
                        act.wait_ge(m["h_ready"], n - 1 + 2)
                        if not first_turn(i) or r >= 3:
                            act.wait_ge(m["h_turned"], n - 3 + 2)
                        act.activation(hid[q], ps[:, q, :], ACT.Gelu if l == 0 else ACT.Relu).then_inc(m["h_active"], 1)
                for r in range(DEPTH):
                    step(0, r, True, r >= 1)
                with act.Fori(1, ET // DEPTH) as i:
                    for r in range(DEPTH):
                        step(i, r)
                step(ET // DEPTH, 0, False, True)

            def look_up():
                with act.Fori(0, NT // 4) as i:
                    for r in range(2):
                        k = 2 * i + r
                        act.wait_ge(ls["zT"], k + 2)
                        act.activation(xnT[r][:], ps[:, BT + r, 0:S], ACT.Copy).then_inc(ls["zT_copied"], 1)
                    for r in range(2):
                        k = 2 * i + r
                        act.wait_ge(ls["means"], k + 2)
                        act.wait_ge(ls["um"], 4 * i + 1)
                        act.activation(usb[r], ps[:, r, 0:2 * D], ACT.Copy).then_inc(ls["u_copied"], 1)
                        act.activation(means[r][:], ps[:, 2 + r, 0:NC], ACT.Copy).then_inc(ls["means_copied"], 1)
                    for r in range(2):
                        act.wait_ge(ls["wmeans"], 2 * i + r + 2)
                        act.activation(wmeans[r][:], ps[:, 2 + r, NC:2 * NC], ACT.Copy).then_inc(ls["wmeans_copied"], 1)
                act.wait_ge(ls["soft"], 2 + 1)
                act.activation(SC[:], SCd[:], ACT.Exp, scale=float(D) ** -0.5).then_inc(ls["soft_exp"], 1)

            def elu_exp(b):
                wait(act, "elu_step", b, 1)
                signal(act.activation(rot[1][:], rot[0][:], ACT.Exp), "elu_exp")

            def copy_v1(b, r):
                wait(act, "proj", b, 1)
                signal(act.activation(vst[r][:, :, :, 0:HD], ps[:, BT, 0:S].rearrange("p (t h d) -> p t h d", t=2, d=HD), ACT.Copy), "v_copied")

            def copy_pk(b, r):
                wait(act, "pkT", b, 1)
                signal(act.activation(pkt[r][:].rearrange("p t d -> p (t d)"), ps[:, BB, 0:2 * D], ACT.Copy), "pk_copied")

            if last_stage >= 1:
                experts(0)
            if last_stage >= 2:
                look_up()
                tables.append(s1)
                act.wait_ge(recleared, 2 * G)
                copy_xT(0, 0)
                elu_exp(0)
                copy_v1(0, 0)
                copy_pk(0, 0)
                for n in range(2):
                    stack(0, 0, n)
                    key_copies(0, 0, n)

                def step1(b, r, g, first=False, prep=True, tail=False):
                    if not tail:
                        exps(b, g)
                    if not (first and g == 0):
                        bb, _, gg = back(b, r, g - 1)
                        copy_o(bb, gg)
                    if g == 0 and prep:
                        copy_xT(b + 1, 1 - r)
                    if g == 1 and prep:
                        elu_exp(b + 1)
                        copy_v1(b + 1, 1 - r)
                    if g == 2 and prep:
                        copy_pk(b + 1, 1 - r)
                    if g >= 2 and prep:
                        stack(b + 1, 1 - r, g - 2)
                        key_copies(b + 1, 1 - r, g - 2)
                all_steps(act, step1, 1)
                tables.pop()
            if last_stage >= 3:
                experts(1)

        @block.tensor
        def _(pe):
            pe.wait_ge(started, 4)
            pe.wait_ge(loaded, 16 * NLOAD)
            pe.matmul(ps[:, BA, 0:2 * D], wqa_t[:], wqb[:], start=True, stop=True)
            pe.matmul(ps[:, BB, 0:2 * D + KVH * HD], wkva_t[:], wkvb[:], start=True, stop=True).then_inc(w_mm, 1)
            pe.wait_ge(consts_cast, 5)
            pe.wait_ge(w_copied, 2)
            pe.wait_ge(init_done, NINIT)

            def residual_read(b):
                wait(pe, "residual", b, RESIDUAL_READ[len(tables) - 1])

            def turn_x(b, r):
                wait(pe, "normed", b, 2)
                wait(pe, "v_copied", b, 0)
                if tables[-1] is s0:
                    wait(pe, "mT_copied", b, -G)
                for t in range(2):
                    mm = pe.transpose(ps[:, BT, t * P:(t + 1) * P], xn[r][:, t, :], ident)
                signal(mm, "xT")

            def project_qk(b, r):
                wait(pe, "xT_copied", b, 1)
                wait(pe, "stacked", b, 0)
                wait(pe, "keyed", b, 0)
                pe.matmul(ps[:, BA, 0:S], wq[:, 0, :], xnT[r][:], start=True, stop=True)
                pe.matmul(ps[:, BA, S:2 * S], wkv[:, 0:D], xnT[r][:], start=True, stop=True)
                pe.matmul(ps[:, BB, 0:S], wq[:, 1, :], xnT[r][:], start=True, stop=True)
                pe.matmul(ps[:, BB, S:2 * S], wkv[:, D:2 * D], xnT[r][:], start=True, stop=True)

            def project_v(b, r):
                wait(pe, "mT_copied", b, 2 - G)
                for t in range(2):
                    c = t * KVH * HD
                    mm = pe.matmul(ps[:, BT, c:c + KVH * HD], xnT[r][:, t * P:(t + 1) * P], wkv[:, 2 * D:], start=True, stop=True)
                signal(mm, "proj")

            def spread(b, n):
                if tables[-1] is s0:
                    wait(pe, "rope_step", b, 5)
                else:
                    wait(pe, "elu_step", b, 4)
                    wait(pe, "pk_copied", b, 1)
                if n == 2:
                    wait(pe, "stacked", b, 1)
                if n == 3:
                    wait(pe, "keyed", b, 4)
                c, w = (0, 0) if n % 2 == 0 else (S, 2)
                for gg in range(2):
                    g = 2 * (n // 2) + gg
                    dst = ps[:, BA + n % 2, gg * S:(gg + 1) * S]
                    pe.matmul(dst, selr[:, w, g, :], hi[:, c:c + S], start=True, stop=False)
                    mm = pe.matmul(dst, selr[:, w + 1, g, :], lo[:, c:c + S], start=False, stop=True)
                signal(mm, "sel")

            def ring(b, kind, g, n):
                R = rings[len(tables) - 1]
                at = ring_at(kind, g, n)
                pk, pg, pn = R[at - 4]
                bb = b if at >= 4 else b - 1
                if tables[-1] is s0 and pk == "prob":
                    bb, _, pg = back(bb, 0, pg - 1)
                if pk == "max":
                    wait(pe, "maxed", bb, 3 * pg + pn + 1)
                elif pk == "prob":
                    wait(pe, "probs_done", bb, 3 * pg + pn + 1)
                elif pk == "look":
                    wait(pe, "found", bb, (3, 7, 10)[pn])
                else:
                    wait(pe, "probs_done", bb, 3 * R[at - 8][1] + R[at - 8][2] + 1)
                return bank_of(kind, g, n)

            def max_scores(b, r, g, n):
                bank = ring(b, "max", g, n)
                wide = lambda h: aboveb[:].unsqueeze(1).broadcast_to((P, h, P))
                if n == 0:
                    pe.matmul(bank, qst[r][:, g, 0:P], keys[r][g][:, :, 0:P], start=True, stop=False)
                    mm = pe.matmul(bank, identb[:], wide(4), start=False, stop=True)
                else:
                    pe.matmul(bank, qst[r][:, g, P:S], keys[r][g][:, 2 * n - 2:2 * n, :], start=True, stop=False)
                    mm = pe.matmul(bank.rearrange("p (j s) -> p j s", s=S)[:, :, P:S], identb[:], wide(2), start=False, stop=True)
                signal(mm, "p1")

            def turn_max(b, g, prep):
                wait(pe, "msplit", b, 2 * g + 2)
                wait(pe, "mT_copied", b, g)
                if g < 2 and prep:
                    wait(pe, "xT_copied", b + 1, 1)
                if g == 2 and prep:
                    wait(pe, "v_copied", b + 1, 1)
                if g == 3:
                    residual_read(b - 1)
                for t in range(2):
                    mm = pe.transpose(ps[0:8, BT, S + t * P:S + (t + 1) * P], mparts[g % 2][:, t].rearrange("p a j -> p (a j)").bitcast(F32), ident)
                signal(mm, "mTr")

            def prob_scores(b, r, g, n, bring):
                bank = ring(bring, "prob", g, n)
                if tables[-1] is s0:
                    wait(pe, "mT_copied", b, g + 1)
                for c in range(2 if n < 2 else 4):
                    j, k, q = (2 * n + c, slice(0, P), slice(0, S)) if n < 2 else (c, slice(P, S), slice(P, S))
                    w = q.stop - q.start
                    dst = bank[:, c * w:(c + 1) * w]
                    mm = pe.matmul(dst, keys[r][g][:, j, k], qst[r][:, g, q], start=True, stop=tables[-1] is s1)
                    if tables[-1] is s0:
                        mm = pe.matmul(dst, pickr[:, j, :], mT[g % 2][:, q], start=False, stop=True)
                signal(mm, "p2")

            def weigh(b, r, g):
                wait(pe, "masked", b, g + 1)
                wait(pe, "divided", b, g)
                first = lambda j: probs[g % 2][:, j * S:(j + 1) * S]
                second = lambda j: probs[g % 2][:, 4 * S + j * P:4 * S + (j + 1) * P]
                values = lambda t, j: vst[r][:, t, g if tables[-1] is s0 else 4 * g + j, :]
                for j in range(4):
                    pe.matmul(ps[32 * j:32 * j + 32, BO, 0:S], values(0, j), first(j), start=True, stop=False)
                for j in range(4):
                    mm = pe.matmul(ps[32 * j:32 * j + 32, BO, P:S], values(1, j), second(j), start=False, stop=True)
                signal(mm, "pv")

            def turn_den(b, g):
                wait(pe, "o_copied", b, g + 1)
                for t in range(2):
                    mm = pe.matmul(ps[:, BO, S + 4 * t:S + 4 * t + 4], o[g % 2][:, t * P:(t + 1) * P], weight_row, start=True, stop=True)
                signal(mm, "den")

            def widen(b, g):
                wait(pe, "rden", b, RDEN[len(tables) - 1] * (g + 1))
                for t in range(2):
                    mm = pe.matmul(ps[:, BO, S + t * P:S + (t + 1) * P], rden[g % 2][:, t].rearrange("p j m -> p (j m)"), ident, start=True, stop=True)
                signal(mm, "wide")

            def give_out(b, prep, tail):
                if tables[-1] is s0:
                    wait(pe, "mT_copied", b + 1, 0 if tail else 3)
                wait(pe, "divided", b, G)
                if tables[-1] is s0:
                    wait(pe, "v_copied", b + 1, 2 if prep else 0 if tail else 1)
                elif prep:
                    wait(pe, "xT_copied", b + 1, 2)
                elif tail:
                    residual_read(b - 1)
                w = wout if tables[-1] is s0 else wo
                for t in range(2):
                    for g in range(G):
                        mm = pe.matmul(ps[:, BT, t * P:(t + 1) * P], on[:, g, t * P:(t + 1) * P], w[:, g, :], start=(g == 0), stop=(g == G - 1))
                signal(mm, "outp")

            turn_x(0, 0)
            project_qk(0, 0)
            project_v(0, 0)
            for n in range(4):
                spread(0, n)

            def step0(b, r, g, first=False, prep=True, tail=False):
                if g == 0 and not tail:
                    wait(pe, "stacked", b, 2)
                    wait(pe, "keyed", b, 8)
                    wait(pe, "v_copied", b, 1)
                for n in range(3):
                    if n == 1 and (g >= 3 if first else g < 3 if tail else True):
                        bb, _, gg = back(b, r, g - 3)
                        widen(bb, gg)
                    if not (first and g == 0) and not (tail and g > 0):
                        bb, rr, gg = back(b, r, g - 1)
                        prob_scores(bb, rr, gg, n, b)
                    if not tail:
                        max_scores(b, r, g, n)
                if g == 0 and prep:
                    turn_x(b + 1, 1 - r)
                if g >= 2 if first else g < 2 if tail else True:
                    weigh(*back(b, r, g - 2))
                if g == 1 and prep:
                    project_qk(b + 1, 1 - r)
                if g >= 2 and prep:
                    spread(b + 1, 2 * (g - 2))
                    spread(b + 1, 2 * (g - 2) + 1)
                if not tail:
                    turn_max(b, g, prep)
                if g >= 2 if first else g < 2 if tail else True:
                    bb, _, gg = back(b, r, g - 2)
                    turn_den(bb, gg)
                if g == 1 and prep:
                    project_v(b + 1, 1 - r)
                if g == 2 and not first:
                    give_out(b - 1, prep, tail)
            all_steps(pe, step0, 3)

            def experts(l):
                m = ms[l]
                pe.wait_ge(w_loaded[l], 16 * (8 if l == 0 else 4))

                def turn_pair(k, i, r):
                    pe.wait_ge(m["normed"], 2 * k + 2 + 1)
                    pe.wait_ge(m["xT_copied"], 2 * i + 1)
                    for t in range(2):
                        mm = pe.transpose(ps[:, BT + r, t * P:(t + 1) * P], xn[r][:, t, :], ident)
                    mm.then_inc(m["xT"], 1)

                w = D + E if l == 0 else E
                per = 2 if l == 0 else 1
                with pe.Fori(0, NT // 4) as i:
                    for r in range(2):
                        turn_pair(2 * i + r, i, r)
                    for r in range(2):
                        k = 2 * i + r
                        pe.wait_ge(m["xT_copied"], k + 2)
                        pe.wait_ge(m["logits"], 2 * i * per + 1)
                        for t in range(2):
                            mm = pe.matmul(ps[:, 6 + r, t * w:(t + 1) * w], xnT[r][:, t * P:(t + 1) * P], gates[l][:], start=True, stop=True)
                        mm.then_inc(m["gated"], 1)
                pe.wait_ge(m["routed"], 13 + 1)
                picks = picked[:].rearrange("p t e -> p (t e)")
                pe.matmul(ps[:, BT, 0:P], before_m, picks, start=True, stop=True)
                pe.matmul(ps[:, BT, P:2 * P], ones_m, picks, start=True, stop=True).then_inc(m["counted"], 1)
                nothing = X[:, NT, :]
                pe.matmul(ps[:, BA, 0:ETS], nothing, iota_t, start=True, stop=False)
                with pe.Fori(0, NT) as t:
                    for k in range(TOPK):
                        pe.wait_ge(m["hot_b"], 2 * t + k + 2)
                        pe.matmul(ps[:, BA, 0:ETS], hot[k][:], hotn[k][:], start=False, stop=False).then_inc(m["hot_used"], 1)
                pe.matmul(ps[:, BA, 0:ETS], nothing, iota_t, start=False, stop=True).then_inc(m["inverse"], 1)
                pe.wait_ge(m["tabled"], 6 + 1)
                pe.wait_ge(moe_cast, 7 + 6 * l)

                def turn_rows(n, i, r):
                    pe.wait_ge(gathered[r], gathers(l, i + 1))
                    pe.transpose(ps[:, 4 + r % 2, 0:P], xg[r][:], ident).then_inc(m["x_turned"], 1)

                def into_hidden(n, r, e):
                    pe.wait_ge(m["x_copied"], n + 2)
                    pe.matmul(ps[:, r % 2, :], of_expert[:, ds(e * P, P)], bias3[l][:, 0:FF], start=True, stop=False)
                    pe.matmul(ps[:, r % 2, :], xgT[r % 2][:], w1[:, ds(e * FF, FF)], start=False, stop=True).then_inc(m["h_ready"], 1)

                def turn_hidden(n, r):
                    pe.wait_ge(m["h_active"], n + 2)
                    for c in range(FC):
                        mm = pe.transpose(ps[:, 2 + r % 2, c * P:(c + 1) * P], hid[r % 2][:, c * P:(c + 1) * P], ident)
                    mm.then_inc(m["h_turned"], 1)

                def out_of_hidden(n, r, e, first):
                    pe.wait_ge(m["h_copied"], n + 2)
                    if not first:
                        pe.wait_ge(m["y_copied"], n - 2 + 2)
                    pe.matmul(ps[:, 6 + r % 2, 0:D], of_expert[:, ds(e * P, P)], bias3[l][:, FF:], start=True, stop=False)
                    for c in range(FC):
                        mm = pe.matmul(ps[:, 6 + r % 2, 0:D], hidT[r % 2][:, c * P:(c + 1) * P], w2[:, ds(e * FF + c * D, D)], start=False, stop=(c == FC - 1))
                    mm.then_inc(m["y_ready"], 1)

                expert_of = lambda n: pe.value_load(eid[0:1, ds(n, 1)], min_val=0, max_val=E - 1)

                def step(i, r, a=True, b=True, c=True, d=True):
                    n = DEPTH * i + r
                    e_in = expert_of(n - 1) if b else None
                    e_out = expert_of(n - 3) if d else None
                    if a:
                        turn_rows(n, i, r)
                    if b:
                        into_hidden(n - 1, r + 3, e_in)
                    if c:
                        turn_hidden(n - 2, r + 2)
                    if d:
                        out_of_hidden(n - 3, r + 1, e_out, first_turn(i))
                for r in range(DEPTH):
                    step(0, r, True, r >= 1, r >= 2, r >= 3)
                with pe.Fori(1, ET // DEPTH) as i:
                    for r in range(DEPTH):
                        step(i, r)
                for r in range(3):
                    step(ET // DEPTH, r, False, r < 1, r < 2, True)

            def look_up():
                pe.wait_ge(look_loaded, 64)
                with pe.Fori(0, NT // 4) as i:
                    for r in range(2):
                        k = 2 * i + r
                        pe.wait_ge(ls["normed"], 2 * k + 2 + 1)
                        pe.wait_ge(ls["zT_copied"], 2 * i + 1)
                        for t in range(2):
                            mm = pe.transpose(ps[:, BT + r, t * P:(t + 1) * P], xn[r][:, t, :], ident)
                        mm.then_inc(ls["zT"], 1)
                    for r in range(2):
                        k = 2 * i + r
                        pe.wait_ge(ls["gate_in"], 2 * i + 1)
                        pe.wait_ge(ls["zT_copied"], k + 2)
                        for t in range(2):
                            pe.matmul(ps[:, 6 + r, t * D:(t + 1) * D], running, xn[r][:, t, :], start=True, stop=True)
                            pe.matmul(ps[:, r, t * D:(t + 1) * D], xnT[r][:, t * P:(t + 1) * P], w_look[:, 3, :], start=True, stop=True)
                            mm = pe.matmul(ps[:, 2 + r, 4 * t:4 * t + 4], xn[r][:, t, :], chunk_mean, start=True, stop=True)
                        mm.then_inc(ls["means"], 1)
                    for r in range(2):
                        pe.wait_ge(ls["means_copied"], 2 * i + r + 2)
                        pe.matmul(ps[:, 2 + r, NC:2 * NC], w_look[:, 4, :], means[r][:], start=True, stop=True).then_inc(ls["wmeans"], 1)
                    for r in range(2):
                        pe.wait_ge(ls["wmeans_copied"], 2 * i + r + 2)
                        for t in range(2):
                            mm = pe.matmul(ps[:, 2 + r, (2 + t) * NC:(3 + t) * NC], xnT[r][:, t * P:(t + 1) * P], wmeans[r][:], start=True, stop=True)
                        mm.then_inc(ls["scores"], 1)

            def project1(b, r):
                wait(pe, "xT_copied", b, 1)
                wait(pe, "stacked", b, 0)
                wait(pe, "state_own", b, -1)
                for n in range(2):
                    pe.matmul(ps[:, BA, n * S:(n + 1) * S], wqkv[:, n, :], xnT[r][:], start=True, stop=True)
                residual_read(b - 2)
                for t in range(2):
                    mm = pe.matmul(ps[:, BT, t * D:(t + 1) * D], xnT[r][:, t * P:(t + 1) * P], wqkv[:, 2, :], start=True, stop=True)
                signal(mm, "proj")

            def turn_keys(b, r):
                wait(pe, "elu_step", b, 2)
                wait(pe, "state_own", b, 0)
                for t in range(2):
                    mm = pe.transpose(ps[:, BB, t * D:(t + 1) * D], pqk[r][:, S + t * P:S + (t + 1) * P], ident)
                signal(mm, "pkT")

            def chunk_states(b, r):
                wait(pe, "stacked", b, 2)
                wait(pe, "keyed", b, 8)
                wait(pe, "v_copied", b, 1)
                for n in range(NS):
                    rows_n = SEG * (n % 4 + 1)
                    dst = ps[:, BA + n // 4, (n % 4) * D:(n % 4 + 1) * D].rearrange("p (h d) -> p h d", d=HD)
                    if n >= 4:
                        pe.matmul(dst, pkt[r][:, 0, :], vst[r][:, 0, :, 0:HD], start=True, stop=False)
                    mm = pe.matmul(dst, pkt[r][0:rows_n, n // 4, :], vst[r][0:rows_n, n // 4, :, 0:HD], start=(n < 4), stop=True)
                    if n in (3, NS - 1):
                        signal(mm, "state")

            def look_states(b, r):
                wait(pe, "state_own", b, 2)
                for n, (t, c, at) in enumerate(LOOKS):
                    bank = ring(b, "look", 0, n)
                    signal(pe.matmul(bank[:, 0:c * D], pqk[r][:, t * P:(t + 1) * P], states[:, at:at + c, :], start=True, stop=True), "looked")

            if last_stage >= 1:
                experts(0)
            if last_stage >= 2:
                look_up()
                tables.append(s1)
                pe.wait_ge(ls["w_scaled"], 1 + 1)
                pe.wait_ge(ls["gate_in"], NT // 2 + 1)
                turn_x(0, 0)
                project1(0, 0)
                turn_keys(0, 0)
                for n in range(4):
                    spread(0, n)

                def step1(b, r, g, first=False, prep=True, tail=False):
                    if g >= 2 if first else True:
                        bb, _, gg = back(b, r, g - 2)
                        widen(bb, gg)
                    if g == 0 and not tail:
                        chunk_states(b, r)
                    if not tail:
                        for n in range(3):
                            prob_scores(b, r, g, n, b)
                    if g == 1 and not first:
                        give_out(b - 1, prep, tail)
                    if g == 2 and not tail:
                        look_states(b, r)
                    if not (first and g == 0) and not (tail and g > 0):
                        weigh(*back(b, r, g - 1))
                    if g == 0 and prep:
                        turn_x(b + 1, 1 - r)
                    if g == 1 and prep:
                        project1(b + 1, 1 - r)
                    if not (first and g == 0) and not (tail and g > 0):
                        bb, _, gg = back(b, r, g - 1)
                        turn_den(bb, gg)
                    if g == 2 and prep:
                        turn_keys(b + 1, 1 - r)
                    if g >= 2 and prep:
                        spread(b + 1, 2 * (g - 2))
                        spread(b + 1, 2 * (g - 2) + 1)
                all_steps(pe, step1, 2)
                tables.pop()
            if last_stage >= 3:
                experts(1)


def kernel(**inputs):
    import concourse.bacc as _bacc
    from concourse.bass_utils import run_bass_kernel_spmd as _run

    arrays = {f"in_{k}": v for k, v in _layout(inputs).items()}
    nc = _bacc.Bacc("TRN2", target_bir_lowering=False, num_devices=1)
    aps = {k[3:]: nc.dram_tensor(k, v.shape, mybir.dt.from_np(v.dtype), kind="ExternalInput").ap() for k, v in arrays.items()}
    out = nc.dram_tensor("out_y", (B * S, D), F32, kind="ExternalOutput").ap()
    build(nc, aps, out)
    r = _run(nc, [arrays], core_ids=[0])
    return r.results[0]["out_y"].reshape(B, S, D)
```

```python
from contextlib import ExitStack

import numpy as np

import concourse.bass as bass
from concourse import mybir

F32 = mybir.dt.float32
F32R = mybir.dt.float32r
BF16 = mybir.dt.bfloat16
I32 = mybir.dt.int32
ALU = mybir.AluOpType
ACT = mybir.ActivationFunctionType
AX = mybir.AxisListType
ds = bass.ds

P = 128
B, S, D = 8, 256, 128
NT = B * S // P
H, HD = 16, 8
KVH, QL, KVL = 4, 64, 32
G = 4
LN_EPS = 1e-5
QK_SCALE = float(HD) ** -0.5
SEG = 32
NC = S // SEG
NS = NC - 1
RMS_EPS = 1e-6
NEG = -1e30
E, FF, TOPK = 8, 512, 2
FC = FF // P
W1 = FF + FC
ET = (B * S * TOPK - E) // P + E
ET += -ET % 4
ETS = ET + 1
DEPTH = 4
LOWEST = -3e38
MAGIC = 0x5F3759DF


def _constants():
    inv = (1.0 / np.float32(10000.0) ** (np.arange(0, HD, 2, dtype=np.float32) / np.float32(HD))).astype(np.float32)
    angle = np.outer(np.arange(S, dtype=np.float32), inv)
    row = np.arange(P) % HD
    cos = np.cos(angle)[:, row // 2].T
    sin = (np.sin(angle)[:, row // 2] * np.where(row % 2 == 0, -1.0, 1.0)).T
    rope = np.concatenate([cos, cos, sin, sin], axis=1).astype(np.float32)
    sel = np.zeros((4, P, G, P), np.float32)
    for h in range(H):
        for d in range(HD):
            for s in range(3):
                sel[s % 2, h * HD + d, h // 4, 32 * (h % 4) + 8 * s + d] = 1.0
                sel[2 + s // 2, h * HD + d, h // 4, 32 * (h % 4) + 8 * s + d] = 1.0
    p = np.arange(P)
    above = np.where(p[None, :] > p[:, None], np.float32(NEG), np.float32(0.0))
    ident = np.eye(P, dtype=np.float32)
    max_rows = ((p[:, None] % 32 == 3 * HD) | (p[:, None] % 32 == 3 * HD + 1)).astype(np.float32)
    weight_row = (p[:, None] == 32 * np.arange(4)[None, :] + HD).astype(np.float32)
    before = (p[:, None] < p[None, :]).astype(np.float32)
    pair = 2 * (P * np.arange(NT)[None, :, None] + p[:, None, None]) + np.arange(TOPK)[None, None, :] + 1
    of_expert = np.zeros((P, E, P), np.float32)
    for part in range(3):
        for e in range(E):
            of_expert[32 * part + e, e, :] = 1.0
    same = (p[:, None] // SEG == p[None, :] // SEG) & (p[:, None] <= p[None, :])
    running = np.where(same, np.float32(1) / (p[None, :] % SEG + 1).astype(np.float32), np.float32(0))
    chunk = np.where(p[:, None] // SEG == np.arange(P // SEG)[None, :], np.float32(1 / SEG), np.float32(0))
    at = (p[:, None] // SEG + (P // SEG) * np.arange(2)[None, :])[:, :, None]
    unseen = np.where(at > np.arange(NC)[None, None, :], np.float32(0), np.float32(NEG)).reshape(P, 2 * NC)
    own_head = (p[:, None] // HD == p[None, :] // HD).astype(np.float32)
    every = lambda a: np.broadcast_to(np.asarray(a, np.float32), (P, len(a)))
    route = np.concatenate([before, np.ones((P, P)), every(np.arange(P)), every(np.arange(ETS)),
                            pair.reshape(P, NT * TOPK), every(E - np.arange(E)), TOPK * B * S + 1 + p[:, None] + P * (np.arange(ETS)[None, :] % DEPTH),
                            of_expert.reshape(P, E * P)], axis=1).astype(np.float32)
    return {"c_look": np.concatenate([running, chunk, unseen, own_head], axis=1).astype(np.float32),
            "c_rope": rope, "c_sel": sel.transpose(1, 0, 2, 3).reshape(P, 4 * G * P).copy(),
            "c_route": route,
            "c_misc": np.concatenate([ident, above, weight_row, max_rows], axis=1)}


def _by_head(w, row=None):
    out = np.zeros((G, 4, 32, D), np.float32)
    out[:, :, 0:HD] = w.reshape(G, 4, HD, D)
    if row is not None:
        out[0, 0, HD] = row
    return out.reshape(G, P, D).transpose(1, 0, 2)


def _layout(a):
    f = {k: np.asarray(v) for k, v in a.items()}
    swap = np.arange(P) ^ 1
    kv = f["L0_attn_Wkvb"].reshape(KVL, KVH, HD, 2)
    k_rep = np.repeat(kv[..., 0][:, :, None, :], H // KVH, axis=2).reshape(KVL, P)
    v_own = kv[..., 1].reshape(KVL, KVH * HD)
    out = {
        "x": f["L0_attn_x"].reshape(NT, P, D),
        "wqa_t": f["L0_attn_Wqa"].T,
        "wqb": np.concatenate([f["L0_attn_Wqb"], f["L0_attn_Wqb"][:, swap]], axis=1),
        "wkva_t": f["L0_attn_Wkva"].T,
        "wkvb": np.concatenate([k_rep, k_rep[:, swap], v_own], axis=1),
        "wout": _by_head(f["L0_attn_Wout"], f["L0_attn_bout"]),
    }
    for n, names in enumerate((("W1", "b1", "W2", "b2"), ("w1", "b1", "w2", "b2"))):
        w1, b1, w2, b2 = (f[f"L{n}_ffn_{m}"] for m in names)
        out |= {f"w1_{n}": np.concatenate([w1.transpose(1, 0, 2), b1.reshape(E, FC, P).transpose(2, 0, 1)], axis=2),
                f"w2_{n}": w2.reshape(E, FC, P, D).transpose(2, 0, 1, 3), f"b_{n}": b2}
    out["w_look"] = np.concatenate([f["L1_attn_Wq"].T, f["L1_attn_Wk"].T, f["L1_attn_Wv"].T,
                                    f["L1_attn_Wu"].T, f["L1_attn_Wu"]], axis=1)
    out["wo"] = _by_head(f["L1_attn_Wo"].T)
    out["norm_w"] = f["L1_attn_norm_w"].reshape(D, 1)
    out["gates_0"] = np.concatenate([f["L0_ffn_shared_W"], f["L0_ffn_gate_W"]], axis=1)
    out["gates_1"] = f["L1_ffn_gate_w"]
    out["rows"] = np.concatenate([f["L0_ffn_shared_b"], f["L0_ffn_gamma"], f["L0_ffn_beta"], f["L1_ffn_gate_b"]]).reshape(1, -1)
    out |= _constants()
    return {k: np.ascontiguousarray(v) for k, v in out.items()}


def first_turn(i):
    return isinstance(i, int) and i == 0


class Chain:

    def __init__(self, eng, sem, n=0):
        self.eng, self.sem, self.n = eng, sem, n

    def add(self, ins):
        ins.then_inc(self.sem, 1)
        self.n += 1

    def wait(self):
        self.eng.wait_ge(self.sem, self.n)

    def __call__(self, ins):
        self.add(ins)
        self.wait()


def build(nc, inp, out, last_stage=3):
    ctx = ExitStack()
    with ctx:
        def sb(name, shape, dt=F32):
            return ctx.enter_context(nc.sbuf_tensor(name, shape, dt))

        def sem(name):
            return ctx.enter_context(nc.semaphore(name))

        ps = ctx.enter_context(nc.psum_tensor("ps", [P, 8, 512], F32))
        BT, BA, BB, BO = 4, 5, 6, 7

        X = sb("X", [P, NT + 2, D])
        stats = sb("stats", [P, NT + 2, 6])
        mv = sb("mv", [P, NT + 2, 2])
        rstd2 = sb("rstd2", [P, 2, NT + 2])
        rstd = rstd2[:, 0, :]
        var2 = sb("var2", [P, 2, NT + 2])
        nt1 = sb("nt1", [P, 2, NT + 2])
        nt2 = sb("nt2", [P, 2, NT + 2])
        rope = sb("rope", [P, 2, 2 * S])
        misc = sb("misc", [P, 2 * P + 5])
        selr = sb("selr", [P, 4, G, P], F32R)
        ident = misc[:, 0:P]
        max_rows = misc[:, 2 * P + 4:]
        weight_row = misc[:, 2 * P:2 * P + 4]
        identb = sb("identb", [P, P], BF16)
        aboveb = sb("aboveb", [P, P], BF16)
        wqa_t = sb("wqa_t", [QL, D])
        wqb = sb("wqb", [QL, 2 * D])
        wkva_t = sb("wkva_t", [KVL, D])
        wkvb = sb("wkvb", [KVL, 2 * D + KVH * HD])
        wq = sb("wq", [D, 2, D])
        wkv = sb("wkv", [D, 2 * D + KVH * HD])
        wout = sb("wout", [P, G, D])

        xn = [sb(f"xn{r}", [P, 2, D]) for r in range(2)]
        xnT = [sb(f"xnT{r}", [D, S]) for r in range(2)]
        rot = [sb(f"rot{r}", [P, 2 * S]) for r in range(3)]
        hi = sb("hi", [P, 2 * S], F32R)
        lo = sb("lo", [P, 2 * S], F32R)
        qst = [sb(f"qst{r}", [P, G, S], F32R) for r in range(2)]
        keys_a = [sb(f"keys_a{n}", [P, 4, S], F32R) for n in range(2)]
        with ExitStack() as shared:
            keys_b = [shared.enter_context(nc.sbuf_tensor(f"keys_b{n}", [P, 4, S], F32R)) for n in range(6)]
        SH = sb("SH", [P, NT, D])
        YB = sb("YB", [P, NT, TOPK * D])
        keys = [k[:] for k in keys_a + keys_b]
        keys = [keys[0:G], keys[G:]]
        vst = [sb(f"vst{r}", [P, 2, H, 32]) for r in range(2)]
        negm = [sb(f"negm{r}", [P, 2, 4]) for r in range(2)]
        mparts = [sb(f"mparts{r}", [P, 2, 4, 32], F32R) for r in range(2)]
        qm = [sb(f"qm{r}", [P, S], F32R) for r in range(2)]
        probs = [sb(f"probs{r}", [P, 4 * 3 * P]) for r in range(2)]
        on = sb("on", [P, G, S])
        o = [sb(f"o{r}", [P, W1]) for r in range(2)]
        denq = sb("denq", [P, 2, 4])
        rdenq = sb("rdenq", [P, 2, 4])
        rden = [sb(f"rden{r}", [P, 2, 4, 32]) for r in range(2)]

        look = sb("look", [P, 2 * P + P // SEG + 2 * NC])
        running, chunk_mean = look[:, 0:P], look[:, P:P + P // SEG]
        unseen = look[:, P + P // SEG:P + P // SEG + 2 * NC]
        own_head = look[:, P + P // SEG + 2 * NC:]
        w_look = sb("w_look", [D, 5, D])
        wo = sb("wo", [P, G, D])
        norm_w = sb("norm_w", [D, 1])
        wqkv = sb("wqkv", [D, 3, D])
        rms = sb("rms", [P, NT + 2])
        usb = [rot[r][:, 0:2 * D] for r in range(2)]
        um = [rot[r][:, 2 * D:4 * D] for r in range(2)]
        means = sb("means", [D, B * NC])
        wmeans = sb("wmeans", [D, B * NC])
        SC = sb("SC", [P, NT, NC + 1])
        SCd = sb("SCd", [P, NT, NC + 1])
        GT = sb("GT", [P, NT + 2, NC + 1])
        sct = sb("sct", [P, 3, NT])
        pqk = [sb(f"pqk{r}", [P, 2 * S]) for r in range(2)]
        pkt = [sb(f"pkt{r}", [P, 2, D]) for r in range(2)]
        states = sb("states", [P, NS, D])
        found = [rot[2][:, 2 * D * n:2 * D * (n + 1)].rearrange("p (t d) -> p t d", d=D) for n in range(2)]
        zt = sb("zt", [P, 2, D])

        NROUTE = 3 * P + 2 * ETS + NT * TOPK + E
        route = sb("route", [P, NROUTE])
        before_m, ones_m, iota_p = route[:, 0:P], route[:, P:2 * P], route[:, 2 * P:3 * P]
        iota_t = route[:, 3 * P:3 * P + ETS]
        pair_no = route[:, 3 * P + ETS:3 * P + ETS + NT * TOPK]
        rev_e = route[:, NROUTE - ETS - E:NROUTE - ETS]
        spare_no = route[:, NROUTE - ETS:NROUTE]
        of_expert = sb("of_expert", [P, E * P], BF16)
        rows = sb("rows", [P, 3 * D + E])
        shared_b, gamma, beta, gate_b = rows[:, 0:D], rows[:, D:2 * D], rows[:, 2 * D:3 * D], rows[:, 3 * D:]
        w1 = sb("w1", [D, E * W1])
        w2 = sb("w2", [P, E * FC * D])
        gates = [sb("gates_0", [D, D + E]), sb("gates_1", [D, E])]
        bias = [sb(f"bias_{n}", [E, D]) for n in range(2)]
        bias_rest = sb("bias_rest", [E, D])
        bias_mid = sb("bias_mid", [E, D], BF16)
        bias3 = [sb(f"bias3_{n}", [P, D], BF16) for n in range(2)]
        LG = sb("LG", [P, NT, E])
        LG2 = sb("LG2", [P, NT, E])
        rt = [sb(f"rt{n}", [P, NT, E]) for n in range(3)]
        top = sb("top", [P, 4, NT])
        first = [sb(f"first{n}", [P, NT, E]) for n in range(2)]
        picked = sb("picked", [P, NT, E])
        wts = sb("wts", [P, 5, NT])
        totals = sb("totals", [P, E, NT])
        upto = sb("upto", [P, E, NT])
        per_e = sb("per_e", [P, 8, E])
        per_ei = sb("per_ei", [P, E], I32)
        slot = sb("slot", [P, NT, TOPK])
        sloti = sb("sloti", [P, 3, NT * TOPK], I32)
        slotf = sb("slotf", [P, 2, NT * TOPK])
        halves = [YB[:, n * NT // 2:(n + 1) * NT // 2, :].rearrange("p a s -> p (a s)").rearrange("p (t d) -> p t d", d=D) for n in range(2)]
        rows_n, turned = halves
        HB = 8
        hot = [turned[:, n * HB:(n + 1) * HB, :] for n in range(2)]
        hotn = probs[0][:, 0:NT * TOPK * ETS].rearrange("p (q t) -> p q t", t=ETS)
        etab = sb("etab", [P, ETS, E])
        eidf = sb("eidf", [P, 2, ETS])
        eid = sb("eid", [P, ETS], I32)
        inv = sb("inv", [P, 3, ETS])
        tab = sb("tab", [P, 2, ETS], I32)
        gidx = [sb(f"gidx{r}", [P, 1], I32) for r in range(DEPTH)]
        sidx = [sb(f"sidx{r}", [P, 1], I32) for r in range(DEPTH)]
        xg = [sb(f"xg{r}", [P, D]) for r in range(DEPTH)]
        xgT = [sb(f"xgT{r}", [D, P]) for r in range(2)]
        hidT = [probs[r][:, 0:FF] for r in range(2)]
        w1s = [o[r][:] for r in range(2)]
        yt = [sb(f"yt{r}", [P, D]) for r in range(DEPTH)]
        xbuf = [nc.dram_tensor(f"xbuf_{n}", (B * S + DEPTH * P // 2, D), F32, kind="Internal").ap() for n in range(2)]
        ybuf = [nc.dram_tensor(f"ybuf_{n}", (TOPK * B * S + DEPTH * P, D), F32, kind="Internal").ap() for n in range(2)]

        x_loaded = sem("x_loaded")
        loaded = sem("loaded")
        exp_ready = sem("exp_ready")
        w_loaded = [sem(f"w_loaded_{n}") for n in range(2)]
        moe_cast = sem("moe_cast")
        MN = ("stats", "rstd", "normed", "xT", "xT_copied", "gated", "logits", "routed", "exp_diff",
              "counted", "hot", "hot_used", "inverse", "tabled", "gidx", "sidx", "x_turned", "x_copied",
              "staged", "h_ready", "h_active", "y_ready", "y_copied", "gelu", "mixed", "combined")
        ms = [{n: sem(f"m{l}_{n}") for n in MN} for l in range(2)]
        rows_out = [sem(f"rows_out{q}") for q in range(4)]
        gathered = [sem(f"gathered{r}") for r in range(DEPTH)]
        scattered = [sem(f"scattered{r}") for r in range(DEPTH)]

        def gathers(l, k):
            return 16 * k + 16 * l * (ET // DEPTH)

        def scatters(l, k):
            return 16 * k + 16 + 16 * l * (ET // DEPTH + 1)

        ms_back = [[sem(f"m{l}_back{q}") for q in range(4)] for l in range(2)]
        consts_cast = sem("consts_cast")
        w_mm = sem("w_mm")
        w_copied = sem("w_copied")
        init_done = sem("init_done")
        started = sem("started")
        recleared = sem("recleared")
        stats_done = sem("stats_done")
        rstd_step = sem("rstd_step")
        stored = sem("stored")

        A0 = dict(normed=2, xT=1, xT_copied=1, proj=1, rope_step=5, v_copied=1, sel=4, stacked=2, keyed=4, keyed_v=4,
                  p1=12, maxed=12, msplit=8, mTr=4, max_added=4, p2=12, probs_done=12, masked=4, pv=4,
                  o_copied=4, den=4, rden=8, wide=4, divided=4, outp=1, residual=3)
        s0 = {n: (sem("a_" + n), c, 0) for n, c in A0.items()}
        A1 = dict(normed=2, xT=1, xT_copied=1, proj=1, elu_step=4, elu_exp=1, v_copied=1, sel=4, stacked=2, keyed=4, keyed_v=4,
                  pkT=1, pk_copied=1, p2=12, probs_done=12, masked=4, pv=4, o_copied=4, den=4, rden=12, wide=4, divided=4, outp=1,
                  state=2, state_own=2, looked=3, found=10, residual=8)
        s1 = {n: (s0[n][0], c, B * A0[n]) if n in A0 else (sem("a1_" + n), c, 0) for n, c in A1.items()}
        LN = ("stats", "rstd", "normed", "zT", "zT_copied", "means", "means_copied", "wmeans", "wmeans_copied", "scores",
              "u_copied", "gate_in", "um", "soft", "soft_exp", "w_scaled")
        ls = {n: sem("look_" + n) for n in LN}
        look_loaded = sem("look_loaded")
        tables = [s0]

        def wait(eng, name, b, k):
            sm, c, before = tables[-1][name]
            value = b * c + k
            if isinstance(value, int) and value <= 0:
                return
            eng.wait_ge(sm, value + before + 1)

        def signal(ins, name):
            ins.then_inc(tables[-1][name][0], 1)

        block = ctx.enter_context(nc.Block())

        LOOKS = ((1, 4, 0), (1, 3, 4), (0, 3, 0))
        LOOKED = (4, 7, 10)
        ORDER0 = [[(k, n) for k in ("prob", "max") for n in range(3)]] + [[(k, n) for n in range(3) for k in ("prob", "max")]] * (G - 1)
        RING0 = [(k, g, n) for g in range(G) for k, n in ORDER0[g]]
        RING1 = [("prob", 0, n) for n in range(3)] + [("state", 0, n) for n in range(2)] \
            + [("prob", g, n) for g in (1, 2) for n in range(3)] + [("look", 0, n) for n in range(2)] \
            + [("prob", 3, n) for n in range(3)] + [("none", 0, n) for n in range(3)] + [("look", 0, 2)]
        rings = {0: RING0, 1: RING1}

        def ring_at(kind, g, n):
            if tables[-1] is s0 and kind == "prob":
                g = (g + 1) % G
            return rings[len(tables) - 1].index((kind, g, n))

        def bank_of(kind, g, n):
            return ps[:, ring_at(kind, g, n) % 4, :]

        def look_bank(n):
            return bank_of("look", 0, n)

        NLOAD = 9
        NINIT = 7 + 2 * G
        RDEN = (2, 3)
        RESIDUAL_READ = (1, 3)

        def back(b, r, g):
            return (b - 1, 1 - r, g + G) if g < 0 else (b, r, g)

        def all_steps(eng, step, tail):
            for g in range(G):
                step(0, 0, g, first=True)
            with eng.Fori(0, (B - 2) // 2) as i:
                for n in range(2):
                    for g in range(G):
                        step(2 * i + 1 + n, 1 - n, g)
            for g in range(G):
                step(B - 1, (B - 1) % 2, g, prep=False)
            for g in range(tail):
                step(B, B % 2, g, prep=False, tail=True)

        @block.sync
        def _(sp):
            for t in range(4):
                sp.dma_start(X[:, 4 * t:4 * t + 4, :], inp["x"][4 * t:4 * t + 4].rearrange("t p d -> p t d")).then_inc(x_loaded, 16)
            sp.dma_start(wqa_t[:], inp["wqa_t"][:, :]).then_inc(loaded, 16)
            sp.dma_start(wqb[:], inp["wqb"][:, :]).then_inc(loaded, 16)
            sp.dma_start(wkva_t[:], inp["wkva_t"][:, :]).then_inc(loaded, 16)
            sp.dma_start(wkvb[:], inp["wkvb"][:, :]).then_inc(loaded, 16)
            sp.dma_start(wout[:], inp["wout"][:, :, :]).then_inc(loaded, 16)
            sp.dma_start(rope[:].rearrange("p a s -> p (a s)"), inp["c_rope"][:, :]).then_inc(loaded, 16)
            sp.dma_start(misc[:], inp["c_misc"][:, :]).then_inc(loaded, 16)
            sp.dma_start(probs[0][:, 0:1024], inp["c_sel"][:, 0:1024]).then_inc(loaded, 16)
            sp.dma_start(probs[1][:, 0:1024], inp["c_sel"][:, 1024:2048]).then_inc(loaded, 16)
            for sm in [a for a, _, _ in s0.values()] + (list(ms[0].values()) if last_stage >= 1 else []) \
                    + ([a for n, (a, _, _) in s1.items() if n not in s0] + list(ls.values()) if last_stage >= 2 else []) \
                    + (list(ms[1].values()) if last_stage >= 3 else []):
                sp.sem_inc(sm, 1)
            sp.sem_inc(started, 4)
            sp.dma_start(route[:], inp["c_route"][:, 0:NROUTE]).then_inc(w_loaded[0], 16)
            for n in range(2):
                sp.dma_start(pqk[n][:], inp["c_route"][:, NROUTE + n * FF:NROUTE + (n + 1) * FF]).then_inc(w_loaded[0], 16)
            sp.dma_start(rows[:], inp["rows"][0:1, :].broadcast_to((P, 3 * D + E))).then_inc(w_loaded[0], 16)
            def load_experts(n):
                sp.dma_start(gates[n][:], inp[f"gates_{n}"][:, :]).then_inc(w_loaded[n], 16)
                sp.dma_start(bias[n][:], inp[f"b_{n}"][:, :]).then_inc(w_loaded[n], 16)
                sp.dma_start(w1[:].rearrange("p (e f) -> p e f", e=E), inp[f"w1_{n}"][:, :, :]).then_inc(w_loaded[n], 16)
                sp.dma_start(w2[:].rearrange("p (e c d) -> p e c d", e=E, c=FC), inp[f"w2_{n}"][:, :, :, :]).then_inc(w_loaded[n], 16)

            load_experts(0)
            sp.dma_start(look[:], inp["c_look"][:, :]).then_inc(look_loaded, 16)
            sp.dma_start(w_look[:].rearrange("p a d -> p (a d)"), inp["w_look"][:, :]).then_inc(look_loaded, 16)
            sp.dma_start(norm_w[:], inp["norm_w"][:, :]).then_inc(look_loaded, 16)
            sp.dma_start(wo[:], inp["wo"][:, :, :]).then_inc(look_loaded, 16)

            def experts(l):
                m = ms[l]
                xr = xbuf[l][0:B * S, :].rearrange("(t p) d -> t p d", p=P)
                sp.wait_ge(init_done, NINIT)
                for r in range(2):
                    sp.dma_start(xbuf[l][B * S + r * P:B * S + (r + 1) * P, :], X[:, NT + r, :]).then_inc(rows_out[r], 16)
                for q in range(4):
                    sp.wait_ge(m["normed"], 4 * q + 4 + 1)
                    sp.dma_start(xr[4 * q:4 * q + 4, :, :].rearrange("t p d -> p t d"), rows_n[:, 4 * q:4 * q + 4, :]).then_inc(rows_out[q], 16)
                for r in range(DEPTH):
                    sp.wait_ge(scattered[r], scatters(l, ET // DEPTH))
                yr = ybuf[l][0:TOPK * B * S, :].rearrange("(t p k) d -> p t (k d)", p=P, k=TOPK)
                for q in range(4):
                    sp.dma_start(YB[:, 4 * q:4 * q + 4, :], yr[:, 4 * q:4 * q + 4, :]).then_inc(ms_back[l][q], 16)

            if last_stage == 0:
                sp.wait_ge(s0["residual"][0], 3 * B + 1)
            if last_stage >= 1:
                experts(0)
                if last_stage >= 3:
                    load_experts(1)
                sp.wait_ge(ms[0]["combined"], 1 + 1)
            if last_stage >= 2:
                sp.wait_ge(s1["residual"][0], (3 + 8) * B + 1)
            y = out.rearrange("(t p) d -> p t d", p=P)
            if last_stage >= 3:
                experts(1)
            for q in range(4):
                if last_stage >= 3:
                    sp.wait_ge(ms[1]["combined"], q + 1 + 1)
                sp.dma_start(y[:, 4 * q:4 * q + 4, :], X[:, 4 * q:4 * q + 4, :]).then_inc(stored, 16)
            sp.wait_ge(stored, 64)

        @block.gpsimd
        def _(pool):
            def own_wait():
                pool.nop(nofuse=True)

            def clear_keys(sm, parities):
                for r in parities:
                    for g in range(G):
                        pool.memset(keys[r][g].bitcast(F32), 0.0).then_inc(sm, 1)

            for r in range(2):
                pool.memset(vst[r][:], 0.0).then_inc(init_done, 1)
                pool.memset(mparts[r][:].bitcast(F32), 0.0).then_inc(init_done, 1)
            pool.memset(X[:, NT:NT + 2, :], 0.0).then_inc(init_done, 1)
            pool.wait_ge(init_done, 5)
            own_wait()
            for r in range(2):
                pool.memset(vst[r][:, :, :, HD:HD + 1], 1.0).then_inc(init_done, 1)
            clear_keys(init_done, (0, 1))
            pool.wait_ge(started, 4)
            own_wait()

            def mask_probs(b, g):
                wait(pool, "probs_done", b, 3 * g + 3)
                own_wait()
                for diag in (probs[g % 2][:, 0:4 * S].rearrange("p (j s) -> p j s", s=S)[:, :, 0:P],
                             probs[g % 2][:, 4 * S:].rearrange("p (j s) -> p j s", s=P)):
                    last = pool.affine_select(out=diag, in_=diag, compare_op=ALU.is_ge, fill=0.0, base=0,
                                              pattern=[[0, 4], [1, P]], channel_multiplier=-1)
                signal(last, "masked")

            with pool.Fori(0, B) as b:
                for g in range(G):
                    mask_probs(b, g)

            def expert_constants(l):
                pool.wait_ge(w_loaded[l], 16 * (8 if l == 0 else 4))
                own_wait()
                c = Chain(pool, moe_cast, 8 * l)
                if l == 0:
                    for n in range(2):
                        c.add(pool.tensor_copy(of_expert[:, n * FF:(n + 1) * FF], pqk[n][:]))
                c.add(pool.memset(bias3[l][:], 0.0))
                c.wait()
                own_wait()
                for ins in (lambda: pool.tensor_copy(bias3[l][0:E, :], bias[l][:]),
                            lambda: pool.tensor_tensor(bias_rest[:], bias[l][:], bias3[l][0:E, :], ALU.subtract),
                            lambda: pool.tensor_copy(bias_mid[:], bias_rest[:]),
                            lambda: pool.tensor_copy(bias3[l][32:32 + E, :], bias_mid[:]),
                            lambda: pool.tensor_tensor(bias3[l][64:64 + E, :], bias_rest[:], bias_mid[:], ALU.subtract)):
                    c(ins())
                    own_wait()

            def experts(l):
                m = ms[l]
                expert_constants(l)
                for r in range(DEPTH):
                    pool.dma_start(ybuf[l][TOPK * B * S + r * P:TOPK * B * S + (r + 1) * P, :], X[:, NT, :]).then_inc(scattered[r], 16)
                pool.wait_ge(m["tabled"], 6 + 1)
                own_wait()
                for q in range(4):
                    pool.wait_ge(rows_out[q], (32 if q < 2 else 16) * (l + 1))
                    own_wait()

                def gather(n, r):
                    pool.wait_ge(m["gidx"], n + 2)
                    own_wait()
                    pool.indirect_dma_start(out=xg[r][:], out_offset=None, in_=xbuf[l][:, :],
                                            in_offset=bass.IndirectOffsetOnAxis(ap=gidx[r][:], axis=0)).then_inc(gathered[r], 16)

                def scatter(n, r):
                    pool.wait_ge(m["sidx"], n + 2)
                    pool.wait_ge(m["y_copied"], n + 2)
                    own_wait()
                    pool.indirect_dma_start(out=ybuf[l][:, :], out_offset=bass.IndirectOffsetOnAxis(ap=sidx[r][:], axis=0),
                                            in_=yt[r][:], in_offset=None).then_inc(scattered[r], 16)

                def step(i, r, fetch=True):
                    n = DEPTH * i + r
                    if fetch:
                        pool.wait_ge(m["x_turned"], n + 2)
                        own_wait()
                        gather(n + DEPTH, r)
                    if r >= 2 or not first_turn(i):
                        scatter(n - 2, (r + 2) % DEPTH)
                for r in range(DEPTH):
                    gather(r, r)
                for r in range(DEPTH):
                    step(0, r)
                with pool.Fori(1, ET // DEPTH - 1) as i:
                    for r in range(DEPTH):
                        step(i, r)
                for r in range(DEPTH):
                    step(ET // DEPTH - 1, r, fetch=False)
                for r in range(2):
                    scatter(ET - 2 + r, (r + 2) % DEPTH)

            if last_stage >= 1:
                experts(0)
            if last_stage >= 2:
                pool.wait_ge(ms[0]["combined"], 1 + 1)
                own_wait()
                clear_keys(recleared, (0,))
                pool.wait_ge(ls["scores"], 1 + 1)
                own_wait()
                clear_keys(recleared, (1,))
                tables.append(s1)
                with pool.Fori(0, B) as b:
                    for g in range(G):
                        mask_probs(b, g)
                tables.pop()
            if last_stage >= 3:
                experts(1)

        @block.vector
        def _(dve):
            def inv_sqrt(y, v, t1, t2, eps, step, n0):
                n = n0

                def then(ins):
                    nonlocal n
                    n += 1
                    ins.then_inc(step, 1)
                    dve.wait_ge(step, n)
                then(dve.tensor_scalar(t1, v, eps, None, ALU.add))
                then(dve.tensor_scalar(y.bitcast(I32), t1.bitcast(I32), 1, None, ALU.logical_shift_right))
                then(dve.tensor_scalar(y.bitcast(I32), y.bitcast(I32), -1.0, float(MAGIC), ALU.mult, ALU.add))
                for _ in range(3):
                    then(dve.tensor_tensor(t2, y, y, ALU.mult))
                    then(dve.tensor_tensor(t2, t2, t1, ALU.mult))
                    then(dve.tensor_scalar(t2, t2, -0.5, 1.5, ALU.mult, ALU.add))
                    then(dve.tensor_tensor(y, y, t2, ALU.mult))
                return n

            dve.memset(mv[:, NT:NT + 2, :], 0.0).then_inc(stats_done, 1)
            dve.wait_ge(x_loaded, 64)
            for t in range(NT):
                dve.bn_stats(stats[:, t, :], X[:, t, :]).then_inc(stats_done, 1)
            dve.wait_ge(stats_done, NT + 1)
            for t in range(NT):
                dve.bn_aggr(mv[:, t, :], stats[:, t, :]).then_inc(stats_done, 1)
            dve.wait_ge(stats_done, 2 * NT + 1)
            inv_sqrt(rstd, mv[:, :, 1], nt1[:, 0, :], nt2[:, 0, :], LN_EPS, rstd_step, 0)

            def norm(b, b2, r):
                for t in range(2):
                    signal(dve.tensor_scalar(xn[r][:, t, :], X[:, ds(b2 + t, 1), :].rearrange("p a d -> p (a d)"),
                                             mv[:, ds(b2 + t, 1), 0:1].rearrange("p a s -> p (a s)"),
                                             rstd[:, ds(b2 + t, 1)], ALU.subtract, ALU.mult), "normed")

            def rotate(b, part):
                if part == 0:
                    wait(dve, "proj", b, 1)
                    wait(dve, "rope_step", b, 0)
                    signal(dve.tensor_tensor(rot[0][:], ps[:, BA, :], rope[:, 0, :], ALU.mult), "rope_step")
                if part == 1:
                    signal(dve.tensor_tensor(rot[1][:], ps[:, BB, :], rope[:, 1, :], ALU.mult), "rope_step")
                if part == 2:
                    wait(dve, "rope_step", b, 2)
                    signal(dve.tensor_tensor(rot[2][:], rot[0][:], rot[1][:], ALU.add), "rope_step")
                if part == 3:
                    wait(dve, "sel", b, 0)
                    wait(dve, "rope_step", b, 3)
                    signal(dve.tensor_copy(hi[:], rot[2][:]), "rope_step")
                    wait(dve, "rope_step", b, 4)
                    signal(dve.tensor_tensor(lo[:], rot[2][:], hi[:].bitcast(F32), ALU.subtract), "rope_step")

            def maximum(b, g, n):
                wait(dve, "p1", b, 3 * g + n + 1)
                if n == 0:
                    wait(dve, "msplit", b, 2 * (g - 1))
                    src = bank_of("max", g, n).rearrange("p (j s) -> p j s", s=P)
                    dst = negm[g % 2][:, 0, :]
                else:
                    src = bank_of("max", g, n).rearrange("p (j s) -> p j s", s=S)
                    dst = negm[g % 2][:, 1, 2 * n - 2:2 * n]
                signal(dve.tensor_reduce(dst, src, AX.X, ALU.max, negate=True), "maxed")

            def split_max(b, g):
                wait(dve, "maxed", b, 3 * g + 3)
                wait(dve, "mTr", b, g - 1)
                signal(dve.tensor_copy(mparts[g % 2][:, :, :, 3 * HD], negm[g % 2][:]), "msplit")
                wait(dve, "msplit", b, 2 * g + 1)
                signal(dve.tensor_tensor(mparts[g % 2][:, :, :, 3 * HD + 1], negm[g % 2][:], mparts[g % 2][:, :, :, 3 * HD].bitcast(F32), ALU.subtract), "msplit")

            def key_copies(b, r, n):
                wait(dve, "sel", b, 2 * n + 2)
                for g in (2 * n, 2 * n + 1):
                    for j in (2, 3):
                        rows_j = slice(32 * j, 32 * j + 32)
                        dst, src = keys[r][g][rows_j, j, :], ps[rows_j, BB, (g % 2) * S:(g % 2 + 1) * S]
                        if tables[-1] is s0:
                            ins = dve.tensor_scalar(dst, src, max_rows[rows_j], None, ALU.add)
                        else:
                            ins = dve.tensor_copy(dst, src)
                    signal(ins, "keyed_v")

            def add_max(b, r, g):
                wait(dve, "mTr", b, g + 1)
                wait(dve, "p2", b, 3 * (g - 1))
                signal(dve.tensor_tensor(qm[g % 2][:], qst[r][:, g, :].bitcast(F32), ps[:, BT, S:2 * S], ALU.add), "max_added")

            def reciprocals(b, g):
                wait(dve, "den", b, g + 1)
                wait(dve, "wide", b, g - 1)
                k = RDEN[len(tables) - 1]
                den = ps[:, BO, S:S + 8].rearrange("p (t j) -> p t j", j=4)
                if tables[-1] is s1:
                    wait(dve, "rden", b, k * g)
                    signal(dve.tensor_scalar(denq[:], den, RMS_EPS, None, ALU.add), "rden")
                    wait(dve, "rden", b, k * g + 1)
                    den = denq[:]
                wait(dve, "rden", b, k * g)
                signal(dve.reciprocal(rdenq[:], den), "rden")
                wait(dve, "rden", b, k * (g + 1) - 1)
                signal(dve.tensor_copy(rden[g % 2][:], rdenq[:].unsqueeze(3).broadcast_to((P, 2, 4, 32))), "rden")

            def divide(b, g):
                wait(dve, "wide", b, g + 1)
                if g == 0:
                    wait(dve, "outp", b, 0)
                signal(dve.tensor_tensor(on[:, g, :], o[g % 2][:, 0:S], ps[:, BO, S:2 * S], ALU.mult), "divided")

            def stats_of(b):
                wait(dve, "residual", b, STEPS_OF_RESIDUAL[len(tables) - 1])
                for t in range(2):
                    signal(dve.bn_stats(stats[:, ds(2 * b + t, 1), :].rearrange("p a s -> p (a s)"),
                                        X[:, ds(2 * b + t, 1), :].rearrange("p a d -> p (a d)")), "residual")

            def residual(b):
                wait(dve, "outp", b, 1)
                signal(dve.tensor_tensor(X[:, ds(2 * b, 2), :].rearrange("p a d -> p (a d)"),
                                         X[:, ds(2 * b, 2), :].rearrange("p a d -> p (a d)"), ps[:, BT, 0:2 * D], ALU.add), "residual")
                stats_of(b)

            STEPS_OF_RESIDUAL = (1, 6)
            dve.wait_ge(started, 4)
            norm(0, 0, 0)
            dve.wait_ge(loaded, 16 * NLOAD)
            dve.wait_ge(w_mm, 1)
            dve.tensor_copy(wq[:].rearrange("p a m -> p (a m)"), ps[:, BA, 0:2 * D]).then_inc(w_copied, 1)
            dve.tensor_copy(wkv[:], ps[:, BB, 0:2 * D + KVH * HD]).then_inc(w_copied, 1)
            for n in range(2):
                dve.tensor_copy(selr[:, 2 * n:2 * n + 2].rearrange("p a g m -> p (a g m)"), probs[n][:, 0:1024]).then_inc(consts_cast, 1)
            dve.tensor_copy(identb[:], misc[:, 0:P]).then_inc(consts_cast, 1)
            dve.tensor_copy(aboveb[:], misc[:, P:2 * P]).then_inc(consts_cast, 1)
            for part in range(4):
                rotate(0, part)
            key_copies(0, 0, 0)

            def step0(b, r, g, first=False, prep=True, tail=False):
                if g == 0 and prep:
                    norm(b + 1, 2 * b + 2, 1 - r)
                for n in range(3):
                    if not tail:
                        maximum(b, g, n)
                    if g == 2 and prep and n < 2:
                        rotate(b + 1, 1 + n)
                    if n == 0 and (g >= 3 if first else g < 3 if tail else True):
                        bb, _, gg = back(b, r, g - 3)
                        divide(bb, gg)
                if not tail:
                    split_max(b, g)
                    add_max(b, r, g)
                if g >= 2 if first else g < 2 if tail else True:
                    bb, _, gg = back(b, r, g - 2)
                    reciprocals(bb, gg)
                if g == 1 and prep:
                    rotate(b + 1, 0)
                if g == 2 and prep:
                    rotate(b + 1, 3)
                if g == 0 and not tail:
                    key_copies(b, r, 1)
                if g == 3 and prep:
                    key_copies(b + 1, 1 - r, 0)
                if g == 2 and not first:
                    residual(b - 1)
            all_steps(dve, step0, 3)
            dve.wait_ge(s0["residual"][0], 3 * B + 1)

            def experts(l, have):
                m = ms[l]
                for t in range(NT):
                    dve.bn_aggr(mv[:, t, :], stats[:, t, :]).then_inc(m["stats"], 1)
                dve.wait_ge(m["stats"], NT + 1)
                inv_sqrt(rstd, mv[:, :, 1], nt1[:, 0, :], nt2[:, 0, :], LN_EPS, m["rstd"], 1)

                for t in range(NT):
                    dve.tensor_scalar(rows_n[:, t, :], X[:, t, :], mv[:, t, 0:1], rstd[:, t:t + 1], ALU.subtract, ALU.mult).then_inc(m["normed"], 1)
                w = D + E if l == 0 else E
                for k in range(NT // 2):
                    dve.wait_ge(m["gated"], k + 2)
                    src = ps[:, 6 + k % 2, 0:2 * w].rearrange("p (t w) -> p t w", t=2)
                    two = slice(2 * k, 2 * k + 2)
                    if l == 0:
                        dve.tensor_tensor(SH[:, two, :], src[:, :, 0:D], shared_b.unsqueeze(1).broadcast_to((P, 2, D)), ALU.add).then_inc(m["logits"], 1)
                        dve.tensor_copy(LG[:, two, :], src[:, :, D:D + E]).then_inc(m["logits"], 1)
                    else:
                        dve.tensor_tensor(LG[:, two, :], src, gate_b.unsqueeze(1).broadcast_to((P, 2, E)), ALU.add).then_inc(m["logits"], 1)
                dve.wait_ge(m["logits"], (NT if l == 0 else NT // 2) + 1)

                c = Chain(dve, m["routed"], 1)
                wide = lambda a: a.unsqueeze(2).broadcast_to((P, NT, E))
                for n in range(2):
                    L = LG if n == 0 else LG2
                    c(dve.tensor_reduce(top[:, n, :], L[:], AX.X, ALU.max))
                    c(dve.tensor_tensor(rt[0][:], L[:], wide(top[:, n, :]), ALU.is_ge))
                    c(dve.tensor_tensor(rt[1][:], rt[0][:], rev_e.unsqueeze(1).broadcast_to((P, NT, E)), ALU.mult))
                    c(dve.tensor_reduce(top[:, 2, :], rt[1][:], AX.X, ALU.max))
                    c(dve.tensor_tensor(first[n][:], rt[1][:], wide(top[:, 2, :]), ALU.is_equal))
                    if n == 0:
                        c(dve.scalar_tensor_tensor(LG2[:], first[0][:], LOWEST, LG[:], ALU.mult, ALU.add))
                c(dve.tensor_tensor(picked[:], first[0][:], first[1][:], ALU.add))
                c(dve.tensor_tensor(wts[:, 0, :], top[:, 1, :], top[:, 0, :], ALU.subtract))
                ROUTED = c.n
                assert ROUTED == 14
                dve.wait_ge(m["counted"], 1 + 1)
                c(dve.tensor_copy(totals[:], ps[:, BT, P:2 * P].rearrange("p (t e) -> p e t", e=E)))
                flat = lambda a: a[:].rearrange("p e t -> p (e t)")
                c(dve.tensor_tensor_scan(flat(upto), ones_m, flat(totals), 0.0, ALU.mult, ALU.add))
                last = upto[:, :, NT - 1]
                cnt, til, cum, off = (per_e[:, n, :] for n in range(4))
                c(dve.tensor_copy(cnt, last))
                c(dve.tensor_tensor(per_e[:, 4, 1:E], last[:, 1:E], last[:, 0:E - 1], ALU.subtract))
                c(dve.tensor_copy(per_e[:, 4, 0:1], last[:, 0:1]))
                num = per_e[:, 4, :]
                c(dve.tensor_scalar(per_ei[:], num, float(P - 1), None, ALU.add))
                c(dve.tensor_scalar(per_ei[:], per_ei[:], P.bit_length() - 1, None, ALU.arith_shift_right))
                c(dve.tensor_copy(til, per_ei[:]))
                c(dve.tensor_tensor_scan(cum, ones_m[:, 0:E], til, 0.0, ALU.mult, ALU.add))
                c(dve.tensor_tensor(per_e[:, 5, :], cum, til, ALU.subtract))
                c(dve.tensor_tensor(per_e[:, 6, :], num, last, ALU.subtract))
                c(dve.scalar_tensor_tensor(off, per_e[:, 5, :], float(P), per_e[:, 6, :], ALU.mult, ALU.add))
                c(dve.tensor_tensor(flat(upto), flat(upto), flat(totals), ALU.subtract))
                c(dve.tensor_tensor(upto[:], upto[:], off.unsqueeze(2).broadcast_to((P, E, NT)), ALU.add))
                c(dve.tensor_tensor(rt[0][:], ps[:, BT, 0:P].rearrange("p (t e) -> p t e", e=E), upto[:].rearrange("p e t -> p t e"), ALU.add))
                for n in range(TOPK):
                    c(dve.tensor_tensor(rt[1][:], rt[0][:], first[n][:], ALU.mult))
                    c(dve.tensor_reduce(slot[:, :, n], rt[1][:], AX.X, ALU.add))
                c(dve.tensor_copy(sloti[:, 0, :], slot[:].rearrange("p t k -> p (t k)")))
                c(dve.tensor_scalar(sloti[:, 1, :], sloti[:, 0, :], P - 1, None, ALU.bitwise_and))
                c(dve.tensor_scalar(sloti[:, 2, :], sloti[:, 0, :], P.bit_length() - 1, None, ALU.arith_shift_right))
                c(dve.tensor_copy(slotf[:], sloti[:, 1:3, :]))
                c(dve.tensor_tensor(etab[:], iota_t.unsqueeze(2).broadcast_to((P, ETS, E)), cum.unsqueeze(1).broadcast_to((P, ETS, E)), ALU.is_ge))
                c(dve.tensor_reduce(eidf[:, 0, :], etab[:], AX.X, ALU.add))
                c(dve.tensor_scalar(eidf[:, 1, :], eidf[:, 0, :], float(E - 1), None, ALU.min))
                pairs = lambda a: a.unsqueeze(2).broadcast_to((P, NT * TOPK, ETS))
                c(dve.tensor_tensor(hotn, iota_t.unsqueeze(1).broadcast_to((P, NT * TOPK, ETS)), pairs(slotf[:, 1, :]), ALU.is_equal))
                c(dve.tensor_tensor(hotn, hotn, pairs(pair_no), ALU.mult))
                for n in range(NT * TOPK // HB):
                    if n >= 2:
                        dve.wait_ge(m["hot_used"], n)
                    dve.tensor_tensor(hot[n % 2], iota_p.unsqueeze(1).broadcast_to((P, HB, P)),
                                      slotf[:, 0, n * HB:(n + 1) * HB].unsqueeze(2).broadcast_to((P, HB, P)), ALU.is_equal).then_inc(m["hot"], 1)
                dve.wait_ge(m["inverse"], 1 + 1)
                c = Chain(dve, m["tabled"], 1)
                c(dve.tensor_copy(eid[:], eidf[:, 1, :]))
                c(dve.tensor_copy(inv[:, 0, :], ps[:, BA, 0:ETS]))
                c(dve.scalar_tensor_tensor(inv[:, 1, :], inv[:, 0, :], 0.0, spare_no, ALU.is_equal, ALU.mult))
                c(dve.scalar_tensor_tensor(inv[:, 2, :], inv[:, 0, :], -1.0, inv[:, 1, :], ALU.add, ALU.add))
                c(dve.tensor_copy(tab[:, 0, :], inv[:, 2, :]))
                c(dve.tensor_scalar(tab[:, 1, :], tab[:, 0, :], 1, None, ALU.arith_shift_right))

                c = Chain(dve, m["mixed"], 1)
                if l == 0:
                    dve.wait_ge(m["exp_diff"], 1 + 1)
                    c(dve.tensor_scalar(wts[:, 2, :], wts[:, 1, :], 1.0, None, ALU.add))
                    c(dve.reciprocal(wts[:, 3, :], wts[:, 2, :]))
                    c(dve.tensor_tensor(wts[:, 4, :], wts[:, 3, :], wts[:, 1, :], ALU.mult))

                def stage_gather(n, i, r):
                    if i is not None:
                        dve.wait_ge(gathered[r], gathers(l, i))
                    dve.tensor_copy(gidx[r][:], tab[:, 1, ds(n, 1)]).then_inc(m["gidx"], 1)

                def step(i, r, weights=True, fetch=True, store=True, ready=True):
                    n = DEPTH * i + r
                    if weights:
                        e = dve.value_load(eid[0:1, ds(n, 1)], min_val=0, max_val=E - 1)
                        if r >= 2 or not first_turn(i):
                            dve.wait_ge(m["h_active"], n - 2 + 2)
                        dve.tensor_copy(w1s[r % 2], w1[:, ds(e * W1, W1)]).then_inc(m["staged"], 1)
                    if fetch:
                        stage_gather(n + DEPTH + 1, i + (r + 1) // DEPTH + 1, (r + 1) % DEPTH)
                    if store:
                        q = (r + 3) % DEPTH
                        dve.wait_ge(scattered[q], scatters(l, i - (r < 1)))
                        dve.tensor_copy(sidx[q][:], tab[:, 0, ds(n - 1, 1)]).then_inc(m["sidx"], 1)
                    if ready:
                        q = (r + 2) % DEPTH
                        dve.wait_ge(m["y_ready"], n - 2 + 2)
                        dve.wait_ge(scattered[q], scatters(l, i - (r < 2)))
                        dve.tensor_copy(yt[q][:], ps[:, 6 + r % 2, 0:D]).then_inc(m["y_copied"], 1)
                for r in range(DEPTH):
                    stage_gather(r, None, r)
                stage_gather(DEPTH, 1, 0)
                if l == 0:
                    dve.wait_ge(m["gelu"], 1 + 1)
                    c(dve.tensor_scalar(SH[:], SH[:], 0.5, None, ALU.mult))
                    c(dve.tensor_tensor(X[:, 0:NT, :], X[:, 0:NT, :], beta.unsqueeze(1).broadcast_to((P, NT, D)), ALU.add))
                for r in range(DEPTH):
                    step(0, r, store=r >= 1, ready=r >= 2)
                with dve.Fori(1, ET // DEPTH - 1) as i:
                    for r in range(DEPTH):
                        step(i, r)
                for r in range(DEPTH):
                    step(ET // DEPTH - 1, r, fetch=False)
                for r in range(2):
                    step(ET // DEPTH, r, weights=False, fetch=False, store=r < 1)

                for q in range(4):
                    dve.wait_ge(ms_back[l][q], 16)
                    some = slice(4 * q, 4 * q + 4)
                    if l == 1:
                        dve.tensor_tensor(X[:, some, :], X[:, some, :], YB[:, some, 0:D], ALU.add).then_inc(m["mixed"], 1)
                        dve.wait_ge(m["mixed"], q + 1 + 1)
                        dve.tensor_tensor(X[:, some, :], X[:, some, :], YB[:, some, D:], ALU.add).then_inc(m["combined"], 1)
                        continue
                    for k in range(TOPK):
                        for t in range(4 * q, 4 * q + 4):
                            if k == 1:
                                dve.wait_ge(m["mixed"], c.n - 3)
                            c.add(dve.scalar_tensor_tensor(SH[:, t, :], YB[:, t, k * D:(k + 1) * D], wts[:, 3 + k, t:t + 1], SH[:, t, :], ALU.mult, ALU.add))
                if l == 1:
                    return
                def each(op):
                    for t in range(NT):
                        dve.wait_ge(m["mixed"], c.n - NT + 1)
                        c.add(op(t))
                c.wait()
                each(lambda t: dve.bn_stats(stats[:, t, :], SH[:, t, :]))
                each(lambda t: dve.bn_aggr(mv[:, t, :], stats[:, t, :]))
                c.wait()
                c.n = inv_sqrt(rstd, mv[:, :, 1], nt1[:, 0, :], nt2[:, 0, :], LN_EPS, m["mixed"], c.n)
                each(lambda t: dve.scalar_tensor_tensor(SH[:, t, :], SH[:, t, :], mv[:, t, 0:1], gamma, ALU.subtract, ALU.mult))
                each(lambda t: dve.scalar_tensor_tensor(X[:, t, :], SH[:, t, :], rstd[:, t:t + 1], X[:, t, :], ALU.mult, ALU.add))
                each(lambda t: dve.bn_stats(stats[:, t, :], X[:, t, :]))
                c.wait()
                dve.bn_aggr(mv[:, 0, :], stats[:, 0, :]).then_inc(m["combined"], 1)

            def look_up():
                for t in range(1, NT):
                    dve.bn_aggr(mv[:, t, :], stats[:, t, :]).then_inc(ls["stats"], 1)
                dve.wait_ge(ls["stats"], NT - 1 + 1)
                c = Chain(dve, ls["rstd"], 1)
                c(dve.tensor_scalar(var2[:, 0, :], mv[:, :, 1], LN_EPS, None, ALU.add))
                c(dve.reciprocal(var2[:, 1, :], var2[:, 0, :]))
                c(dve.tensor_tensor(var2[:, 1, :], var2[:, 1, :], mv[:, :, 1], ALU.mult))
                c(dve.tensor_scalar(var2[:, 1, :], var2[:, 1, :], RMS_EPS, None, ALU.add))
                c.n = inv_sqrt(rstd2[:], var2[:], nt1[:], nt2[:], 0.0, ls["rstd"], c.n)
                c(dve.tensor_tensor(rms[:], rstd2[:, 1, :], rstd, ALU.mult))
                dve.wait_ge(look_loaded, 64)
                dve.tensor_scalar(wqkv[:], w_look[:, 0:3, :], norm_w[:], None, ALU.mult).then_inc(ls["w_scaled"], 1)
                for t in range(NT):
                    dve.tensor_scalar(rows_n[:, t, :], X[:, t, :], mv[:, t, 0:1], rstd[:, t:t + 1], ALU.subtract, ALU.mult).then_inc(ls["normed"], 1)
                for k in range(NT // 2):
                    r = k % 2
                    dve.wait_ge(ls["u_copied"], k + 2)
                    dve.wait_ge(ls["means"], k + 2)
                    if k >= 2:
                        dve.wait_ge(ls["um"], 2 * (k - 1) + 1)
                    dve.tensor_tensor(um[r], usb[r], ps[:, 6 + r, 0:2 * D], ALU.mult).then_inc(ls["um"], 1)
                    dve.wait_ge(ls["um"], 2 * k + 2)
                    dve.tensor_reduce(SC[:, 2 * k:2 * k + 2, NC:NC + 1].rearrange("p a o -> p (a o)"), um[r].rearrange("p (t d) -> p t d", t=2), AX.X, ALU.add).then_inc(ls["um"], 1)
                dve.wait_ge(ls["scores"], 1 + 1)
                dve.tensor_tensor(SC[:, :, 0:NC].rearrange("p (s t) n -> p s t n", t=2),
                                  ps[:, 3, B * NC:B * NC + NT * NC].rearrange("p (s t n) -> p s t n", t=2, n=NC),
                                  unseen.rearrange("p (t n) -> p t n", t=2).unsqueeze(1).broadcast_to((P, B, 2, NC)), ALU.add).then_inc(ls["gate_in"], 1)
                dve.wait_ge(ls["um"], NT + 1)
                dve.wait_ge(ls["gate_in"], 1 + 1)
                c = Chain(dve, ls["soft"], 1)
                wide = lambda a: a.unsqueeze(2).broadcast_to((P, NT, NC + 1))
                c(dve.tensor_reduce(sct[:, 0, :], SC[:], AX.X, ALU.max))
                c(dve.tensor_tensor(SCd[:], SC[:], wide(sct[:, 0, :]), ALU.subtract))
                dve.wait_ge(ls["soft_exp"], 1 + 1)
                c(dve.tensor_reduce(sct[:, 1, :], SC[:], AX.X, ALU.add))
                c(dve.reciprocal(sct[:, 2, :], sct[:, 1, :]))
                c(dve.tensor_tensor(GT[:, 0:NT, :], SC[:], wide(sct[:, 2, :]), ALU.mult))

            def norm1(b, b2, r):
                for t in range(2):
                    signal(dve.tensor_scalar(xn[r][:, t, :], X[:, ds(b2 + t, 1), :].rearrange("p a d -> p (a d)"),
                                             mv[:, ds(b2 + t, 1), 0:1].rearrange("p a s -> p (a s)"),
                                             rms[:, ds(b2 + t, 1)], ALU.subtract, ALU.mult), "normed")

            def elu(b, r):
                wait(dve, "proj", b, 1)
                wait(dve, "sel", b, 0)
                wait(dve, "elu_step", b, 0)
                signal(dve.tensor_scalar(rot[0][:], ps[:, BA, :], 0.0, None, ALU.min), "elu_step")

            def elu2(b, r):
                wait(dve, "elu_exp", b, 1)
                signal(dve.scalar_tensor_tensor(pqk[r][:], ps[:, BA, :], 0.0, rot[1][:], ALU.max, ALU.add), "elu_step")

            def split(b, r):
                wait(dve, "elu_step", b, 2)
                signal(dve.tensor_copy(hi[:], pqk[r][:]), "elu_step")
                wait(dve, "elu_step", b, 3)
                signal(dve.tensor_tensor(lo[:], pqk[r][:], hi[:].bitcast(F32), ALU.subtract), "elu_step")

            def own_states(b):
                for n, c in ((0, 4), (1, NS - 4)):
                    wait(dve, "state", b, n + 1)
                    wait(dve, "looked", b, 0)
                    signal(dve.tensor_tensor(states[:, 4 * n:4 * n + c, :], bank_of("state", 0, n)[:, 0:c * D].rearrange("p (n d) -> p n d", d=D),
                                             own_head.unsqueeze(1).broadcast_to((P, c, D)), ALU.mult), "state_own")

            def retrieve(b, r, look):
                if look == 0:
                    wait(dve, "residual", b - 1, 0)
                wait(dve, "looked", b, look + 1)
                t, c, at = LOOKS[look]
                for n in range(c):
                    gate = GT[:, ds(2 * b + t, 1), at + n:at + n + 1].rearrange("p a n -> p (a n)")
                    src = look_bank(look)[:, n * D:(n + 1) * D]
                    if at + n == 0:
                        signal(dve.tensor_scalar(found[r][:, t, :], src, gate, None, ALU.mult), "found")
                    else:
                        wait(dve, "found", b, LOOKED[look] - c + n)
                        signal(dve.scalar_tensor_tensor(found[r][:, t, :], src, gate, found[r][:, t, :], ALU.mult, ALU.add), "found")

            def residual1(b, r):
                b2 = 2 * b
                wait(dve, "residual", b, 0)
                for t in range(2):
                    signal(dve.tensor_scalar(zt[:, t, :], X[:, ds(b2 + t, 1), :].rearrange("p a d -> p (a d)"),
                                             mv[:, ds(b2 + t, 1), 0:1].rearrange("p a s -> p (a s)"),
                                             rstd[:, ds(b2 + t, 1)], ALU.subtract, ALU.mult), "residual")

            def residual2(b, r):
                b2 = 2 * b
                wait(dve, "outp", b, 1)
                wait(dve, "residual", b, 2)
                flat = lambda a: a[:].rearrange("p t d -> p (t d)")
                signal(dve.tensor_tensor(flat(zt), flat(zt), ps[:, BT, 0:2 * D], ALU.add), "residual")
                wait(dve, "residual", b, 3)
                wait(dve, "found", b, 10)
                for t in range(2):
                    gate = GT[:, ds(b2 + t, 1), NC:NC + 1].rearrange("p a n -> p (a n)")
                    signal(dve.scalar_tensor_tensor(zt[:, t, :], zt[:, t, :], gate, found[r][:, t, :], ALU.mult, ALU.add), "residual")
                wait(dve, "residual", b, 5)
                signal(dve.tensor_tensor(X[:, ds(b2, 2), :], X[:, ds(b2, 2), :], zt[:], ALU.add), "residual")
                stats_of(b)

            if last_stage >= 1:
                experts(0, 0)
            if last_stage >= 2:
                dve.wait_ge(ms[0]["combined"], 1 + 1)
                look_up()
                tables.append(s1)
                norm1(0, 0, 0)
                elu(0, 0)
                elu2(0, 0)
                split(0, 0)
                key_copies(0, 0, 0)

                def step1(b, r, g, first=False, prep=True, tail=False):
                    if g == 0 and prep:
                        norm1(b + 1, 2 * b + 2, 1 - r)
                    if g >= 2 if first else True:
                        bb, _, gg = back(b, r, g - 2)
                        reciprocals(bb, gg)
                    if g == 0 and not tail:
                        own_states(b)
                    if g == 3 and prep:
                        split(b + 1, 1 - r)
                    if g >= 2 if first else True:
                        divide(bb, gg)
                    if g == 2 and not tail:
                        retrieve(b, r, 0)
                    if g == 0 and not tail:
                        key_copies(b, r, 1)
                    if g == 1 and not first:
                        residual1(b - 1, 1 - r)
                    if g == 1 and prep:
                        elu(b + 1, 1 - r)
                    if g == 1 and not first:
                        residual2(b - 1, 1 - r)
                    if g == 2 and prep:
                        elu2(b + 1, 1 - r)
                    if g == 3 and not tail:
                        retrieve(b, r, 1)
                    if g == 3 and prep:
                        key_copies(b + 1, 1 - r, 0)
                    if g == 3 and not tail:
                        retrieve(b, r, 2)
                all_steps(dve, step1, 2)
                tables.pop()
                dve.wait_ge(s1["residual"][0], (3 + 8) * B + 1)
            if last_stage >= 3:
                experts(1, 0)

        @block.scalar
        def _(act):
            def copy_xT(b, r):
                wait(act, "xT", b, 1)
                signal(act.activation(xnT[r][:], ps[:, BT, 0:S], ACT.Copy), "xT_copied")

            def copy_v(b, r):
                wait(act, "proj", b, 1)
                signal(act.activation(vst[r][:, :, 0:KVH, 0:HD], ps[:, BT, 0:2 * KVH * HD].rearrange("p (t h d) -> p t h d", t=2, d=HD), ACT.Copy), "v_copied")

            def stack(b, r, n):
                wait(act, "sel", b, 2 * n + 1)
                act_dst = qst[r][:, 2 * n:2 * n + 2, :].rearrange("p g s -> p (g s)")
                signal(act.activation(act_dst, ps[:, BA, :], ACT.Copy), "stacked")

            def key_copies(b, r, n):
                wait(act, "sel", b, 2 * n + 2)
                for g in (2 * n, 2 * n + 1):
                    for j in range(2):
                        rows_j = slice(32 * j, 32 * j + 32)
                        dst, src = keys[r][g][rows_j, j, :], ps[rows_j, BB, (g % 2) * S:(g % 2 + 1) * S]
                        if tables[-1] is s0:
                            ins = act.activation(dst, src, ACT.Identity, bias=max_rows[rows_j])
                        else:
                            ins = act.activation(dst, src, ACT.Copy)
                    signal(ins, "keyed")

            def exps(b, g):
                for n in range(3):
                    wait(act, "p2", b, 3 * g + n + 1)
                    if n == 0:
                        wait(act, "pv", b, g - 1)
                    kind, scale = (ACT.Exp, QK_SCALE) if tables[-1] is s0 else (ACT.Copy, 1.0)
                    signal(act.activation(probs[g % 2][:, 512 * n:512 * (n + 1)], bank_of("prob", g, n), kind, scale=scale), "probs_done")

            def copy_o(b, g):
                wait(act, "pv", b, g + 1)
                wait(act, "divided", b, g - 1)
                signal(act.activation(o[g % 2][:, 0:S], ps[:, BO, 0:S], ACT.Copy), "o_copied")

            act.wait_ge(started, 4)
            act.wait_ge(init_done, NINIT)
            act.activation(wmeans[:, 0:1], X[:, NT, 0:1], ACT.Exp).then_inc(exp_ready, 1)
            act.wait_ge(exp_ready, 1)
            copy_xT(0, 0)
            copy_v(0, 0)
            stack(0, 0, 0)
            key_copies(0, 0, 0)

            def step0(b, r, g, first=False, prep=True, tail=False):
                if not (first and g == 0) and not (tail and g > 0):
                    bb, _, gg = back(b, r, g - 1)
                    exps(bb, gg)
                if g == 0 and prep:
                    copy_xT(b + 1, 1 - r)
                if g >= 2 if first else g < 2 if tail else True:
                    bb, _, gg = back(b, r, g - 2)
                    copy_o(bb, gg)
                if g == 1 and prep:
                    copy_v(b + 1, 1 - r)
                if g == 0 and not tail:
                    stack(b, r, 1)
                    key_copies(b, r, 1)
                if g == 3 and prep:
                    stack(b + 1, 1 - r, 0)
                    key_copies(b + 1, 1 - r, 0)
            all_steps(act, step0, 2)

            def experts(l):
                m = ms[l]
                for k in range(NT // 2):
                    act.wait_ge(m["xT"], k + 2)
                    if k >= 2:
                        act.wait_ge(m["gated"], k)
                    act.activation(xnT[k % 2][:], ps[:, BT + k % 2, 0:S], ACT.Copy).then_inc(m["xT_copied"], 1)
                if l == 0:
                    act.wait_ge(m["routed"], 13 + 1)
                    act.activation(wts[:, 1, :], wts[:, 0, :], ACT.Exp).then_inc(m["exp_diff"], 1)
                    act.wait_ge(m["logits"], NT + 1)
                    act.activation(SH[:], SH[:], ACT.Gelu).then_inc(m["gelu"], 1)

                def step(i, r, turned=True, hidden=True):
                    n = DEPTH * i + r
                    if turned:
                        act.wait_ge(m["x_turned"], n + 2)
                        act.activation(xgT[r % 2][:], ps[:, 4 + r % 2, 0:P], ACT.Copy).then_inc(m["x_copied"], 1)
                    if hidden:
                        q = (r + 1) % 2
                        act.wait_ge(m["h_ready"], n - 1 + 2)
                        if r >= 3 or not first_turn(i):
                            act.wait_ge(m["y_ready"], n - 3 + 2)
                        for c in range(FC):
                            ins = act.activation(hidT[q][:, c * P:(c + 1) * P], ps[:, q, c * P:(c + 1) * P],
                                                 ACT.Gelu if l == 0 else ACT.Relu, bias=w1s[q][:, FF + c:FF + c + 1])
                        ins.then_inc(m["h_active"], 1)
                for r in range(DEPTH):
                    step(0, r, True, r >= 1)
                with act.Fori(1, ET // DEPTH) as i:
                    for r in range(DEPTH):
                        step(i, r)
                step(ET // DEPTH, 0, False, True)

            def look_up():
                for k in range(NT // 2 + 1):
                    if k < NT // 2:
                        act.wait_ge(ls["zT"], k + 2)
                        act.activation(turned[:, 2 * k:2 * k + 2, :].rearrange("p t d -> p (t d)"), ps[:, BT + k % 2, 0:S], ACT.Copy).then_inc(ls["zT_copied"], 1)
                    if k >= 1:
                        j = k - 1
                        act.wait_ge(ls["means"], j + 2)
                        if j >= 2:
                            act.wait_ge(ls["um"], 2 * (j - 2) + 1 + 1)
                        act.activation(usb[j % 2], ps[:, j % 2, 0:2 * D], ACT.Copy).then_inc(ls["u_copied"], 1)
                act.activation(means[:], ps[:, 2, 0:B * NC], ACT.Copy).then_inc(ls["means_copied"], 1)
                act.wait_ge(ls["wmeans"], 1 + 1)
                act.activation(wmeans[:], ps[:, 3, 0:B * NC], ACT.Copy).then_inc(ls["wmeans_copied"], 1)
                act.wait_ge(ls["soft"], 2 + 1)
                act.activation(SC[:], SCd[:], ACT.Exp, scale=float(D) ** -0.5).then_inc(ls["soft_exp"], 1)

            def elu_exp(b):
                wait(act, "elu_step", b, 1)
                signal(act.activation(rot[1][:], rot[0][:], ACT.Exp), "elu_exp")

            def copy_v1(b, r):
                wait(act, "proj", b, 1)
                signal(act.activation(vst[r][:, :, :, 0:HD], ps[:, BT, 0:S].rearrange("p (t h d) -> p t h d", t=2, d=HD), ACT.Copy), "v_copied")

            def copy_pk(b, r):
                wait(act, "pkT", b, 1)
                signal(act.activation(pkt[r][:].rearrange("p t d -> p (t d)"), ps[:, BB, 0:2 * D], ACT.Copy), "pk_copied")

            if last_stage >= 1:
                experts(0)
            if last_stage >= 2:
                look_up()
                tables.append(s1)
                act.wait_ge(recleared, 2 * G)
                copy_xT(0, 0)
                elu_exp(0)
                copy_v1(0, 0)
                copy_pk(0, 0)
                stack(0, 0, 0)
                key_copies(0, 0, 0)

                def step1(b, r, g, first=False, prep=True, tail=False):
                    if not tail:
                        exps(b, g)
                    if g == 0 and prep:
                        copy_xT(b + 1, 1 - r)
                    if g == 2 and prep:
                        elu_exp(b + 1)
                    if g == 3 and prep:
                        copy_pk(b + 1, 1 - r)
                    if g == 0 and not tail:
                        stack(b, r, 1)
                        key_copies(b, r, 1)
                    if g == 3 and prep:
                        stack(b + 1, 1 - r, 0)
                        key_copies(b + 1, 1 - r, 0)
                    if g == 1 and prep:
                        copy_v1(b + 1, 1 - r)
                    if not (first and g == 0):
                        bb, _, gg = back(b, r, g - 1)
                        copy_o(bb, gg)
                all_steps(act, step1, 1)
                tables.pop()
            if last_stage >= 3:
                experts(1)

        @block.tensor
        def _(pe):
            pe.wait_ge(started, 4)
            pe.wait_ge(loaded, 16 * NLOAD)
            pe.matmul(ps[:, BA, 0:2 * D], wqa_t[:], wqb[:], start=True, stop=True)
            pe.matmul(ps[:, BB, 0:2 * D + KVH * HD], wkva_t[:], wkvb[:], start=True, stop=True).then_inc(w_mm, 1)
            pe.wait_ge(init_done, NINIT)

            def residual_read(b):
                wait(pe, "residual", b, RESIDUAL_READ[len(tables) - 1])

            def turn_x(b, r):
                wait(pe, "normed", b, 2)
                wait(pe, "v_copied", b, 0)
                if tables[-1] is s0:
                    wait(pe, "max_added", b, -G)
                for t in range(2):
                    mm = pe.transpose(ps[:, BT, t * P:(t + 1) * P], xn[r][:, t, :], ident)
                signal(mm, "xT")

            def project_qk(b, r):
                wait(pe, "xT_copied", b, 1)
                wait(pe, "stacked", b, 0)
                wait(pe, "keyed", b, 0)
                wait(pe, "keyed_v", b, 0)
                pe.matmul(ps[:, BA, 0:S], wq[:, 0, :], xnT[r][:], start=True, stop=True)
                pe.matmul(ps[:, BA, S:2 * S], wkv[:, 0:D], xnT[r][:], start=True, stop=True)
                pe.matmul(ps[:, BB, 0:S], wq[:, 1, :], xnT[r][:], start=True, stop=True)
                pe.matmul(ps[:, BB, S:2 * S], wkv[:, D:2 * D], xnT[r][:], start=True, stop=True)

            def project_v(b, r):
                wait(pe, "max_added", b, 2 - G)
                for t in range(2):
                    c = t * KVH * HD
                    mm = pe.matmul(ps[:, BT, c:c + KVH * HD], xnT[r][:, t * P:(t + 1) * P], wkv[:, 2 * D:], start=True, stop=True)
                signal(mm, "proj")

            def spread(b, n):
                if tables[-1] is s0:
                    wait(pe, "rope_step", b, 5)
                else:
                    wait(pe, "elu_step", b, 4)
                    wait(pe, "pk_copied", b, 1)
                if n == 2:
                    wait(pe, "stacked", b, 1)
                if n == 3:
                    wait(pe, "keyed", b, 2)
                    wait(pe, "keyed_v", b, 2)
                c, w = (0, 0) if n % 2 == 0 else (S, 2)
                for gg in range(2):
                    g = 2 * (n // 2) + gg
                    dst = ps[:, BA + n % 2, gg * S:(gg + 1) * S]
                    pe.matmul(dst, selr[:, w, g, :], hi[:, c:c + S], start=True, stop=False)
                    mm = pe.matmul(dst, selr[:, w + 1, g, :], lo[:, c:c + S], start=False, stop=True)
                signal(mm, "sel")

            def ring(b, kind, g, n):
                R = rings[len(tables) - 1]
                at = ring_at(kind, g, n)
                at -= 4
                while R[at][0] == "none":
                    at -= 4
                pk, pg, pn = R[at]
                bb = b if at >= 0 else b - 1
                if tables[-1] is s0 and pk == "prob":
                    bb, _, pg = back(bb, 0, pg - 1)
                if pk == "max":
                    wait(pe, "maxed", bb, 3 * pg + pn + 1)
                elif pk == "prob":
                    wait(pe, "probs_done", bb, 3 * pg + pn + 1)
                elif pk == "look":
                    wait(pe, "found", bb, LOOKED[pn])
                else:
                    wait(pe, "state_own", bb, pn + 1)
                return bank_of(kind, g, n)

            def max_scores(b, r, g, n):
                bank = ring(b, "max", g, n)
                wide = lambda h: aboveb[:].unsqueeze(1).broadcast_to((P, h, P))
                if n == 0:
                    pe.matmul(bank, qst[r][:, g, 0:P], keys[r][g][:, :, 0:P], start=True, stop=False)
                    mm = pe.matmul(bank, identb[:], wide(4), start=False, stop=True)
                else:
                    pe.matmul(bank, qst[r][:, g, P:S], keys[r][g][:, 2 * n - 2:2 * n, :], start=True, stop=False)
                    mm = pe.matmul(bank.rearrange("p (j s) -> p j s", s=S)[:, :, P:S], identb[:], wide(2), start=False, stop=True)
                signal(mm, "p1")

            def keys_ready(b, g):
                wait(pe, "stacked", b, 1 + g // 2)
                wait(pe, "keyed", b, 1 + g)
                wait(pe, "keyed_v", b, 1 + g)

            def turn_max(b, g, prep):
                wait(pe, "msplit", b, 2 * g + 2)
                wait(pe, "max_added", b, g)
                if g < 2 and prep:
                    wait(pe, "xT_copied", b + 1, 1)
                if g == 2 and prep:
                    wait(pe, "v_copied", b + 1, 1)
                if g == 3:
                    residual_read(b - 1)
                for t in range(2):
                    mm = pe.transpose(ps[:, BT, S + t * P:S + (t + 1) * P], mparts[g % 2][:, t].rearrange("p j m -> p (j m)").bitcast(F32), ident)
                signal(mm, "mTr")

            def prob_scores(b, r, g, n, bring):
                bank = ring(bring, "prob", g, n)
                if tables[-1] is s0:
                    wait(pe, "max_added", b, g + 1)
                for c in range(2 if n < 2 else 4):
                    j, k, q = (2 * n + c, slice(0, P), slice(0, S)) if n < 2 else (c, slice(P, S), slice(P, S))
                    w = q.stop - q.start
                    dst = bank[:, c * w:(c + 1) * w]
                    src = qm[g % 2][:, q] if tables[-1] is s0 else qst[r][:, g, q]
                    mm = pe.matmul(dst, keys[r][g][:, j, k], src, start=True, stop=True)
                signal(mm, "p2")

            def weigh(b, r, g):
                wait(pe, "masked", b, g + 1)
                if g == 0:
                    wait(pe, "v_copied", b, 1)
                wait(pe, "divided", b, g)
                first = lambda j: probs[g % 2][:, j * S:(j + 1) * S]
                second = lambda j: probs[g % 2][:, 4 * S + j * P:4 * S + (j + 1) * P]
                values = lambda t, j: vst[r][:, t, g if tables[-1] is s0 else 4 * g + j, :]
                for j in range(4):
                    pe.matmul(ps[32 * j:32 * j + 32, BO, 0:S], values(0, j), first(j), start=True, stop=False)
                for j in range(4):
                    mm = pe.matmul(ps[32 * j:32 * j + 32, BO, P:S], values(1, j), second(j), start=False, stop=True)
                signal(mm, "pv")

            def turn_den(b, g):
                wait(pe, "o_copied", b, g + 1)
                for t in range(2):
                    mm = pe.matmul(ps[:, BO, S + 4 * t:S + 4 * t + 4], o[g % 2][:, t * P:(t + 1) * P], weight_row, start=True, stop=True)
                signal(mm, "den")

            def widen(b, g):
                wait(pe, "rden", b, RDEN[len(tables) - 1] * (g + 1))
                for t in range(2):
                    mm = pe.matmul(ps[:, BO, S + t * P:S + (t + 1) * P], rden[g % 2][:, t].rearrange("p j m -> p (j m)"), ident, start=True, stop=True)
                signal(mm, "wide")

            def give_out(b, prep, tail):
                if tables[-1] is s0:
                    wait(pe, "max_added", b + 1, 0 if tail else 3)
                wait(pe, "divided", b, G)
                if tables[-1] is s0:
                    wait(pe, "v_copied", b + 1, 2 if prep else 0 if tail else 1)
                elif prep:
                    wait(pe, "v_copied", b + 1, 2)
                elif tail:
                    residual_read(b - 1)
                w = wout if tables[-1] is s0 else wo
                for t in range(2):
                    for g in range(G):
                        mm = pe.matmul(ps[:, BT, t * P:(t + 1) * P], on[:, g, t * P:(t + 1) * P], w[:, g, :], start=(g == 0), stop=(g == G - 1))
                signal(mm, "outp")

            turn_x(0, 0)
            pe.wait_ge(w_copied, 2)
            project_qk(0, 0)
            project_v(0, 0)
            pe.wait_ge(consts_cast, 4)
            for n in range(2):
                spread(0, n)

            def step0(b, r, g, first=False, prep=True, tail=False):
                for at, (kind, n) in enumerate(ORDER0[g % G]):
                    if at == 2 and (g >= 3 if first else g < 3 if tail else True):
                        bb, _, gg = back(b, r, g - 3)
                        widen(bb, gg)
                    if kind == "prob" and not (first and g == 0) and not (tail and g > 0):
                        bb, rr, gg = back(b, r, g - 1)
                        prob_scores(bb, rr, gg, n, b)
                    if kind == "max" and not tail:
                        if n == 0:
                            keys_ready(b, g)
                        max_scores(b, r, g, n)
                if g == 0 and prep:
                    turn_x(b + 1, 1 - r)
                if g == 1 and prep:
                    project_qk(b + 1, 1 - r)
                if g == 0 and not tail:
                    spread(b, 2)
                    spread(b, 3)
                if g == 3 and prep:
                    spread(b + 1, 0)
                    spread(b + 1, 1)
                if g >= 2 if first else g < 2 if tail else True:
                    weigh(*back(b, r, g - 2))
                if not tail:
                    turn_max(b, g, prep)
                if g >= 2 if first else g < 2 if tail else True:
                    bb, _, gg = back(b, r, g - 2)
                    turn_den(bb, gg)
                if g == 1 and prep:
                    project_v(b + 1, 1 - r)
                if g == 2 and not first:
                    give_out(b - 1, prep, tail)
            all_steps(pe, step0, 3)

            def experts(l):
                m = ms[l]
                pe.wait_ge(w_loaded[l], 16 * (8 if l == 0 else 4))

                w = D + E if l == 0 else E
                per = 2 if l == 0 else 1
                for k in range(NT // 2 + 1):
                    if k < NT // 2:
                        pe.wait_ge(m["normed"], 2 * k + 2 + 1)
                        if k >= 2:
                            pe.wait_ge(m["xT_copied"], k)
                        for t in range(2):
                            mm = pe.transpose(ps[:, BT + k % 2, t * P:(t + 1) * P], rows_n[:, 2 * k + t, :], ident)
                        mm.then_inc(m["xT"], 1)
                    if k >= 1:
                        j = k - 1
                        pe.wait_ge(m["xT_copied"], j + 2)
                        if j >= 2:
                            pe.wait_ge(m["logits"], (j - 1) * per + 1)
                        for t in range(2):
                            mm = pe.matmul(ps[:, 6 + j % 2, t * w:(t + 1) * w], xnT[j % 2][:, t * P:(t + 1) * P], gates[l][:], start=True, stop=True)
                        mm.then_inc(m["gated"], 1)
                pe.wait_ge(m["routed"], 13 + 1)
                picks = picked[:].rearrange("p t e -> p (t e)")
                pe.matmul(ps[:, BT, 0:P], before_m, picks, start=True, stop=True)
                pe.matmul(ps[:, BT, P:2 * P], ones_m, picks, start=True, stop=True).then_inc(m["counted"], 1)
                for q in range(NT * TOPK):
                    if q % HB == 0:
                        pe.wait_ge(m["hot"], q // HB + 2)
                    mm = pe.matmul(ps[:, BA, 0:ETS], hot[q // HB % 2][:, q % HB, :], hotn[:, q, :], start=(q == 0), stop=(q == NT * TOPK - 1))
                    if q % HB == HB - 1:
                        mm.then_inc(m["inverse"] if q == NT * TOPK - 1 else m["hot_used"], 1)
                pe.wait_ge(m["tabled"], 6 + 1)
                pe.wait_ge(moe_cast, 7 + 6 * l)

                def turn_rows(n, i, r):
                    pe.wait_ge(gathered[r], gathers(l, i + 1))
                    pe.transpose(ps[:, 4 + r % 2, 0:P], xg[r][:], ident).then_inc(m["x_turned"], 1)

                def into_hidden(n, r):
                    pe.wait_ge(m["x_copied"], n + 2)
                    pe.wait_ge(m["staged"], n + 2)
                    for c in range(FC):
                        mm = pe.matmul(ps[:, r % 2, c * P:(c + 1) * P], w1s[r % 2][:, c * P:(c + 1) * P], xgT[r % 2][:], start=True, stop=True)
                    mm.then_inc(m["h_ready"], 1)

                def out_of_hidden(n, r, e, first):
                    if not first:
                        pe.wait_ge(m["y_copied"], n - 2 + 2)
                    pe.matmul(ps[:, 6 + r % 2, 0:D], of_expert[:, ds(e * P, P)], bias3[l][:], start=True, stop=False)
                    pe.wait_ge(m["h_active"], n + 2)
                    for c in range(FC):
                        mm = pe.matmul(ps[:, 6 + r % 2, 0:D], hidT[r % 2][:, c * P:(c + 1) * P], w2[:, ds(e * FF + c * D, D)], start=False, stop=(c == FC - 1))
                    mm.then_inc(m["y_ready"], 1)

                def step(i, r, a=True, b=True, c=True):
                    n = DEPTH * i + r
                    if c:
                        e = pe.value_load(eid[0:1, ds(n - 2, 1)], min_val=0, max_val=E - 1)
                    if a:
                        turn_rows(n, i, r)
                    if b:
                        into_hidden(n - 1, r + 3)
                    if c:
                        out_of_hidden(n - 2, r + 2, e, first_turn(i))
                for r in range(DEPTH):
                    step(0, r, True, r >= 1, r >= 2)
                with pe.Fori(1, ET // DEPTH) as i:
                    for r in range(DEPTH):
                        step(i, r)
                for r in range(2):
                    step(ET // DEPTH, r, False, r < 1, True)

            def look_up():
                pe.wait_ge(look_loaded, 64)
                for k in range(NT // 2 + 1):
                    if k < NT // 2:
                        pe.wait_ge(ls["normed"], 2 * k + 2 + 1)
                        if k >= 2:
                            pe.wait_ge(ls["zT_copied"], k)
                        for t in range(2):
                            mm = pe.transpose(ps[:, BT + k % 2, t * P:(t + 1) * P], rows_n[:, 2 * k + t, :], ident)
                        mm.then_inc(ls["zT"], 1)
                    if k >= 1:
                        j = k - 1
                        r = j % 2
                        pe.wait_ge(ls["zT_copied"], j + 2)
                        if j >= 2:
                            pe.wait_ge(ls["u_copied"], j)
                            pe.wait_ge(ls["um"], 2 * (j - 2) + 1 + 1)
                        pe.matmul(ps[:, 6 + r, 0:2 * D], running, rows_n[:, 2 * j:2 * j + 2, :], start=True, stop=True)
                        for t in range(2):
                            pe.matmul(ps[:, r, t * D:(t + 1) * D], turned[:, 2 * j + t, :], w_look[:, 3, :], start=True, stop=True)
                            mm = pe.matmul(ps[:, 2, 4 * (2 * j + t):4 * (2 * j + t) + 4], rows_n[:, 2 * j + t, :], chunk_mean, start=True, stop=True)
                        mm.then_inc(ls["means"], 1)
                pe.wait_ge(ls["means_copied"], 1 + 1)
                pe.matmul(ps[:, 3, 0:B * NC], w_look[:, 4, :], means[:], start=True, stop=True).then_inc(ls["wmeans"], 1)
                pe.wait_ge(ls["wmeans_copied"], 1 + 1)
                for t in range(NT):
                    mm = pe.matmul(ps[:, 3, (B + t) * NC:(B + t + 1) * NC], turned[:, t, :], wmeans[:, (t // 2) * NC:(t // 2 + 1) * NC], start=True, stop=True)
                mm.then_inc(ls["scores"], 1)

            def project1_qk(b, r):
                wait(pe, "xT_copied", b, 1)
                wait(pe, "stacked", b, 0)
                for n in range(2):
                    pe.matmul(ps[:, BA, n * S:(n + 1) * S], wqkv[:, n, :], xnT[r][:], start=True, stop=True)

            def project1_v(b, r):
                for t in range(2):
                    mm = pe.matmul(ps[:, BT, t * D:(t + 1) * D], xnT[r][:, t * P:(t + 1) * P], wqkv[:, 2, :], start=True, stop=True)
                signal(mm, "proj")

            def turn_keys(b, r):
                wait(pe, "elu_step", b, 2)
                for t in range(2):
                    mm = pe.transpose(ps[:, BB, t * D:(t + 1) * D], pqk[r][:, S + t * P:S + (t + 1) * P], ident)
                signal(mm, "pkT")

            def chunk_states(b, r):
                wait(pe, "pk_copied", b, 1)
                wait(pe, "v_copied", b, 1)
                banks = [ring(b, "state", 0, n) for n in range(2)]
                for n in range(NS):
                    rows_n = SEG * (n % 4 + 1)
                    dst = banks[n // 4][:, (n % 4) * D:(n % 4 + 1) * D].rearrange("p (h d) -> p h d", d=HD)
                    if n >= 4:
                        pe.matmul(dst, pkt[r][:, 0, :], vst[r][:, 0, :, 0:HD], start=True, stop=False)
                    mm = pe.matmul(dst, pkt[r][0:rows_n, n // 4, :], vst[r][0:rows_n, n // 4, :, 0:HD], start=(n < 4), stop=True)
                    if n in (3, NS - 1):
                        signal(mm, "state")

            def look_states(b, r, looks):
                wait(pe, "state_own", b, 2)
                for n in looks:
                    t, c, at = LOOKS[n]
                    bank = ring(b, "look", 0, n)
                    signal(pe.matmul(bank[:, 0:c * D], pqk[r][:, t * P:(t + 1) * P], states[:, at:at + c, :], start=True, stop=True), "looked")

            if last_stage >= 1:
                experts(0)
            if last_stage >= 2:
                look_up()
                tables.append(s1)
                pe.wait_ge(ls["w_scaled"], 1 + 1)
                pe.wait_ge(ls["gate_in"], 1 + 1)
                pe.wait_ge(ls["um"], NT + 1)
                turn_x(0, 0)
                project1_qk(0, 0)
                project1_v(0, 0)
                turn_keys(0, 0)
                for n in range(2):
                    spread(0, n)

                def step1(b, r, g, first=False, prep=True, tail=False):
                    second = g >= 2 if first else True
                    if not tail:
                        keys_ready(b, g)
                    for n in range(3):
                        if not tail:
                            prob_scores(b, r, g, n, b)
                        if n == 0 and second:
                            bb, _, gg = back(b, r, g - 2)
                            turn_den(bb, gg)
                    if g == 0 and not tail:
                        chunk_states(b, r)
                    if g == 1 and prep:
                        project1_qk(b + 1, 1 - r)
                    if g == 2 and not tail:
                        look_states(b, r, (0, 1))
                    if g == 3 and prep:
                        turn_keys(b + 1, 1 - r)
                    if second:
                        widen(bb, gg)
                    if g == 1 and prep:
                        project1_v(b + 1, 1 - r)
                    if g == 0 and prep:
                        turn_x(b + 1, 1 - r)
                    if g == 0 and not tail:
                        spread(b, 2)
                        spread(b, 3)
                    if g == 3 and prep:
                        spread(b + 1, 0)
                        spread(b + 1, 1)
                    if not (first and g == 0) and not (tail and g > 0):
                        weigh(*back(b, r, g - 1))
                    if g == 1 and not first:
                        give_out(b - 1, prep, tail)
                    if g == 3 and not tail:
                        look_states(b, r, (2,))
                all_steps(pe, step1, 2)
                tables.pop()
            if last_stage >= 3:
                experts(1)


def kernel(**inputs):
    import concourse.bacc as _bacc
    from concourse.bass_utils import run_bass_kernel_spmd as _run

    arrays = {f"in_{k}": v for k, v in _layout(inputs).items()}
    nc = _bacc.Bacc("TRN2", target_bir_lowering=False, num_devices=1)
    aps = {k[3:]: nc.dram_tensor(k, v.shape, mybir.dt.from_np(v.dtype), kind="ExternalInput").ap() for k, v in arrays.items()}
    out = nc.dram_tensor("out_y", (B * S, D), F32, kind="ExternalOutput").ap()
    build(nc, aps, out)
    r = _run(nc, [arrays], core_ids=[0])
    return r.results[0]["out_y"].reshape(B, S, D)
```
